# Optimizing a Trainium2 kernel written in Bass

```python
import numpy as np
import jax
import jax.numpy as jnp

def _softmax(x, axis=-1):
    return jax.nn.softmax(x, axis=axis)

def _gelu(x):
    return jax.nn.gelu(x, approximate=True)

def _silu(x):
    return jax.nn.silu(x)

def _sigmoid(x):
    return jax.nn.sigmoid(x)

def _layernorm(x, axis=-1, eps=1e-05):
    m = jnp.mean(x, axis=axis, keepdims=True)
    v = jnp.var(x, axis=axis, keepdims=True)
    return (x - m) / jnp.sqrt(v + eps)

def _scatter_add(tgt, idx, src, axis=0):
    return tgt.at[idx].add(src)

def _segment_sum(src, seg, n):
    return jax.ops.segment_sum(src, seg, n)
kernel_name = 'mk_sandwich_d1_jaxref_r4_2a57c9'

def setup_inputs(seed: int=0):
    np.random.seed(seed)
    _w = jnp.asarray

    def _L0_attn_setup():
        import math
        import jax, jax.numpy as jnp
        import numpy as np
        NUM_HEAD = 16
        BLOCK_SIZE = 512

        def get_slopes(n):

            def pow2(n):
                start = 2 ** (-2 ** (-(math.log2(n) - 3)))
                return [start * start ** i for i in range(n)]
            if math.log2(n).is_integer():
                return pow2(n)
            c = 2 ** math.floor(math.log2(n))
            return pow2(c) + get_slopes(2 * c)[0::2][:n - c]
        key = jax.random.key(seed)
        ks = jax.random.split(key, 5)
        B, T, C = (4, 512, 256)
        x = jax.random.normal(ks[0], (B, T, C), dtype=jnp.float32)
        Wq = 0.02 * jax.random.normal(ks[1], (C, C), dtype=jnp.float32)
        Wk = 0.02 * jax.random.normal(ks[2], (C, C), dtype=jnp.float32)
        Wv = 0.02 * jax.random.normal(ks[3], (C, C), dtype=jnp.float32)
        Wo = 0.02 * jax.random.normal(ks[4], (C, C), dtype=jnp.float32)
        return {'x': x, 'Wq': Wq, 'Wk': Wk, 'Wv': Wv, 'Wo': Wo}
    _L0_attn_in = _L0_attn_setup()

    def _L0_ffn_setup():
        import jax, jax.numpy as jnp
        import numpy as np
        B, S, H, I, E, TOP_K = (1, 512, 256, 512, 8, 2)
        key = jax.random.key(seed)
        ks = jax.random.split(key, 6)
        x = jax.random.normal(ks[0], (B, S, H), dtype=jnp.float32)
        Wr = jax.random.normal(ks[1], (H, E), dtype=jnp.float32) * (1.0 / np.sqrt(H))
        br = jnp.zeros((E,), dtype=jnp.float32)
        W1 = jax.random.normal(ks[2], (E, H, I), dtype=jnp.float32) * (1.0 / np.sqrt(H))
        W3 = jax.random.normal(ks[3], (E, H, I), dtype=jnp.float32) * (1.0 / np.sqrt(H))
        W2 = jax.random.normal(ks[4], (E, I, H), dtype=jnp.float32) * (1.0 / np.sqrt(I))
        return {'x': x, 'Wr': Wr, 'br': br, 'W1': W1, 'W3': W3, 'W2': W2}
    _L0_ffn_in = _L0_ffn_setup()
    _d = {'L0_attn_x': _L0_attn_in['x'], 'L0_attn_Wq': _L0_attn_in['Wq'], 'L0_attn_Wk': _L0_attn_in['Wk'], 'L0_attn_Wv': _L0_attn_in['Wv'], 'L0_attn_Wo': _L0_attn_in['Wo'], 'L0_ffn_Wr': _L0_ffn_in['Wr'], 'L0_ffn_br': _L0_ffn_in['br'], 'L0_ffn_W1': _L0_ffn_in['W1'], 'L0_ffn_W3': _L0_ffn_in['W3'], 'L0_ffn_W2': _L0_ffn_in['W2']}
    _x0 = _d['L0_attn_x']
    _d['L0_attn_x'] = jax.random.normal(jax.random.fold_in(jax.random.key(seed), 1), (1, 4096, 256), dtype=_x0.dtype)
    del _x0
    return _d

def reference(L0_attn_x, L0_attn_Wq, L0_attn_Wk, L0_attn_Wv, L0_attn_Wo, L0_ffn_Wr, L0_ffn_br, L0_ffn_W1, L0_ffn_W3, L0_ffn_W2):

    def _L0_attn_ref(x, Wq, Wk, Wv, Wo):
        import math
        import jax, jax.numpy as jnp
        import numpy as np
        NUM_HEAD = 16
        BLOCK_SIZE = 512

        def get_slopes(n):

            def pow2(n):
                start = 2 ** (-2 ** (-(math.log2(n) - 3)))
                return [start * start ** i for i in range(n)]
            if math.log2(n).is_integer():
                return pow2(n)
            c = 2 ** math.floor(math.log2(n))
            return pow2(c) + get_slopes(2 * c)[0::2][:n - c]
        B, T, C = x.shape
        nh, hd = (NUM_HEAD, C // NUM_HEAD)
        q = (x @ Wq).reshape(B, T, nh, hd).transpose(0, 2, 1, 3)
        k = (x @ Wk).reshape(B, T, nh, hd).transpose(0, 2, 1, 3)
        v = (x @ Wv).reshape(B, T, nh, hd).transpose(0, 2, 1, 3)
        attn = jnp.einsum('bhqd,bhkd->bhqk', q, k) / jnp.sqrt(jnp.float32(hd))
        slopes = jnp.asarray(get_slopes(nh), dtype=jnp.float32)
        bias = slopes[:, None] * (jnp.arange(T, dtype=jnp.float32) - (BLOCK_SIZE - 1))
        attn = attn + bias[None, :, None, :]
        causal = jnp.tril(jnp.ones((T, T), dtype=bool))
        masked = jnp.where(causal[None, None], attn.astype(jnp.float32), jnp.finfo(jnp.float32).min)
        probs = jax.nn.softmax(masked, axis=-1)
        out = jnp.einsum('bhqk,bhkd->bhqd', probs, v)
        out = out.transpose(0, 2, 1, 3).reshape(B, T, C)
        return out @ Wo

    def _L0_ffn_ref(x, Wr, br, W1, W3, W2):
        import jax, jax.numpy as jnp
        import numpy as np
        B, S, H, I, E, TOP_K = (1, 512, 256, 512, 8, 2)
        logits = jnp.einsum('bsh,he->bse', x, Wr) + br
        routing_weights, expert_indices = jax.lax.top_k(logits, TOP_K)
        routing_weights = jax.nn.softmax(routing_weights, axis=-1)
        c = jnp.sum(jax.nn.one_hot(expert_indices, E, dtype=x.dtype) * routing_weights[..., None], axis=-2)
        gate = jnp.einsum('bsh,ehi->besi', x, W1)
        up = jnp.einsum('bsh,ehi->besi', x, W3)
        h = jax.nn.silu(gate) * up
        y = jnp.einsum('besi,eih->besh', h, W2)
        out = jnp.einsum('bse,besh->bsh', c, y)
        return out
    x = L0_attn_x
    x = x + _layernorm(_L0_attn_ref(_layernorm(x, axis=-1), L0_attn_Wq, L0_attn_Wk, L0_attn_Wv, L0_attn_Wo), axis=-1)
    x = x + _layernorm(_L0_ffn_ref(_layernorm(x, axis=-1), L0_ffn_Wr, L0_ffn_br, L0_ffn_W1, L0_ffn_W3, L0_ffn_W2), axis=-1)
    return x

_drawn_inputs = setup_inputs


def setup_inputs(seed=0):
    import zlib

    import numpy as np

    out = dict(_drawn_inputs(seed))
    spreads = {'L0_ffn_br': (0.0, 0.1)}
    factors = {}
    for name, (base, spread) in spreads.items():
        noise = np.random.default_rng([zlib.crc32(name.encode()), seed]).standard_normal(out[name].shape)
        drawn = base * np.exp(spread * noise) if base else spread * noise
        out[name] = jnp.asarray(drawn.astype(out[name].dtype))
    for name, factor in factors.items():
        out[name] = (out[name] * factor).astype(out[name].dtype)
    return out
```

```python
from contextlib import ExitStack

import concourse.bass as bass
from concourse import mybir

ALU = mybir.AluOpType
ACT = mybir.ActivationFunctionType
AX = mybir.AxisListType
F32 = mybir.dt.float32
BF16 = mybir.dt.bfloat16
I32 = mybir.dt.int32
U32 = mybir.dt.uint32

P = 128
T, C = 4096, 256
NH, HD = 16, 16
E, FF, TOPK = 8, 512, 2
KC = C // P
CH = 512
NCH = T // CH
TPC = CH // P
NT = T // P
G, HPG = 4, 4
EPS = 1e-5
ONE = 1
SCALE = HD ** -0.5

Q_PARTS = (1, 1, 2, 0, 0, 0)
K_PARTS = (0, 1, 0, 0, 1, 2)
PROD = len(Q_PARTS) * HD
MAXROW = PROD
ROWS = PROD + 6
PART_ROWS = 3 * HD


def slopes():
    import numpy as np

    start = 2.0 ** (-(2.0 ** -(NH.bit_length() - 1 - 3)))
    return np.array([start * start ** i for i in range(NH)], np.float32)


def host_constants():
    import numpy as np

    bf16 = np.dtype(mybir.dt.np(BF16))
    f32 = np.float32
    bias = slopes()[:, None] * (np.arange(T, dtype=f32) - f32(511))
    high = bias.astype(bf16)
    mid = (bias - high.astype(f32)).astype(bf16)
    low = (bias - high.astype(f32) - mid.astype(f32)).astype(bf16)
    k_rows = np.ones((G, 6, HPG, T), bf16)
    for n, part in enumerate((high, mid, low)):
        k_rows[:, 3 + n] = part.reshape(G, HPG, T)
    q_rows = np.zeros((6, HPG, CH), bf16)
    q_rows[3:] = 1
    future = np.triu(np.ones((P, P), f32), 1) * f32(-1e30)
    masks = np.stack([np.eye(P, dtype=f32), future, future.T]).astype(bf16)
    tri = np.triu(np.ones((P, P), f32), 1)
    tile_starts = (np.arange(TABLE) * P).astype(f32)
    return {"eye": np.eye(P, dtype=f32), "tri": tri, "tile_starts": tile_starts, "q_rows": q_rows, "k_rows": k_rows, "masks": masks}


class Kit:

    def __init__(self, nc, ctx):
        self.nc, self.ctx = nc, ctx

    def sb(self, name, shape, dt=F32):
        return self.ctx.enter_context(self.nc.sbuf_tensor(name, shape, dt))

    def ps(self, name, shape, dt=F32):
        return self.ctx.enter_context(self.nc.psum_tensor(name, shape, dt))

    def sem(self, name):
        return self.ctx.enter_context(self.nc.semaphore(name))


def start_at_one(eng, semaphores):
    for semaphore in semaphores:
        eng.sem_inc(semaphore, ONE)


def pass_wait(eng, passed):
    eng.sem_inc(passed, 1)


def project_phase(nc, x, wq, wk, wv, eye, q_parts, k_parts, v_aug):
    with ExitStack() as ctx:
        kit = Kit(nc, ctx)
        ident = kit.sb("p_ident", [P, P])
        w_raw = [kit.sb(f"p_w{n}_raw", [P, KC, C]) for n in "qk"]
        w_sb = [kit.sb(f"p_w{n}", [P, KC, C]) for n in "qkv"]
        x_sb = [kit.sb(f"p_x{s}", [P, TPC, C]) for s in range(2)]
        xn = kit.sb("p_xn", [P, TPC, C])
        stats = kit.sb("p_stats", [P, TPC, 6])
        mv = kit.sb("p_mv", [P, TPC, 2])
        var_eps = kit.sb("p_var_eps", [P, TPC])
        std = kit.sb("p_std", [P, TPC])
        rstd = kit.sb("p_rstd", [P, TPC])
        xnT = kit.sb("p_xnT", [P, KC, CH])
        rest = kit.sb("p_rest", [P, CH])
        parts = [kit.sb(f"p_parts{s}", [P, 4, 3, CH], BF16) for s in range(2)]
        v_st = [kit.sb(f"p_v{s}", [P, TPC, NH, 32]) for s in range(2)]
        xT_ps = kit.ps("p_xT_ps", [P, KC, CH])
        qk_ps = kit.ps("p_qk_ps", [P, 4, CH])
        v_ps = kit.ps("p_v_ps", [P, 2, 2, C])

        weights_in = kit.sem("p_weights_in")
        weights_ordered = kit.sem("p_weights_ordered")
        x_in = [kit.sem(f"p_x_in{s}") for s in range(2)]
        v_ones = kit.sem("p_v_ones")
        ln = kit.sem("p_ln")
        var_ready = kit.sem("p_var_ready")
        std_ready = kit.sem("p_std_ready")
        xn_ready = kit.sem("p_xn_ready")
        transposed = kit.sem("p_transposed")
        xT_ready = kit.sem("p_xT_ready")
        qk_done = kit.sem("p_qk_done")
        v_done = kit.sem("p_v_done")
        high_ready = kit.sem("p_high_ready")
        split_done = kit.sem("p_split_done")
        v_ready = kit.sem("p_v_ready")
        qk_stored = [kit.sem(f"p_qk_stored{s}") for s in range(2)]
        v_stored = [kit.sem(f"p_v_stored{s}") for s in range(2)]
        passed = kit.sem("p_passed")
        from_one = (transposed, v_done, *qk_stored, *v_stored, xT_ready, split_done, v_ready)
        block = ctx.enter_context(nc.Block())
        STORES = 4 * 2
        LN_STEPS = 3 + 2 * 4

        @block.gpsimd
        def _(pool):
            start_at_one(pool, from_one)
            pool.dma_start(ident[:], eye).then_inc(weights_in, 16)
            for w, src in zip((*w_raw, w_sb[2]), (wq, wk, wv)):
                pool.dma_start(w[:], src.rearrange("(k p) n -> p k n", p=P)).then_inc(weights_in, 16)
            for s in range(2):
                pool.memset(v_st[s][:, :, :, HD:HD + 1], 1.0)
                last = pool.memset(v_st[s][:, :, :, HD + 1:32], 0.0)
            last.then_inc(v_ones, 1)
            pool.wait_ge(weights_in, 64)
            for w, raw in zip(w_sb, w_raw):
                for k in range(KC):
                    last = pool.tensor_copy(w[:, k, :].rearrange("p (g d h) -> p g h d", g=G, d=HD),
                                            raw[:, k, :].rearrange("p (g h d) -> p g h d", g=G, d=HD))
            last.then_inc(weights_ordered, 1)

        @block.sync
        def _(sp):
            for s in range(2):
                sp.dma_start(x_sb[s][:], x[s * CH:(s + 1) * CH, :].rearrange("(j p) c -> p j c", p=P)).then_inc(
                    x_in[s], 16)
            with sp.Fori(0, NCH // 2) as it:
                for s in range(2):
                    n = it * 2 + s
                    sp.wait_ge(xn_ready, n + 1)
                    pass_wait(sp, passed)
                    nxt = (n + 2) % NCH
                    sp.dma_start(x_sb[s][:], x[bass.ds(nxt * CH, CH), :].rearrange(
                        "(j p) c -> p j c", p=P)).then_inc(x_in[s], 16)
                    for t in range(4):
                        sp.wait_ge(split_done, n * 4 + (t + 1) + ONE)
                        pass_wait(sp, passed)
                        store = (q_parts, k_parts)[t // 2]
                        for gg in range(2):
                            dst = store[2 * (t % 2) + gg, 0:PART_ROWS, :, bass.ds(n * CH, CH)].rearrange(
                                "(part d) h t -> (d h) part t", d=HD)
                            sp.dma_start(dst, parts[s][64 * gg:64 * gg + 64, t, :, :]).then_inc(
                                qk_stored[s], 16)
                    sp.wait_ge(v_ready, n * 2 + 2 + ONE)
                    pass_wait(sp, passed)
                    sp.dma_start(v_aug[bass.ds(n * CH, CH), :].rearrange("(j p) f -> p j f", p=P),
                                 v_st[s][:].rearrange("p j h e -> p j (h e)")).then_inc(v_stored[s], 16)
            for s in range(2):
                sp.wait_ge(qk_stored[s], 16 * STORES * NCH // 2 + ONE)
                sp.wait_ge(v_stored[s], 16 * NCH // 2 + ONE)
                sp.wait_ge(x_in[s], 16 * (NCH // 2 + 1))

        @block.vector
        def _(dve):
            with dve.Fori(0, NCH // 2) as it:
                for s in range(2):
                    n = it * 2 + s
                    base = n * LN_STEPS
                    dve.wait_ge(x_in[s], (it + 1) * 16)
                    for j in range(TPC):
                        last = nc.vector.bn_stats(stats[:, j, :], x_sb[s][:, j, :])
                    last.then_inc(ln, 1)
                    dve.wait_ge(ln, base + 1)
                    pass_wait(dve, passed)
                    for j in range(TPC):
                        last = nc.vector.bn_aggr(mv[:, j, :], stats[:, j, :])
                    last.then_inc(ln, 1)
                    dve.wait_ge(ln, base + 2)
                    nc.vector.tensor_scalar_add(var_eps[:], mv[:, :, 1], EPS).then_inc(var_ready, 1)
                    dve.wait_ge(std_ready, n + 1)
                    nc.vector.reciprocal(rstd[:], std[:]).then_inc(ln, 1)
                    dve.wait_ge(ln, base + 3)
                    dve.wait_ge(transposed, n + ONE)
                    for j in range(TPC):
                        last = nc.vector.tensor_scalar(xn[:, j, :], x_sb[s][:, j, :], mv[:, j, 0:1],
                                                       rstd[:, j:j + 1], ALU.subtract, ALU.mult)
                    last.then_inc(xn_ready, 1)
                    for t in range(4):
                        dve.wait_ge(high_ready, n * 4 + (t + 1))
                        nc.vector.scalar_tensor_tensor(
                            out=rest[:], in0=qk_ps[:, t, :], scalar=SCALE if t < 2 else 1.0,
                            in1=parts[s][:, t, 0, :], op0=ALU.mult, op1=ALU.subtract).then_inc(ln, 1)
                        dve.wait_ge(ln, base + 4 + 2 * t)
                        nc.vector.tensor_copy(parts[s][:, t, 1, :], rest[:]).then_inc(ln, 1)
                        dve.wait_ge(ln, base + 5 + 2 * t)
                        nc.vector.tensor_tensor(parts[s][:, t, 2, :], rest[:], parts[s][:, t, 1, :],
                                                ALU.subtract).then_inc(split_done, 1)
                        dve.wait_ge(split_done, n * 4 + (t + 1) + ONE)

        @block.scalar
        def _(act):
            act.wait_ge(v_ones, 1)
            with act.Fori(0, NCH // 2) as it:
                for s in range(2):
                    n = it * 2 + s
                    act.wait_ge(var_ready, n + 1)
                    nc.scalar.activation(std[:], var_eps[:], ACT.Sqrt).then_inc(std_ready, 1)
                    act.wait_ge(transposed, n + 1 + ONE)
                    act.wait_ge(v_done, n * 2 + ONE)
                    for k in range(KC):
                        last = nc.scalar.activation(xnT[:, k, :], xT_ps[:, k, :], ACT.Copy)
                    last.then_inc(xT_ready, 1)
                    act.wait_ge(qk_stored[s], it * (16 * STORES) + ONE)
                    for t in range(4):
                        act.wait_ge(qk_done, n * 4 + (t + 1))
                        nc.scalar.activation(parts[s][:, t, 0, :], qk_ps[:, t, :], ACT.Copy,
                                             scale=SCALE if t < 2 else 1.0).then_inc(high_ready, 1)
                    act.wait_ge(v_stored[s], it * 16 + ONE)
                    for u in range(2):
                        act.wait_ge(v_done, n * 2 + (u + 1) + ONE)
                        nc.scalar.activation(v_st[s][:, 2 * u:2 * u + 2, :, 0:HD],
                                             v_ps[:, u, :, :].rearrange("p j (h d) -> p j h d", h=NH),
                                             ACT.Copy).then_inc(v_ready, 1)

        @block.tensor
        def _(pe):
            pe.wait_ge(weights_in, 64)
            pe.wait_ge(weights_ordered, 1)
            with pe.Fori(0, NCH) as n:
                pe.wait_ge(xn_ready, n + 1)
                pe.wait_ge(xT_ready, n + ONE)
                for k in range(KC):
                    for j in range(TPC):
                        last = nc.tensor.transpose(xT_ps[:, k, j * P:(j + 1) * P],
                                                   xn[:, j, k * P:(k + 1) * P], ident[:])
                last.then_inc(transposed, 1)
                pe.wait_ge(xT_ready, n + 1 + ONE)
                pe.wait_ge(split_done, n * 4 + ONE)
                for t in range(4):
                    w, m = w_sb[t // 2], t % 2
                    for k in range(KC):
                        last = nc.tensor.matmul(qk_ps[:, t, :], w[:, k, m * P:(m + 1) * P], xnT[:, k, :],
                                                start=(k == 0), stop=(k == KC - 1))
                    last.then_inc(qk_done, 1)
                pe.wait_ge(v_ready, n * 2 + ONE)
                for j in range(TPC):
                    for k in range(KC):
                        last = nc.tensor.matmul(v_ps[:, j // 2, j % 2, :], xnT[:, k, j * P:(j + 1) * P],
                                                w_sb[2][:, k, :], start=(k == 0), stop=(k == KC - 1))
                    if j % 2:
                        last.then_inc(v_done, 1)


def chunk_steps(c):
    return TPC * (c + 1)


STEPS = sum(chunk_steps(c) for c in range(NCH))
UNITS = STEPS * HPG
STEP0 = [sum(chunk_steps(d) for d in range(c)) for c in range(NCH + 1)]
LEAD = 3
TURN_GAP = 4
Q_RELOAD = 16
RELOAD = 10
TAIL = 8


def max_units(c):
    return [(kc, j, hp) for kc in range(c + 1) for j in range(TPC) for hp in range(2)]


def max_unit0(c):
    return c // NCH * MAX_UNITS + sum(len(max_units(d)) for d in range(c % NCH))


MAX_UNITS = sum(len(max_units(c)) for c in range(NCH))


def turn_behind(c):
    return 0 if c % NCH == NCH - 1 else 4


def max_events(c):
    events = [("unit", c, i) for i in range(len(max_units(c % NCH)))]
    if c > 0:
        events.insert(turn_behind(c - 1), ("turn", c - 1))
    return events


def group_plan():
    deadlines = [(STEP0[c] * HPG - TAIL, max_unit0(c + 1)) for c in range(LEAD, NCH)]
    at, done = Q_RELOAD, max_unit0(LEAD)
    after = {}
    place = {}
    while deadlines:
        knot = max(deadlines, key=lambda d: (d[1] - done) / (d[0] - at))
        for m in range(done, knot[1]):
            place[m] = at + (m - done) * (knot[0] - at) // (knot[1] - done)
        deadlines = [d for d in deadlines if d[0] > knot[0]]
        at, done = knot
    at = (STEP0[NCH - 1] + TPC) * HPG + RELOAD
    for m in range(done, max_unit0(NCH + LEAD)):
        place[m] = at + (m - done) * (UNITS - TAIL - at) // (max_unit0(NCH + LEAD) - done)
    u = 0
    for c in range(LEAD, NCH + LEAD):
        for what in max_events(c):
            if what[0] == "unit":
                u = max(u, place[max_unit0(c) + what[2]])
            elif turn_behind(what[1]) == 0:
                u += TURN_GAP
            if c >= NCH and what[0] == "unit":
                u = max(u, (STEP0[NCH - 1] + TPC * (c - NCH + 1)) * HPG + RELOAD)
            u = min(u, UNITS - 1)
            after.setdefault(u, []).append(what)
    return after


def attention_phase(nc, q_parts, k_parts, v_aug, q_rows, k_rows, masks, o_dram, table, weight_loads, weights_in):
    with ExitStack() as ctx:
        kit = Kit(nc, ctx)
        SLOTS_Q, SLOTS_ST, SLOTS_P = LEAD + 1, 3, 3
        assert NCH % SLOTS_Q == 0
        PLAN = group_plan()
        IN_ORDER = [w for c in range(NCH + LEAD) for w in max_events(c)]
        EVENTS = MAX_UNITS + NCH
        assert EVENTS % 2 == 0 and STEPS % SLOTS_P == 0 and UNITS % SLOTS_ST == 0
        k_sb = kit.sb("a_k", [P, HPG, T], BF16)
        v_sb = kit.sb("a_v", [P, NT, HPG * 32])
        q_sb = [kit.sb(f"a_q{s}", [P, HPG, CH], BF16) for s in range(SLOTS_Q)]
        probs = [kit.sb(f"a_p{s}", [P, HPG, CH]) for s in range(SLOTS_P)]
        o_sb = [kit.sb(f"a_o{s}", [P, CH]) for s in range(2)]
        ZEROS = 2048
        zeros = kit.sb("a_zeros", [P, ZEROS])
        ident = kit.sb("a_ident", [P, P], BF16)
        mask_q = kit.sb("a_mask_q", [P, P], BF16)
        mask_k = kit.sb("a_mask_k", [P, P], BF16)
        part_max = kit.sb("a_part_max", [P, TPC * HPG, NCH])
        neg_max = kit.sb("a_neg_max", [P, TPC, HPG])
        max_rest = kit.sb("a_max_rest", [P, TPC, HPG])
        max_cols = kit.sb("a_max_cols", [P, TPC, HPG, 32], BF16)

        st_ps = kit.ps("a_st_ps", [P, SLOTS_ST, CH])
        mx_ps = [kit.ps(f"a_mx_ps{s}", [P, 2, CH]) for s in range(2)]
        ot_ps = kit.ps("a_ot_ps", [P, CH])

        consts_in = kit.sem("a_consts_in")
        cols_zero = kit.sem("a_cols_zero")
        zeros_ready = kit.sem("a_zeros_ready")
        table_zeroed = kit.sem("a_table_zeroed")
        q_in = [kit.sem(f"a_q_in{s}") for s in range(SLOTS_Q)]
        k_in = [kit.sem(f"a_k_in{n}") for n in range(NCH)]
        v_in = [kit.sem(f"a_v_in{n}") for n in range(NCH)]
        scores_ready = kit.sem("a_scores_ready")
        probs_ready = kit.sem("a_probs_ready")
        pv_done = kit.sem("a_pv_done")
        o_copied = kit.sem("a_o_copied")
        o_stored = [kit.sem(f"a_o_stored{s}") for s in range(2)]
        max_ready = kit.sem("a_max_ready")
        max_reduced = kit.sem("a_max_reduced")
        max_step = kit.sem("a_max_step")
        cols_ready = kit.sem("a_cols_ready")
        turned = kit.sem("a_turned")
        rows_written = kit.sem("a_rows_written")
        passed = kit.sem("a_passed")
        from_one = (scores_ready, *o_stored, o_copied)
        block = ctx.enter_context(nc.Block())
        Q_LOAD, K_LOAD = 7 * 16, 4 * 16
        MAX_STEPS = 4

        EVENT = {what: n for n, what in enumerate(IN_ORDER)}

        def load_q(eng, g, c):
            dst, tok = q_sb[c % SLOTS_Q], slice(c * CH, (c + 1) * CH)
            done = q_in[c % SLOTS_Q]
            for r, part in enumerate(Q_PARTS):
                eng.dma_start(dst[r * HD:(r + 1) * HD, :, :],
                              q_parts[g, part * HD:(part + 1) * HD, :, tok]).then_inc(done, 16)
            eng.dma_start(dst[PROD:ROWS, :, :], q_rows).then_inc(done, 16)

        def load_k(eng, g, n):
            tok = slice(n * CH, (n + 1) * CH)
            for r0, r1 in ((0, 2 * HD), (2 * HD, PART_ROWS), (PART_ROWS, PROD)):
                eng.dma_start(k_sb[r0:r1, :, tok], k_parts[g, 0:r1 - r0, :, tok]).then_inc(k_in[n], 16)
            eng.dma_start(k_sb[PROD:ROWS, :, tok], k_rows[g, :, :, tok]).then_inc(k_in[n], 16)
            eng.dma_start(v_sb[:, n * TPC:(n + 1) * TPC, :],
                          v_aug[tok, :].rearrange("(b p) (g f) -> g p b f", p=P, g=G)[g]).then_inc(v_in[n], 16)

        @block.gpsimd
        def _(pool):
            start_at_one(pool, from_one)
            pool.dma_start(ident[:], masks[0]).then_inc(consts_in, 16)
            pool.dma_start(mask_q[:], masks[1]).then_inc(consts_in, 16)
            pool.dma_start(mask_k[:], masks[2]).then_inc(consts_in, 16)
            pool.memset(max_cols[:], 0.0).then_inc(cols_zero, 1)
            pool.memset(zeros[:], 0.0).then_inc(zeros_ready, 1)
            pool.wait_ge(zeros_ready, 1)
            flat = table.rearrange("(p r) c -> p (r c)", p=P)
            for f in range(0, flat.shape[1], ZEROS):
                pool.dma_start(flat[:, f:f + ZEROS], zeros[:]).then_inc(table_zeroed, 16)
            for dst, src in weight_loads:
                pool.dma_start(dst, src).then_inc(weights_in, 16)
            pool.wait_ge(table_zeroed, 16 * (TABLE * C // ZEROS))

        @block.sync
        def _(sp):
            def store_o(g, c):
                sp.wait_ge(o_copied, g * NCH + (c + 1) + ONE)
                pass_wait(sp, passed)
                sp.dma_start(o_dram[g, :, c * CH:(c + 1) * CH], o_sb[c % 2][:]).then_inc(o_stored[c % 2], 16)

            for c in range(LEAD):
                load_q(sp, 0, c)
                load_k(sp, 0, c)
            for n in range(LEAD, NCH):
                load_k(sp, 0, n)
            with sp.Fori(0, G) as g:
                nxt = (g + 1) % G
                for c in range(NCH):
                    sp.wait_ge(scores_ready, g * UNITS + STEP0[c] * HPG + ONE)
                    pass_wait(sp, passed)
                    load_q(sp, g if c + LEAD < NCH else nxt, (c + LEAD) % NCH)
                    if c > 0:
                        store_o(g, c - 1)
                for n in range(NCH):
                    last_step = STEP0[NCH - 1] + TPC * (n + 1)
                    sp.wait_ge(scores_ready, g * UNITS + last_step * HPG + ONE)
                    pass_wait(sp, passed)
                    sp.wait_ge(pv_done, g * STEPS + last_step)
                    pass_wait(sp, passed)
                    load_k(sp, nxt, n)
                store_o(g, NCH - 1)
            for s in range(2):
                sp.wait_ge(o_stored[s], 16 * G * NCH // 2 + ONE)
            for s in range(SLOTS_Q):
                sp.wait_ge(q_in[s], Q_LOAD * (G * NCH // SLOTS_Q + (1 if s < LEAD else 0)))
            for n in range(NCH):
                sp.wait_ge(k_in[n], K_LOAD * (G + 1))
                sp.wait_ge(v_in[n], 16 * (G + 1))

        @block.tensor
        def _(pe):
            pe.wait_ge(consts_in, 48)

            def wait_slot(g, n):
                if n < 2:
                    return
                what, c, *i = IN_ORDER[n - 2]
                if what == "unit":
                    pe.wait_ge(max_reduced, g * MAX_UNITS + (max_unit0(c) + i[0] + 1))
                else:
                    pe.wait_ge(rows_written, (g * NCH + (c + 1)) * HPG)

            def max_unit(slot, c, kc, j, hp):
                diagonal = kc == c % NCH
                width = (j + 1) * P if diagonal else CH
                for hh in range(2):
                    h = 2 * hp + hh
                    last = nc.tensor.matmul(mx_ps[slot][:, hh, 0:width], q_sb[c % SLOTS_Q][0:ROWS, h, j * P:(j + 1) * P],
                                            k_sb[0:ROWS, h, kc * CH:kc * CH + width], start=True, stop=not diagonal)
                    if diagonal:
                        last = nc.tensor.matmul(mx_ps[slot][:, hh, width - P:width], ident[:], mask_q[:],
                                                start=False, stop=True)
                last.then_inc(max_ready, 1)

            def turn(slot):
                for j in range(TPC):
                    last = nc.tensor.matmul(mx_ps[slot][:, 0, j * P:(j + 1) * P],
                                            max_cols[:, j, :, :].rearrange("p h e -> p (h e)"), ident[:],
                                            start=True, stop=True)
                last.then_inc(turned, 1)

            def max_event(g, what, c, i=None):
                n = EVENT[(what, c) if i is None else (what, c, i)]
                if what == "unit":
                    kc, j, hp = max_units(c % NCH)[i]
                    if i == 0:
                        pe.wait_ge(q_in[c % SLOTS_Q], (g * (NCH // SLOTS_Q) + (c // SLOTS_Q + 1)) * Q_LOAD)
                    if kc == c % NCH and j == 0 and hp == 0:
                        pe.wait_ge(k_in[kc], (g + (c // NCH + 1)) * K_LOAD)
                    wait_slot(g, n)
                    max_unit(n % 2, c, kc, j, hp)
                else:
                    wait_slot(g, n)
                    pe.wait_ge(cols_ready, g * NCH + (c + 1))
                    turn(n % 2)

            for c in range(LEAD):
                for what in max_events(c):
                    max_event(0, *what)

            with pe.Fori(0, G) as g:
                def pv(c, b):
                    n = TPC * c
                    q0 = max(0, b - n) * P
                    s = STEP0[c] + b
                    if b == 0:
                        pe.wait_ge(o_copied, g * NCH + c + ONE)
                    if b >= n and c == b // TPC and b % TPC == 0:
                        pe.wait_ge(v_in[c], (g + 1) * 16)
                    pe.wait_ge(probs_ready, g * UNITS + (s + 1) * HPG)
                    for h in range(HPG):
                        last = nc.tensor.matmul(ot_ps[32 * h:32 * h + 32, q0:CH], v_sb[:, b, 32 * h:32 * h + 32],
                                                probs[s % SLOTS_P][:, h, q0:CH], start=(b == 0),
                                                stop=(b == n + TPC - 1))
                    last.then_inc(pv_done, 1)

                pending = None
                for c in range(NCH):
                    pe.wait_ge(rows_written, (g * NCH + (c + 1)) * HPG)
                    for i in range(HPG * chunk_steps(c)):
                        b, h = divmod(i, HPG)
                        u = STEP0[c] * HPG + i
                        j = b - TPC * c
                        q0 = max(0, j) * P
                        if u >= SLOTS_ST:
                            pe.wait_ge(probs_ready, g * UNITS + (u - SLOTS_ST + 1))
                        last = nc.tensor.matmul(st_ps[:, u % SLOTS_ST, q0:CH], k_sb[0:ROWS, h, b * P:(b + 1) * P],
                                                q_sb[c % SLOTS_Q][0:ROWS, h, q0:CH], start=True, stop=(j < 0))
                        if j >= 0:
                            last = nc.tensor.matmul(st_ps[:, u % SLOTS_ST, q0:q0 + P], ident[:], mask_k[:],
                                                    start=False, stop=True)
                        last.then_inc(scores_ready, 1)
                        if h == 2 and pending is not None:
                            pv(*pending)
                        if h == 3:
                            pending = (c, b)
                        for what in PLAN.get(u, ()):
                            max_event(g, *what)
                pv(*pending)

        @block.scalar
        def _(act):
            def write_rows(g, c):
                slot = EVENT["turn", c] % 2
                act.wait_ge(turned, g * NCH + (c + 1))
                for h in range(HPG):
                    nc.scalar.activation(q_sb[c % SLOTS_Q][MAXROW:MAXROW + 3, h, :],
                                         mx_ps[slot][32 * h:32 * h + 3, 0, :], ACT.Copy).then_inc(rows_written, 1)

            for c in range(LEAD - 1):
                write_rows(0, c)
            with act.Fori(0, G) as g:

                def copy_out(c):
                    act.wait_ge(pv_done, g * STEPS + (STEP0[c] + chunk_steps(c)))
                    act.wait_ge(o_stored[c % 2], (g * (NCH // 2) + c // 2) * 16 + ONE)
                    nc.scalar.activation(o_sb[c % 2][:], ot_ps[:], ACT.Copy).then_inc(o_copied, 1)

                for c in range(NCH):
                    for i in range(HPG * chunk_steps(c)):
                        b, h = divmod(i, HPG)
                        s = STEP0[c] + b
                        q0 = max(0, b - TPC * c) * P
                        act.wait_ge(scores_ready, g * UNITS + (s * HPG + h + 1) + ONE)
                        if h == 0 and s >= SLOTS_P:
                            act.wait_ge(pv_done, g * STEPS + (s - SLOTS_P + 1))
                        nc.scalar.activation(probs[s % SLOTS_P][:, h, q0:CH], st_ps[:, (s * HPG + h) % SLOTS_ST, q0:CH],
                                             ACT.Exp).then_inc(probs_ready, 1)
                        if c > 0 and i == 4:
                            copy_out(c - 1)
                        for what, chunk, *_ in PLAN.get(s * HPG + h, ()):
                            if what == "turn":
                                write_rows(g, chunk)
                copy_out(NCH - 1)

        @block.vector
        def _(dve):
            def reduce_units(g, c):
                for i, (kc, j, hp) in enumerate(max_units(c % NCH)):
                    width = (j + 1) * P if kc == c % NCH else CH
                    dve.wait_ge(max_ready, g * MAX_UNITS + (max_unit0(c) + i + 1))
                    nc.vector.tensor_reduce(part_max[:, HPG * j + 2 * hp:HPG * j + 2 * hp + 2, kc],
                                            mx_ps[EVENT["unit", c, i] % 2][:, :, 0:width], AX.X,
                                            ALU.max).then_inc(max_reduced, 1)

            def split_max(g, c):
                turn_no = g * NCH + c
                step = turn_no * MAX_STEPS
                dve.wait_ge(max_reduced, g * MAX_UNITS + max_unit0(c + 1))
                nc.vector.tensor_reduce(neg_max[:].rearrange("p j h -> p (j h)"), part_max[:, :, 0:c % NCH + 1], AX.X,
                                        ALU.max, negate=True).then_inc(max_step, 1)
                dve.wait_ge(turned, turn_no)
                dve.wait_ge(max_step, step + 1)
                nc.vector.tensor_copy(max_cols[:, :, :, 0], neg_max[:]).then_inc(max_step, 1)
                dve.wait_ge(max_step, step + 2)
                nc.vector.tensor_tensor(max_rest[:], neg_max[:], max_cols[:, :, :, 0], ALU.subtract).then_inc(
                    max_step, 1)
                dve.wait_ge(max_step, step + 3)
                nc.vector.tensor_copy(max_cols[:, :, :, 1], max_rest[:]).then_inc(max_step, 1)
                dve.wait_ge(max_step, step + 4)
                nc.vector.tensor_tensor(max_cols[:, :, :, 2], max_rest[:], max_cols[:, :, :, 1],
                                        ALU.subtract).then_inc(cols_ready, 1)

            dve.wait_ge(cols_zero, 1)
            for c in range(LEAD):
                reduce_units(0, c)
                split_max(0, c)
            with dve.Fori(0, G) as g:
                for c in range(LEAD, NCH + LEAD):
                    reduce_units(g, c)
                    split_max(g, c)


class Steps:

    def __init__(self, eng, sem, base):
        self.eng, self.sem, self.base, self.count = eng, sem, base, 0

    def link(self, instruction):
        self.count += 1
        instruction.then_inc(self.sem, 1)
        self.eng.wait_ge(self.sem, self.base + self.count)


def combine_phase(nc, x, wo, wr, br, eye, o_dram, x1, xn2, top_val, top_idx):
    with ExitStack() as ctx:
        kit = Kit(nc, ctx)
        ident = kit.sb("c_ident", [P, P])
        wo_sb = kit.sb("c_wo", [P, KC, C])
        wr_sb = kit.sb("c_wr", [P, KC, E])
        br_sb = kit.sb("c_br", [P, E])
        o_in_sb = [kit.sb(f"c_o{s}", [P, G, CH]) for s in range(2)]
        x_sb = [kit.sb(f"c_x_in{s}_sb", [P, TPC, C]) for s in range(2)]
        recip = kit.sb("c_recip", [P, TPC, NH])
        o_norm = kit.sb("c_o_norm", [P, TPC, C])
        o_nT = kit.sb("c_o_nT", [P, TPC, KC * P])
        y = kit.sb("c_y", [P, TPC, C])
        x1_c = kit.sb("c_x1_chunk", [P, TPC, C])
        x2_c = kit.sb("c_x2_chunk", [P, TPC, C])
        x2T = kit.sb("c_x2T", [P, TPC, KC * P])
        logits = kit.sb("c_logits", [P, TPC, E])
        top8 = kit.sb("c_top8", [P, TPC, E])
        idx8 = kit.sb("c_idx8", [P, TPC, E], U32)
        stats = kit.sb("c_stats", [P, TPC, 6])
        mv = kit.sb("c_mv", [P, TPC, 2])
        rstd = kit.sb("c_rstd", [P, TPC])
        var_eps = [kit.sb(f"c_var_eps{s}", [P, TPC]) for s in range(2)]
        std = [kit.sb(f"c_std{s}", [P, TPC]) for s in range(2)]
        o_ps = [kit.ps(f"c_o_ps{s}", [P, NH, 32]) for s in range(2)]
        tr_ps = [kit.ps(f"c_tr_ps{s}", [P, 2, KC * P]) for s in range(2)]
        att_ps = kit.ps("c_att_ps", [P, TPC, C])
        log_ps = kit.ps("c_log_ps", [P, TPC, E])

        weights_in = kit.sem("c_weights_in")
        o_in = [kit.sem(f"c_o_in{s}") for s in range(2)]
        x_in = [kit.sem(f"c_x_in{s}") for s in range(2)]
        kept = kit.sem("c_kept")
        o_turned = kit.sem("c_o_turned")
        o_divided = kit.sem("c_o_divided")
        on_turned = kit.sem("c_on_turned")
        on_copied = kit.sem("c_on_copied")
        att_done = kit.sem("c_att_done")
        att_read = kit.sem("c_att_read")
        ln_var = kit.sem("c_ln_var")
        ln_std = kit.sem("c_ln_std")
        x2_ready = kit.sem("c_x2_ready")
        x2_turned = kit.sem("c_x2_turned")
        x2_copied = kit.sem("c_x2_copied")
        logits_done = kit.sem("c_logits_done")
        logits_read = kit.sem("c_logits_read")
        div_step = kit.sem("c_div_step")
        res_step = kit.sem("c_res_step")
        ln_step = kit.sem("c_ln_step")
        top_step = kit.sem("c_top_step")
        passed = kit.sem("c_passed")
        from_one = (logits_read, logits_done, kept, x2_turned)
        block = ctx.enter_context(nc.Block())
        KEEP = 2 * 16

        def chunk(n):
            return bass.ds(n * CH, CH)

        def tiles(n):
            return bass.ds(n * TPC, TPC)

        def skewed(eng, first, second, residual=None):
            def step(n, s):
                if residual is not None:
                    residual(n - 1, 1 - s)
                first(n, s)
                second(n - 1, 1 - s)

            first(0, 0)
            with eng.Fori(0, NCH // 2 - 1) as it:
                step(it * 2 + 1, 1)
                step(it * 2 + 2, 0)
            step(NCH - 1, 1)
            if residual is not None:
                residual(NCH - 1, 1)
            second(NCH - 1, 1)

        @block.sync
        def _(sp):
            sp.dma_start(ident[:], eye).then_inc(weights_in, 16)
            sp.dma_start(wo_sb[:], wo.rearrange("(k p) n -> p k n", p=P)).then_inc(weights_in, 16)
            sp.dma_start(wr_sb[:], wr.rearrange("(k p) n -> p k n", p=P)).then_inc(weights_in, 16)
            sp.dma_start(br_sb[:], br.partition_broadcast(P)).then_inc(weights_in, 16)

            def load(n, s):
                sp.dma_start(o_in_sb[s][:], o_dram[:, :, chunk(n)].rearrange("g r t -> r g t")).then_inc(o_in[s], 16)
                sp.dma_start(x_sb[s][:], x[chunk(n), :].rearrange("(j p) c -> p j c", p=P)).then_inc(x_in[s], 16)

            def keep(n):
                sp.wait_ge(x2_ready, n + 1)
                pass_wait(sp, passed)
                sp.dma_start(x1[chunk(n), :].rearrange("(j p) c -> p j c", p=P), x1_c[:]).then_inc(kept, 16)
                sp.dma_start(xn2[:, tiles(n), :], x2_c[:]).then_inc(kept, 16)

            load(0, 0)
            load(1, 1)
            with sp.Fori(1, NCH // 2) as it:
                for s in range(2):
                    n = it * 2 + s
                    keep(n - 2)
                    sp.wait_ge(o_turned, (n - 1) * TPC)
                    pass_wait(sp, passed)
                    load(n, s)
            keep(NCH - 2)
            keep(NCH - 1)
            sp.wait_ge(kept, NCH * KEEP + ONE)

        @block.gpsimd
        def _(pool):
            start_at_one(pool, from_one)

        @block.tensor
        def _(pe):
            pe.wait_ge(weights_in, 64)

            def first(n, s):
                pe.wait_ge(o_in[s], (n + (2 - s)) * 8)
                for j in range(TPC):
                    if j < 2:
                        pe.wait_ge(o_divided, n * TPC)
                    else:
                        pe.wait_ge(o_divided, n * TPC + (j - 1))
                    for g in range(G):
                        last = nc.tensor.transpose(o_ps[j % 2][:, 4 * g:4 * g + 4, :].rearrange("p h e -> p (h e)"),
                                                   o_in_sb[s][:, g, j * P:(j + 1) * P], ident[:])
                    last.then_inc(o_turned, 1)
                for jj in range(2):
                    pe.wait_ge(o_divided, n * TPC + (2 * jj + 2))
                    for j in (2 * jj, 2 * jj + 1):
                        for k in range(KC):
                            last = nc.tensor.transpose(tr_ps[jj][:, j % 2, k * P:(k + 1) * P],
                                                       o_norm[:, j, k * P:(k + 1) * P], ident[:])
                    last.then_inc(on_turned, 1)
                pe.wait_ge(att_read, n)
                for jj in range(2):
                    pe.wait_ge(on_copied, n * 2 + (jj + 1))
                    for j in (2 * jj, 2 * jj + 1):
                        for k in range(KC):
                            last = nc.tensor.matmul(att_ps[:, j, :], o_nT[:, j, k * P:(k + 1) * P], wo_sb[:, k, :],
                                                    start=(k == 0), stop=(k == KC - 1))
                last.then_inc(att_done, 1)

            def second(n, s):
                pe.wait_ge(x2_ready, n + 1)
                for jj in range(2):
                    for j in (2 * jj, 2 * jj + 1):
                        for k in range(KC):
                            last = nc.tensor.transpose(tr_ps[jj][:, j % 2, k * P:(k + 1) * P],
                                                       x2_c[:, j, k * P:(k + 1) * P], ident[:])
                    last.then_inc(x2_turned, 1)
                pe.wait_ge(logits_read, n + ONE)
                for jj in range(2):
                    pe.wait_ge(x2_copied, n * 2 + (jj + 1))
                    for j in (2 * jj, 2 * jj + 1):
                        for k in range(KC):
                            last = nc.tensor.matmul(log_ps[:, j, :], x2T[:, j, k * P:(k + 1) * P], wr_sb[:, k, :],
                                                    start=(k == 0), stop=(k == KC - 1))
                last.then_inc(logits_done, 1)

            skewed(pe, first, second)

        @block.scalar
        def _(act):
            def std_of(k, count):
                act.wait_ge(ln_var, count + 1)
                nc.scalar.activation(std[k][:], var_eps[k][:], ACT.Sqrt).then_inc(ln_std, 1)

            def first(n, s):
                act.wait_ge(att_done, n)
                for jj in range(2):
                    act.wait_ge(on_turned, n * 2 + (jj + 1))
                    nc.scalar.activation(o_nT[:, 2 * jj:2 * jj + 2, :], tr_ps[jj][:], ACT.Copy).then_inc(on_copied, 1)

            def second(n, s):
                std_of(1, n * 2 + 1)
                act.wait_ge(logits_done, n + ONE)
                for jj in range(2):
                    act.wait_ge(x2_turned, n * 2 + (jj + 1) + ONE)
                    nc.scalar.activation(x2T[:, 2 * jj:2 * jj + 2, :], tr_ps[jj][:], ACT.Copy).then_inc(x2_copied, 1)

            skewed(act, first, second, residual=lambda n, s: std_of(0, n * 2))

        @block.vector
        def _(dve):
            def layer_norm(src, dst, k, n, st):
                for j in range(TPC):
                    last = nc.vector.bn_stats(stats[:, j, :], src[:, j, :])
                st.link(last)
                pass_wait(dve, passed)
                for j in range(TPC):
                    last = nc.vector.bn_aggr(mv[:, j, :], stats[:, j, :])
                st.link(last)
                nc.vector.tensor_scalar_add(var_eps[k][:], mv[:, :, 1], EPS).then_inc(ln_var, 1)
                dve.wait_ge(ln_std, n * 2 + (k + 1))
                st.link(nc.vector.reciprocal(rstd[:], std[k][:]))
                if k == 1:
                    dve.wait_ge(x2_turned, n * 2 + ONE)
                    dve.wait_ge(kept, n * KEEP + ONE)
                for j in range(TPC):
                    last = nc.vector.tensor_scalar(dst[:, j, :], src[:, j, :], mv[:, j, 0:1], rstd[:, j:j + 1],
                                                   ALU.subtract, ALU.mult)
                return last

            def first(n, s):
                st = Steps(dve, div_step, n * TPC)
                dve.wait_ge(on_turned, n * 2)
                for j in range(TPC):
                    dve.wait_ge(o_turned, n * TPC + (j + 1))
                    st.link(nc.vector.reciprocal(recip[:, j, :], o_ps[j % 2][:, :, HD]))
                    nc.vector.tensor_tensor(o_norm[:, j, :].rearrange("p (h d) -> p h d", h=NH),
                                            o_ps[j % 2][:, :, 0:HD],
                                            recip[:, j, :].unsqueeze(2).broadcast_to([P, NH, HD]),
                                            ALU.mult).then_inc(o_divided, 1)

            def residual(n, s):
                st = Steps(dve, res_step, n * 4)
                dve.wait_ge(att_done, n + 1)
                layer_norm(att_ps, y, 0, n, st).then_inc(att_read, 1)
                dve.wait_ge(att_read, n + 1)
                dve.wait_ge(x_in[s], (n + (2 - s)) * 8)
                dve.wait_ge(kept, n * KEEP + ONE)
                st.link(nc.vector.tensor_tensor(x1_c[:], y[:], x_sb[s][:], ALU.add))

            def second(n, s):
                st = Steps(dve, ln_step, n * 3)
                layer_norm(x1_c, x2_c, 1, n, st).then_inc(x2_ready, 1)
                st = Steps(dve, top_step, n * 3)
                dve.wait_ge(logits_done, n + 1 + ONE)
                nc.vector.tensor_tensor(logits[:], log_ps[:], br_sb[:].unsqueeze(1).broadcast_to([P, TPC, E]),
                                        ALU.add).then_inc(logits_read, 1)
                dve.wait_ge(logits_read, n + 1 + ONE)
                pass_wait(dve, passed)
                for j in range(TPC):
                    last = nc.vector.max(top8[:, j, :], logits[:, j, :])
                st.link(last)
                pass_wait(dve, passed)
                for j in range(TPC):
                    last = nc.vector.max_index(idx8[:, j, :], top8[:, j, :], logits[:, j, :])
                st.link(last)
                nc.vector.tensor_copy(top_val[:, tiles(n), :], top8[:, :, 0:TOPK])
                st.link(nc.vector.tensor_copy(top_idx[:, tiles(n), :], idx8[:, :, 0:TOPK]))

            skewed(dve, first, second, residual)


ROUTE_TILES = (TOPK * T + E * (P - 1)) // P
TABLE = 72
assert TABLE == ROUTE_TILES + ROUTE_TILES % 2


def route_phase(nc, tri, tile_starts, xn2, top_val, top_idx, place, weight, tile_expert, xs_dram):
    with ExitStack() as ctx:
        kit = Kit(nc, ctx)
        tri_sb = kit.sb("r_tri", [P, P])
        starts_sb = kit.sb("r_tile_starts", [P, TABLE])
        ones = kit.sb("r_ones", [P, P])
        experts = kit.sb("r_experts", [P, E])
        chosen = [kit.sb(f"r_chosen{k}", [P, NT, E]) for k in range(TOPK)]
        both = kit.sb("r_both", [P, NT, E])
        through = kit.sb("r_through", [P, NT, E])
        pos = kit.sb("r_pos", [P, NT, E])
        picked = kit.sb("r_picked", [P, NT, E])
        place_f = kit.sb("r_place_f", [P, TOPK, NT])
        diff = kit.sb("r_diff", [P, NT])
        ex = kit.sb("r_ex", [P, NT])
        denom = kit.sb("r_denom", [P, NT])
        count_i = kit.sb("r_count_i", [P, E], I32)
        padded = kit.sb("r_padded", [P, E])
        ends = kit.sb("r_ends", [P, E])
        starts = kit.sb("r_starts", [P, E])
        below = kit.sb("r_below", [P, TABLE, E])
        tile_e = kit.sb("r_tile_e", [P, TABLE])
        rank_ps = kit.ps("r_rank_ps", [P, NT, E])
        total_ps = kit.ps("r_total_ps", [P, NT, E])

        consts_in = kit.sem("r_consts_in")
        experts_ready = kit.sem("r_experts_ready")
        step = kit.sem("r_step")
        diff_ready = kit.sem("r_diff_ready")
        exp_ready = kit.sem("r_exp_ready")
        both_ready = kit.sem("r_both_ready")
        counted = kit.sem("r_counted")
        places_ready = kit.sem("r_places_ready")
        scattered = kit.sem("r_scattered")
        block = ctx.enter_context(nc.Block())

        @block.sync
        def _(sp):
            sp.dma_start(tri_sb[:], tri).then_inc(consts_in, 16)
            sp.dma_start(starts_sb[:], tile_starts.partition_broadcast(P)).then_inc(consts_in, 16)

        @block.scalar
        def _(act):
            act.wait_ge(diff_ready, 1)
            nc.scalar.activation(ex[:], diff[:], ACT.Exp).then_inc(exp_ready, 1)

        @block.tensor
        def _(pe):
            pe.wait_ge(consts_in, 32)
            pe.wait_ge(both_ready, 1)
            flat = both[:].rearrange("p t e -> p (t e)")
            nc.tensor.matmul(rank_ps[:].rearrange("p t e -> p (t e)"), tri_sb[:], flat, start=True, stop=True)
            nc.tensor.matmul(total_ps[:].rearrange("p t e -> p (t e)"), ones[:], flat, start=True,
                             stop=True).then_inc(counted, 1)

        @block.gpsimd
        def _(pool):
            pool.memset(ones[:], 1.0)
            pool.iota(experts[:], [[1, E]], base=0, channel_multiplier=0,
                      allow_small_or_imprecise_dtypes=True).then_inc(experts_ready, 1)
            pool.wait_ge(places_ready, 1)
            for k in range(TOPK):
                for t in range(NT):
                    pool.indirect_dma_start(out=xs_dram, out_offset=bass.IndirectOffsetOnAxis(
                        ap=place[:, k, t:t + 1], axis=0), in_=xn2[:, t, :], in_offset=None).then_inc(scattered, 16)
            pool.wait_ge(scattered, TOPK * NT * 16)

        @block.vector
        def _(dve):
            st = Steps(dve, step, 0)
            nc.vector.tensor_tensor(diff[:], top_val[:, :, 1], top_val[:, :, 0], ALU.subtract).then_inc(diff_ready, 1)
            dve.wait_ge(experts_ready, 1)
            for k in range(TOPK):
                last = nc.vector.tensor_tensor(chosen[k][:], top_idx[:, :, k:k + 1].broadcast_to([P, NT, E]),
                                               experts[:].unsqueeze(1).broadcast_to([P, NT, E]), ALU.is_equal)
            st.link(last)
            nc.vector.tensor_tensor(both[:], chosen[0][:], chosen[1][:], ALU.add).then_inc(both_ready, 1)
            dve.wait_ge(exp_ready, 1)
            st.link(nc.vector.tensor_scalar_add(denom[:], ex[:], 1.0))
            st.link(nc.vector.reciprocal(weight[:, 0, :], denom[:]))
            nc.vector.tensor_tensor(weight[:, 1, :], ex[:], weight[:, 0, :], ALU.mult)
            dve.wait_ge(counted, 1)
            dve.wait_ge(consts_in, 32)
            for e in range(E):
                last = nc.vector.tensor_tensor_scan(through[:, :, e], ones[:, 0:NT], total_ps[:, :, e], 0.0,
                                                    ALU.mult, ALU.add)
            st.link(last)
            st.link(nc.vector.tensor_scalar_add(padded[:], through[:, NT - 1, :], float(P - 1)))
            st.link(nc.vector.tensor_copy(count_i[:], padded[:]))
            shift = P.bit_length() - 1
            st.link(nc.vector.tensor_scalar(count_i[:], count_i[:], shift, shift, ALU.arith_shift_right,
                                            ALU.logical_shift_left))
            st.link(nc.vector.tensor_copy(padded[:], count_i[:]))
            st.link(nc.vector.tensor_tensor_scan(ends[:], ones[:, 0:E], padded[:], 0.0, ALU.mult, ALU.add))
            st.link(nc.vector.tensor_tensor(starts[:], ends[:], padded[:], ALU.subtract))
            st.link(nc.vector.tensor_tensor(pos[:], through[:], total_ps[:], ALU.subtract))
            st.link(nc.vector.tensor_tensor(pos[:], pos[:], rank_ps[:], ALU.add))
            st.link(nc.vector.tensor_tensor(pos[:], pos[:], starts[:].unsqueeze(1).broadcast_to([P, NT, E]), ALU.add))
            for k in range(TOPK):
                st.link(nc.vector.tensor_tensor(picked[:], pos[:], chosen[k][:], ALU.mult))
                st.link(nc.vector.tensor_reduce(place_f[:, k, :], picked[:], AX.X, ALU.add))
            nc.vector.tensor_copy(place[:], place_f[:]).then_inc(places_ready, 1)
            st.link(nc.vector.tensor_tensor(below[:], ends[:].unsqueeze(1).broadcast_to([P, TABLE, E]),
                                            starts_sb[:].unsqueeze(2).broadcast_to([P, TABLE, E]), ALU.is_le))
            st.link(nc.vector.tensor_reduce(tile_e[:], below[:], AX.X, ALU.add))
            st.link(nc.vector.tensor_scalar_min(tile_e[:], tile_e[:], float(E - 1)))
            st.link(nc.vector.tensor_copy(tile_expert[:], tile_e[:]))


def experts_phase(nc, eye, w1_sb, w3_sb, w2_sb, weights_in, weights_count, tile_expert, xs_dram, ys_dram):
    with ExitStack() as ctx:
        kit = Kit(nc, ctx)
        FC = FF // P
        ident = kit.sb("e_ident", [P, P])
        xs = [kit.sb(f"e_xs{s}", [P, C]) for s in range(2)]
        xsT = [kit.sb(f"e_xsT{s}", [P, C]) for s in range(2)]
        act_gate = kit.sb("e_act_gate", [P, FF])
        hidden = kit.sb("e_hidden", [P, FF])
        hT = kit.sb("e_hT", [P, FF])
        ys = [kit.sb(f"e_ys{s}", [P, C]) for s in range(2)]
        xT_ps = kit.ps("e_xT_ps", [P, C])
        gate_ps = [kit.ps(f"e_gate_ps{s}", [P, FF]) for s in range(2)]
        up_ps = [kit.ps(f"e_up_ps{s}", [P, FF]) for s in range(2)]
        hT_ps = kit.ps("e_hT_ps", [P, FF])
        y_ps = kit.ps("e_y_ps", [P, C])

        ident_in = kit.sem("e_ident_in")
        x_in = [kit.sem(f"e_x_in{s}") for s in range(2)]
        x_turned = kit.sem("e_x_turned")
        xT_copied = kit.sem("e_xT_copied")
        gate_done = kit.sem("e_gate_done")
        up_done = kit.sem("e_up_done")
        silu_done = kit.sem("e_silu_done")
        hidden_done = kit.sem("e_hidden_done")
        h_turned = kit.sem("e_h_turned")
        hT_copied = kit.sem("e_hT_copied")
        y_done = kit.sem("e_y_done")
        y_copied = kit.sem("e_y_copied")
        y_stored = [kit.sem(f"e_y_stored{s}") for s in range(2)]
        passed = kit.sem("e_passed")
        from_one = (*y_stored,)
        block = ctx.enter_context(nc.Block())

        def rows(n):
            return bass.ds(n * P, P)

        @block.sync
        def _(sp):
            sp.dma_start(ident[:], eye).then_inc(ident_in, 16)
            for s in range(2):
                sp.dma_start(xs[s][:], xs_dram[rows(s), :]).then_inc(x_in[s], 16)

            def load(n, s):
                sp.wait_ge(x_turned, n - 1)
                pass_wait(sp, passed)
                sp.dma_start(xs[s][:], xs_dram[rows(n), :]).then_inc(x_in[s], 16)

            def store(n, s):
                sp.wait_ge(y_copied, n + 1)
                pass_wait(sp, passed)
                sp.dma_start(ys_dram[rows(n), :], ys[s][:]).then_inc(y_stored[s], 16)

            load(2, 0)
            load(3, 1)
            with sp.Fori(2, TABLE // 2) as it:
                for s in range(2):
                    n = it * 2 + s
                    load(n, s)
                    store(n - 4, s)
            for n in range(TABLE - 4, TABLE):
                store(n, n % 2)
            for s in range(2):
                sp.wait_ge(y_stored[s], 16 * TABLE // 2 + ONE)

        @block.gpsimd
        def _(pool):
            start_at_one(pool, from_one)

        @block.tensor
        def _(pe):
            pe.wait_ge(ident_in, 16)
            pe.wait_ge(weights_in, weights_count)

            def turn_x(n, s):
                pe.wait_ge(x_in[s], (n + (2 - s)) * 8)
                pe.wait_ge(xT_copied, n)
                for k in range(KC):
                    last = nc.tensor.transpose(xT_ps[:, k * P:(k + 1) * P], xs[s][:, k * P:(k + 1) * P], ident[:])
                last.then_inc(x_turned, 1)

            def gate_up(n, s, after):
                e = pe.value_load(tile_expert[0:1, bass.ds(n, 1)], min_val=0, max_val=E - 1)
                pe.wait_ge(xT_copied, n + 1)
                if after:
                    pe.wait_ge(silu_done, n - 1)
                for k in range(KC):
                    last = nc.tensor.matmul(gate_ps[s][:], xsT[s][:, k * P:(k + 1) * P],
                                            w1_sb[:, k, bass.ds(e * FF, FF)], start=(k == 0), stop=(k == KC - 1))
                last.then_inc(gate_done, 1)
                if after:
                    pe.wait_ge(hidden_done, n - 1)
                for k in range(KC):
                    last = nc.tensor.matmul(up_ps[s][:], xsT[s][:, k * P:(k + 1) * P],
                                            w3_sb[:, k, bass.ds(e * FF, FF)], start=(k == 0), stop=(k == KC - 1))
                last.then_inc(up_done, 1)

            def turn_hidden(n):
                pe.wait_ge(hidden_done, n + 1)
                pe.wait_ge(hT_copied, n)
                for k in range(FC):
                    last = nc.tensor.transpose(hT_ps[:, k * P:(k + 1) * P], hidden[:, k * P:(k + 1) * P], ident[:])
                last.then_inc(h_turned, 1)

            def down(n):
                e = pe.value_load(tile_expert[0:1, bass.ds(n, 1)], min_val=0, max_val=E - 1)
                pe.wait_ge(hT_copied, n + 1)
                pe.wait_ge(y_copied, n)
                for k in range(FC):
                    last = nc.tensor.matmul(y_ps[:], hT[:, k * P:(k + 1) * P], w2_sb[:, k, bass.ds(e * C, C)],
                                            start=(k == 0), stop=(k == FC - 1))
                last.then_inc(y_done, 1)

            turn_x(0, 0)
            gate_up(0, 0, False)
            turn_x(1, 1)
            gate_up(1, 1, False)
            turn_hidden(0)
            turn_x(2, 0)
            down(0)
            with pe.Fori(0, TABLE // 2 - 2) as it:
                for s in range(2):
                    n = it * 2 + (2 + s)
                    gate_up(n, s, True)
                    turn_hidden(n - 1)
                    turn_x(n + 1, 1 - s)
                    down(n - 1)
            gate_up(TABLE - 2, 0, True)
            turn_hidden(TABLE - 3)
            turn_x(TABLE - 1, 1)
            down(TABLE - 3)
            gate_up(TABLE - 1, 1, True)
            turn_hidden(TABLE - 2)
            down(TABLE - 2)
            turn_hidden(TABLE - 1)
            down(TABLE - 1)

        @block.scalar
        def _(act):
            def silu(n, s):
                act.wait_ge(gate_done, n + 1)
                act.wait_ge(hidden_done, n)
                nc.scalar.activation(act_gate[:], gate_ps[s][:], ACT.Silu).then_inc(silu_done, 1)

            def copy_hT(n):
                act.wait_ge(h_turned, n + 1)
                act.wait_ge(y_done, n)
                nc.scalar.activation(hT[:], hT_ps[:], ACT.Copy).then_inc(hT_copied, 1)

            silu(0, 0)
            silu(1, 1)
            copy_hT(0)
            with act.Fori(0, TABLE // 2 - 1) as it:
                for s in range(2):
                    n = it * 2 + (2 + s)
                    silu(n, s)
                    copy_hT(n - 1)
            copy_hT(TABLE - 1)

        @block.vector
        def _(dve):
            def copy_xT(n, s, after):
                dve.wait_ge(x_turned, n + 1)
                if after:
                    dve.wait_ge(up_done, n - 1)
                nc.vector.tensor_copy(xsT[s][:], xT_ps[:]).then_inc(xT_copied, 1)

            def hide(n, s):
                dve.wait_ge(silu_done, n + 1)
                dve.wait_ge(up_done, n + 1)
                dve.wait_ge(h_turned, n)
                nc.vector.tensor_tensor(hidden[:], up_ps[s][:], act_gate[:], ALU.mult).then_inc(hidden_done, 1)

            def copy_y(n, s):
                dve.wait_ge(y_done, n + 1)
                dve.wait_ge(y_stored[s], (n - s) * 8 + ONE)
                nc.vector.tensor_copy(ys[s][:], y_ps[:]).then_inc(y_copied, 1)

            copy_xT(0, 0, False)
            copy_xT(1, 1, False)
            hide(0, 0)
            copy_xT(2, 0, True)
            hide(1, 1)
            copy_y(0, 0)
            with dve.Fori(0, TABLE // 2 - 2) as it:
                for s in range(2):
                    n = it * 2 + (2 + s)
                    copy_xT(n + 1, 1 - s, True)
                    hide(n, s)
                    copy_y(n - 1, 1 - s)
            copy_xT(TABLE - 1, 1, True)
            hide(TABLE - 2, 0)
            copy_y(TABLE - 3, 1)
            hide(TABLE - 1, 1)
            copy_y(TABLE - 2, 0)
            copy_y(TABLE - 1, 1)


def gather_phase(nc, x1, place, weight, ys_dram, out):
    with ExitStack() as ctx:
        kit = Kit(nc, ctx)
        SLOTS = 4
        rows_sb = [[kit.sb(f"g_rows{s}_{k}", [P, TPC, C]) for k in range(TOPK)] for s in range(SLOTS)]
        x1_sb = [kit.sb(f"g_x1_{s}", [P, TPC, C]) for s in range(SLOTS)]
        out_sb = [kit.sb(f"g_out{s}", [P, TPC, C]) for s in range(2)]
        mixed = kit.sb("g_mixed", [P, TPC, C])
        normed = kit.sb("g_normed", [P, TPC, C])
        stats = kit.sb("g_stats", [P, TPC, 6])
        mv = kit.sb("g_mv", [P, TPC, 2])
        var_eps = kit.sb("g_var_eps", [P, TPC])
        std = kit.sb("g_std", [P, TPC])
        rstd = kit.sb("g_rstd", [P, TPC])
        rows_in = [kit.sem(f"g_rows_in{s}") for s in range(SLOTS)]
        x1_in = [kit.sem(f"g_x1_in{s}") for s in range(SLOTS)]
        mixed_done = kit.sem("g_mixed_done")
        step = kit.sem("g_step")
        var_ready = kit.sem("g_var_ready")
        std_ready = kit.sem("g_std_ready")
        out_ready = kit.sem("g_out_ready")
        stored = [kit.sem(f"g_stored{s}") for s in range(2)]
        block = ctx.enter_context(nc.Block())
        ROWS_IN = TPC * TOPK * 16
        STEPS_HERE = 5

        @block.gpsimd
        def _(pool):
            for n in range(NCH):
                if n >= SLOTS:
                    pool.wait_ge(mixed_done, n - SLOTS + 1)
                for j in range(TPC):
                    for k in range(TOPK):
                        t = n * TPC + j
                        pool.indirect_dma_start(out=rows_sb[n % SLOTS][k][:, j, :], out_offset=None, in_=ys_dram,
                                                in_offset=bass.IndirectOffsetOnAxis(ap=place[:, k, t:t + 1], axis=0)
                                                ).then_inc(rows_in[n % SLOTS], 16)

        @block.vector
        def _(dve):
            for n in range(NCH):
                st = Steps(dve, step, n * STEPS_HERE)
                s = n % SLOTS
                dve.wait_ge(rows_in[s], (n // SLOTS + 1) * ROWS_IN)
                for j in range(TPC):
                    t = n * TPC + j
                    last = nc.vector.tensor_scalar(mixed[:, j, :], rows_sb[s][0][:, j, :], weight[:, 0, t:t + 1], None,
                                                   ALU.mult)
                st.link(last)
                for j in range(TPC):
                    t = n * TPC + j
                    last = nc.vector.scalar_tensor_tensor(out=mixed[:, j, :], in0=rows_sb[s][1][:, j, :],
                                                          scalar=weight[:, 1, t:t + 1], in1=mixed[:, j, :],
                                                          op0=ALU.mult, op1=ALU.add)
                last.then_inc(mixed_done, 1)
                dve.wait_ge(mixed_done, n + 1)
                for j in range(TPC):
                    last = nc.vector.bn_stats(stats[:, j, :], mixed[:, j, :])
                st.link(last)
                for j in range(TPC):
                    last = nc.vector.bn_aggr(mv[:, j, :], stats[:, j, :])
                st.link(last)
                nc.vector.tensor_scalar_add(var_eps[:], mv[:, :, 1], EPS).then_inc(var_ready, 1)
                dve.wait_ge(std_ready, n + 1)
                st.link(nc.vector.reciprocal(rstd[:], std[:]))
                for j in range(TPC):
                    last = nc.vector.tensor_scalar(normed[:, j, :], mixed[:, j, :], mv[:, j, 0:1], rstd[:, j:j + 1],
                                                   ALU.subtract, ALU.mult)
                st.link(last)
                if n >= 2:
                    dve.wait_ge(stored[n % 2], 16 * (n // 2))
                dve.wait_ge(x1_in[s], (n // SLOTS + 1) * 16)
                nc.vector.tensor_tensor(out_sb[n % 2][:], normed[:], x1_sb[s][:], ALU.add).then_inc(out_ready, 1)

        @block.scalar
        def _(act):
            for n in range(NCH):
                act.wait_ge(var_ready, n + 1)
                nc.scalar.activation(std[:], var_eps[:], ACT.Sqrt).then_inc(std_ready, 1)

        @block.sync
        def _(sp):
            def load_x1(n):
                sp.dma_start(x1_sb[n % SLOTS][:], x1[n * CH:(n + 1) * CH, :].rearrange(
                    "(j p) c -> p j c", p=P)).then_inc(x1_in[n % SLOTS], 16)

            for n in range(SLOTS):
                load_x1(n)
            for n in range(NCH):
                sp.wait_ge(out_ready, n + 1)
                if n + SLOTS < NCH:
                    load_x1(n + SLOTS)
                sp.dma_start(out[n * CH:(n + 1) * CH, :].rearrange("(j p) c -> p j c", p=P),
                             out_sb[n % 2][:]).then_inc(stored[n % 2], 16)
            for s in range(2):
                sp.wait_ge(stored[s], 16 * NCH // 2)


def block_program(nc, x, wq, wk, wv, wo, wr, br, w1, w3, w2, eye, tri, tile_starts, q_rows, k_rows, masks, out):
    x = x.rearrange("b t c -> (b t) c")
    out = out.rearrange("b t c -> (b t) c")
    q_parts = nc.dram_tensor("q_parts", [G, PART_ROWS, HPG, T], BF16).ap()
    k_parts = nc.dram_tensor("k_parts", [G, PART_ROWS, HPG, T], BF16).ap()
    v_aug = nc.dram_tensor("v_aug", [T, NH * 32], F32).ap()
    o_dram = nc.dram_tensor("o_heads", [G, P, T], F32).ap()
    xs_dram = nc.dram_tensor("table_x", [TABLE * P, C], F32).ap()
    x1 = nc.dram_tensor("x1", [T, C], F32).ap()
    ys_dram = nc.dram_tensor("table_y", [TABLE * P, C], F32).ap()

    project_phase(nc, x, wq, wk, wv, eye, q_parts, k_parts, v_aug)
    with ExitStack() as ctx:
        kit = Kit(nc, ctx)
        w1_sb = kit.sb("w1", [P, KC, E * FF])
        w3_sb = kit.sb("w3", [P, KC, E * FF])
        w2_sb = kit.sb("w2", [P, FF // P, E * C])
        weights_in = kit.sem("expert_weights_in")
        loads = [(w1_sb[:, :, e * FF:(e + 1) * FF], w1[e].rearrange("(k p) f -> p k f", p=P)) for e in range(E)]
        loads += [(w3_sb[:, :, e * FF:(e + 1) * FF], w3[e].rearrange("(k p) f -> p k f", p=P)) for e in range(E)]
        loads += [(w2_sb[:, :, e * C:(e + 1) * C], w2[e].rearrange("(k p) c -> p k c", p=P)) for e in range(E)]
        attention_phase(nc, q_parts, k_parts, v_aug, q_rows, k_rows, masks, o_dram, xs_dram, loads, weights_in)
        place = kit.sb("place", [P, TOPK, NT], U32)
        weight = kit.sb("weight", [P, TOPK, NT])
        tile_expert = kit.sb("tile_expert", [P, TABLE], I32)
        with ExitStack() as routing:
            kit = Kit(nc, routing)
            xn2 = kit.sb("xn2", [P, NT, C])
            top_val = kit.sb("top_val", [P, NT, TOPK])
            top_idx = kit.sb("top_idx", [P, NT, TOPK])
            combine_phase(nc, x, wo, wr, br, eye, o_dram, x1, xn2, top_val, top_idx)
            route_phase(nc, tri, tile_starts, xn2, top_val, top_idx, place, weight, tile_expert, xs_dram)
        experts_phase(nc, eye, w1_sb, w3_sb, w2_sb, weights_in, 16 * len(loads), tile_expert, xs_dram, ys_dram)
        gather_phase(nc, x1, place, weight, ys_dram, out)


INPUTS = ("L0_attn_x", "L0_attn_Wq", "L0_attn_Wk", "L0_attn_Wv", "L0_attn_Wo", "L0_ffn_Wr", "L0_ffn_br",
          "L0_ffn_W1", "L0_ffn_W3", "L0_ffn_W2")
CONSTANTS = ("eye", "tri", "tile_starts", "q_rows", "k_rows", "masks")


def kernel(**inputs):
    import numpy as np
    import concourse.bacc as bacc
    from concourse.bass_utils import run_bass_kernel_spmd

    nc = bacc.Bacc("TRN2", target_bir_lowering=False, num_devices=1)
    constants = host_constants()
    arrays, args = {}, []
    for name in INPUTS + CONSTANTS:
        a = np.ascontiguousarray(inputs[name] if name in inputs else constants[name])
        arrays[name] = a
        args.append(nc.dram_tensor(name, a.shape, mybir.dt.from_np(a.dtype), kind="ExternalInput").ap())
    out = nc.dram_tensor("out", (1, T, C), F32, kind="ExternalOutput").ap()
    block_program(nc, *args, out)
    result = run_bass_kernel_spmd(nc, [arrays], core_ids=[0])
    return result.results[0]["out"]
```

```python
from contextlib import ExitStack

import concourse.bass as bass
from concourse import mybir

ALU = mybir.AluOpType
ACT = mybir.ActivationFunctionType
AX = mybir.AxisListType
F32 = mybir.dt.float32
BF16 = mybir.dt.bfloat16
I32 = mybir.dt.int32
U32 = mybir.dt.uint32

P = 128
T, C = 4096, 256
NH, HD = 16, 16
E, FF, TOPK = 8, 512, 2
KC = C // P
CH = 512
NCH = T // CH
TPC = CH // P
NT = T // P
G, HPG = 4, 4
EPS = 1e-5
ONE = 1
SCALE = HD ** -0.5

Q_PARTS = (1, 1, 2, 0, 0, 0)
K_PARTS = (0, 1, 0, 0, 1, 2)
PROD = len(Q_PARTS) * HD
MAXROW = PROD
ROWS = PROD + 6
PART_ROWS = 3 * HD

ROUTE_TILES = (TOPK * T + E * (P - 1)) // P
TILES = ROUTE_TILES + ROUTE_TILES % 2
TABLE_ROWS = (E - 1) * T + TILES * P


def slopes():
    import numpy as np

    start = 2.0 ** (-(2.0 ** -(NH.bit_length() - 1 - 3)))
    return np.array([start * start ** i for i in range(NH)], np.float32)


def host_constants():
    import numpy as np

    bf16 = np.dtype(mybir.dt.np(BF16))
    f32 = np.float32
    bias = slopes()[:, None] * (np.arange(T, dtype=f32) - f32(511))
    high = bias.astype(bf16)
    mid = (bias - high.astype(f32)).astype(bf16)
    low = (bias - high.astype(f32) - mid.astype(f32)).astype(bf16)
    k_rows = np.ones((G, 6, HPG, T), bf16)
    for n, part in enumerate((high, mid, low)):
        k_rows[:, 3 + n] = part.reshape(G, HPG, T)
    q_rows = np.zeros((6, HPG, CH), bf16)
    q_rows[3:] = 1
    future = np.triu(np.ones((P, P), f32), 1) * f32(-1e30)
    masks = np.stack([np.eye(P, dtype=f32), future, future.T]).astype(bf16)
    tri = np.triu(np.ones((P, P), f32), 1)
    tile_starts = (np.arange(TILES) * P).astype(f32)
    return {"eye": np.eye(P, dtype=f32), "tri": tri, "tile_starts": tile_starts, "q_rows": q_rows, "k_rows": k_rows, "masks": masks}


class Kit:

    def __init__(self, nc, ctx):
        self.nc, self.ctx = nc, ctx

    def sb(self, name, shape, dt=F32):
        return self.ctx.enter_context(self.nc.sbuf_tensor(name, shape, dt))

    def ps(self, name, shape, dt=F32):
        return self.ctx.enter_context(self.nc.psum_tensor(name, shape, dt))

    def sem(self, name):
        return self.ctx.enter_context(self.nc.semaphore(name))


def start_at_one(eng, semaphores):
    for semaphore in semaphores:
        eng.sem_inc(semaphore, ONE)


def pass_wait(eng, passed):
    eng.sem_inc(passed, 1)


def project_phase(nc, x, wq, wk, wv, eye, q_parts, k_parts, v_aug):
    with ExitStack() as ctx:
        kit = Kit(nc, ctx)
        ident = kit.sb("p_ident", [P, P])
        w_raw = [kit.sb(f"p_w{n}_raw", [P, KC, C]) for n in "qk"]
        w_sb = [kit.sb(f"p_w{n}", [P, KC, C]) for n in "qkv"]
        x_sb = [kit.sb(f"p_x{s}", [P, TPC, C]) for s in range(2)]
        xn = kit.sb("p_xn", [P, TPC, C])
        stats = kit.sb("p_stats", [P, TPC, 6])
        mv = kit.sb("p_mv", [P, TPC, 2])
        var_eps = kit.sb("p_var_eps", [P, TPC])
        std = kit.sb("p_std", [P, TPC])
        rstd = kit.sb("p_rstd", [P, TPC])
        xnT = [kit.sb(f"p_xnT{s}", [P, KC, CH]) for s in range(2)]
        rest = kit.sb("p_rest", [P, CH])
        parts = [kit.sb(f"p_parts{s}", [P, 4, 3, CH], BF16) for s in range(2)]
        v_st = [kit.sb(f"p_v{s}", [P, TPC, NH, 32]) for s in range(2)]
        xT_ps = kit.ps("p_xT_ps", [P, KC, CH])
        qk_ps = kit.ps("p_qk_ps", [P, 4, CH])
        v_ps = kit.ps("p_v_ps", [P, 2, 2, C])

        ident_in = kit.sem("p_ident_in")
        weights_in = kit.sem("p_weights_in")
        weights_ordered = kit.sem("p_weights_ordered")
        x_in = [kit.sem(f"p_x_in{s}") for s in range(2)]
        v_ones = kit.sem("p_v_ones")
        ln = kit.sem("p_ln")
        split_step = kit.sem("p_split_step")
        var_ready = kit.sem("p_var_ready")
        std_ready = kit.sem("p_std_ready")
        xn_ready = kit.sem("p_xn_ready")
        transposed = kit.sem("p_transposed")
        xT_ready = kit.sem("p_xT_ready")
        qk_done = kit.sem("p_qk_done")
        v_done = kit.sem("p_v_done")
        high_ready = kit.sem("p_high_ready")
        split_done = kit.sem("p_split_done")
        v_ready = kit.sem("p_v_ready")
        qk_stored = [kit.sem(f"p_qk_stored{s}") for s in range(2)]
        v_stored = [kit.sem(f"p_v_stored{s}") for s in range(2)]
        passed = kit.sem("p_passed")
        from_one = (transposed, v_done, *qk_stored, *v_stored, xT_ready, split_done, v_ready)
        block = ctx.enter_context(nc.Block())
        STORES = 4 * 2
        LN_STEPS, SPLIT_STEPS = 3, 2 * 4

        def pipelined(eng, ahead, main):
            ahead(0, 0)
            with eng.Fori(0, NCH // 2 - 1) as it:
                for s in range(2):
                    main(it * 2 + s, s, True)
            main(NCH - 2, 0, True)
            main(NCH - 1, 1, False)

        @block.gpsimd
        def _(pool):
            start_at_one(pool, from_one)
            pool.dma_start(ident[:], eye).then_inc(ident_in, 16)
            for w, src in zip((*w_raw, w_sb[2]), (wq, wk, wv)):
                pool.dma_start(w[:], src.rearrange("(k p) n -> p k n", p=P)).then_inc(weights_in, 16)
            pool.wait_ge(weights_in, 48)
            for w, raw in zip(w_sb, w_raw):
                for k in range(KC):
                    last = pool.tensor_copy(w[:, k, :].rearrange("p (g d h) -> p g h d", g=G, d=HD),
                                            raw[:, k, :].rearrange("p (g h d) -> p g h d", g=G, d=HD))
            last.then_inc(weights_ordered, 1)
            for s in range(2):
                pool.memset(v_st[s][:, :, :, HD:HD + 1], 1.0)
                last = pool.memset(v_st[s][:, :, :, HD + 1:32], 0.0)
            last.then_inc(v_ones, 1)

        @block.sync
        def _(sp):
            def load_x(n, s):
                sp.dma_start(x_sb[s][:], x[bass.ds(n * CH, CH), :].rearrange("(j p) c -> p j c", p=P)).then_inc(
                    x_in[s], 16)

            def stores(n, s, n_more):
                if n_more:
                    sp.wait_ge(xn_ready, n + 1)
                    pass_wait(sp, passed)
                    load_x(n + 2, s)
                for t in range(4):
                    sp.wait_ge(split_done, n * 4 + (t + 1) + ONE)
                    pass_wait(sp, passed)
                    store = (q_parts, k_parts)[t // 2]
                    for gg in range(2):
                        dst = store[2 * (t % 2) + gg, 0:PART_ROWS, :, bass.ds(n * CH, CH)].rearrange(
                            "(part d) h t -> (d h) part t", d=HD)
                        sp.dma_start(dst, parts[s][64 * gg:64 * gg + 64, t, :, :]).then_inc(qk_stored[s], 16)
                sp.wait_ge(v_ready, n * 2 + 2 + ONE)
                pass_wait(sp, passed)
                sp.dma_start(v_aug[bass.ds(n * CH, CH), :].rearrange("(j p) f -> p j f", p=P),
                             v_st[s][:].rearrange("p j h e -> p j (h e)")).then_inc(v_stored[s], 16)

            load_x(0, 0)
            load_x(1, 1)
            with sp.Fori(0, NCH // 2 - 1) as it:
                for s in range(2):
                    stores(it * 2 + s, s, True)
            stores(NCH - 2, 0, False)
            stores(NCH - 1, 1, False)
            for s in range(2):
                sp.wait_ge(qk_stored[s], 16 * STORES * NCH // 2 + ONE)
                sp.wait_ge(v_stored[s], 16 * NCH // 2 + ONE)

        @block.vector
        def _(dve):
            def norm(n, s):
                base = n * LN_STEPS
                dve.wait_ge(x_in[s], (n + (2 - s)) * 8)
                for j in range(TPC):
                    last = nc.vector.bn_stats(stats[:, j, :], x_sb[s][:, j, :])
                last.then_inc(ln, 1)
                dve.wait_ge(ln, base + 1)
                pass_wait(dve, passed)
                for j in range(TPC):
                    last = nc.vector.bn_aggr(mv[:, j, :], stats[:, j, :])
                last.then_inc(ln, 1)
                dve.wait_ge(ln, base + 2)
                nc.vector.tensor_scalar_add(var_eps[:], mv[:, :, 1], EPS).then_inc(var_ready, 1)
                dve.wait_ge(std_ready, n + 1)
                nc.vector.reciprocal(rstd[:], std[:]).then_inc(ln, 1)
                dve.wait_ge(ln, base + 3)
                dve.wait_ge(transposed, n + ONE)
                for j in range(TPC):
                    last = nc.vector.tensor_scalar(xn[:, j, :], x_sb[s][:, j, :], mv[:, j, 0:1],
                                                   rstd[:, j:j + 1], ALU.subtract, ALU.mult)
                last.then_inc(xn_ready, 1)

            def split(n, s, more):
                if more:
                    norm(n + 1, 1 - s)
                for t in range(4):
                    base = n * SPLIT_STEPS + 2 * t
                    dve.wait_ge(high_ready, n * 4 + (t + 1))
                    nc.vector.scalar_tensor_tensor(
                        out=rest[:], in0=qk_ps[:, t, :], scalar=SCALE if t < 2 else 1.0,
                        in1=parts[s][:, t, 0, :], op0=ALU.mult, op1=ALU.subtract).then_inc(split_step, 1)
                    dve.wait_ge(split_step, base + 1)
                    nc.vector.tensor_copy(parts[s][:, t, 1, :], rest[:]).then_inc(split_step, 1)
                    dve.wait_ge(split_step, base + 2)
                    nc.vector.tensor_tensor(parts[s][:, t, 2, :], rest[:], parts[s][:, t, 1, :],
                                            ALU.subtract).then_inc(split_done, 1)
                    dve.wait_ge(split_done, n * 4 + (t + 1) + ONE)

            pipelined(dve, norm, split)

        @block.scalar
        def _(act):
            def take_std(n):
                act.wait_ge(var_ready, n + 1)
                nc.scalar.activation(std[:], var_eps[:], ACT.Sqrt).then_inc(std_ready, 1)

            def copy_xT(n, s, after):
                act.wait_ge(transposed, n + 1 + ONE)
                if after:
                    act.wait_ge(v_done, (n - 1) * 2 + ONE)
                for k in range(KC):
                    last = nc.scalar.activation(xnT[s][:, k, :], xT_ps[:, k, :], ACT.Copy)
                last.then_inc(xT_ready, 1)

            def begin(n, s):
                take_std(n)
                copy_xT(n, s, False)
                act.wait_ge(v_ones, 1)

            def take_out(n, s, more):
                if more:
                    take_std(n + 1)
                act.wait_ge(qk_stored[s], (n - s) * (8 * STORES) + ONE)
                for t in range(4):
                    act.wait_ge(qk_done, n * 4 + (t + 1))
                    nc.scalar.activation(parts[s][:, t, 0, :], qk_ps[:, t, :], ACT.Copy,
                                         scale=SCALE if t < 2 else 1.0).then_inc(high_ready, 1)
                if more:
                    copy_xT(n + 1, 1 - s, True)
                act.wait_ge(v_stored[s], (n - s) * 8 + ONE)
                for u in range(2):
                    act.wait_ge(v_done, n * 2 + (u + 1) + ONE)
                    nc.scalar.activation(v_st[s][:, 2 * u:2 * u + 2, :, 0:HD],
                                         v_ps[:, u, :, :].rearrange("p j (h d) -> p j h d", h=NH),
                                         ACT.Copy).then_inc(v_ready, 1)

            pipelined(act, begin, take_out)

        @block.tensor
        def _(pe):
            def turn(n, s):
                pe.wait_ge(xn_ready, n + 1)
                pe.wait_ge(xT_ready, n + ONE)
                for k in range(KC):
                    for j in range(TPC):
                        last = nc.tensor.transpose(xT_ps[:, k, j * P:(j + 1) * P],
                                                   xn[:, j, k * P:(k + 1) * P], ident[:])
                last.then_inc(transposed, 1)

            def begin(n, s):
                pe.wait_ge(ident_in, 16)
                turn(n, s)
                pe.wait_ge(weights_in, 48)
                pe.wait_ge(weights_ordered, 1)

            def products(n, s, more):
                pe.wait_ge(xT_ready, n + 1 + ONE)
                pe.wait_ge(split_done, n * 4 + ONE)
                for t in range(4):
                    w, m = w_sb[t // 2], t % 2
                    for k in range(KC):
                        last = nc.tensor.matmul(qk_ps[:, t, :], w[:, k, m * P:(m + 1) * P], xnT[s][:, k, :],
                                                start=(k == 0), stop=(k == KC - 1))
                    last.then_inc(qk_done, 1)
                if more:
                    turn(n + 1, 1 - s)
                pe.wait_ge(v_ready, n * 2 + ONE)
                for j in range(TPC):
                    for k in range(KC):
                        last = nc.tensor.matmul(v_ps[:, j // 2, j % 2, :], xnT[s][:, k, j * P:(j + 1) * P],
                                                w_sb[2][:, k, :], start=(k == 0), stop=(k == KC - 1))
                    if j % 2:
                        last.then_inc(v_done, 1)

            pipelined(pe, begin, products)


def chunk_steps(c):
    return TPC * (c + 1)


STEPS = sum(chunk_steps(c) for c in range(NCH))
UNITS = STEPS * HPG
STEP0 = [sum(chunk_steps(d) for d in range(c)) for c in range(NCH + 1)]
LEAD = 3
TURN_GAP = 4
Q_RELOAD = 16
RELOAD = 10
TAIL = 8


def max_units(c):
    return [(kc, j, hp) for kc in range(c + 1) for j in range(TPC) for hp in range(2)]


def max_unit0(c):
    return c // NCH * MAX_UNITS + sum(len(max_units(d)) for d in range(c % NCH))


MAX_UNITS = sum(len(max_units(c)) for c in range(NCH))


def turn_behind(c):
    return 0 if c % NCH == NCH - 1 else 4


def max_events(c):
    events = [("unit", c, i) for i in range(len(max_units(c % NCH)))]
    if c > 0:
        events.insert(turn_behind(c - 1), ("turn", c - 1))
    return events


def group_plan():
    deadlines = [(STEP0[c] * HPG - TAIL, max_unit0(c + 1)) for c in range(LEAD, NCH)]
    at, done = Q_RELOAD, max_unit0(LEAD)
    after = {}
    place = {}
    while deadlines:
        knot = max(deadlines, key=lambda d: (d[1] - done) / (d[0] - at))
        for m in range(done, knot[1]):
            place[m] = at + (m - done) * (knot[0] - at) // (knot[1] - done)
        deadlines = [d for d in deadlines if d[0] > knot[0]]
        at, done = knot
    at = (STEP0[NCH - 1] + TPC) * HPG + RELOAD
    for m in range(done, max_unit0(NCH + LEAD)):
        place[m] = at + (m - done) * (UNITS - TAIL - at) // (max_unit0(NCH + LEAD) - done)
    u = 0
    for c in range(LEAD, NCH + LEAD):
        for what in max_events(c):
            if what[0] == "unit":
                u = max(u, place[max_unit0(c) + what[2]])
            elif turn_behind(what[1]) == 0:
                u += TURN_GAP
            if c >= NCH and what[0] == "unit":
                u = max(u, (STEP0[NCH - 1] + TPC * (c - NCH + 1)) * HPG + RELOAD)
            u = min(u, UNITS - 1)
            after.setdefault(u, []).append(what)
    return after


def attention_phase(nc, q_parts, k_parts, v_aug, q_rows, k_rows, masks, o_dram, table, weight_loads, weights_in):
    with ExitStack() as ctx:
        kit = Kit(nc, ctx)
        SLOTS_Q, SLOTS_ST, SLOTS_P = LEAD + 1, 3, 3
        assert NCH % SLOTS_Q == 0
        PLAN = group_plan()
        IN_ORDER = [w for c in range(NCH + LEAD) for w in max_events(c)]
        EVENTS = MAX_UNITS + NCH
        assert EVENTS % 2 == 0 and STEPS % SLOTS_P == 0 and UNITS % SLOTS_ST == 0
        k_sb = kit.sb("a_k", [P, HPG, T], BF16)
        v_sb = kit.sb("a_v", [P, NT, HPG * 32])
        q_sb = [kit.sb(f"a_q{s}", [P, HPG, CH], BF16) for s in range(SLOTS_Q)]
        probs = [kit.sb(f"a_p{s}", [P, HPG, CH]) for s in range(SLOTS_P)]
        o_sb = [kit.sb(f"a_o{s}", [P, CH]) for s in range(2)]
        ZEROS = 2048
        zeros = kit.sb("a_zeros", [P, ZEROS])
        ident = kit.sb("a_ident", [P, P], BF16)
        mask_q = kit.sb("a_mask_q", [P, P], BF16)
        mask_k = kit.sb("a_mask_k", [P, P], BF16)
        part_max = kit.sb("a_part_max", [P, TPC * HPG, NCH])
        neg_max = kit.sb("a_neg_max", [P, TPC, HPG])
        max_rest = kit.sb("a_max_rest", [P, TPC, HPG])
        max_cols = kit.sb("a_max_cols", [P, TPC, HPG, 32], BF16)

        st_ps = kit.ps("a_st_ps", [P, SLOTS_ST, CH])
        mx_ps = [kit.ps(f"a_mx_ps{s}", [P, 2, CH]) for s in range(2)]
        ot_ps = kit.ps("a_ot_ps", [P, CH])

        consts_in = kit.sem("a_consts_in")
        cols_zero = kit.sem("a_cols_zero")
        zeros_ready = kit.sem("a_zeros_ready")
        table_zeroed = kit.sem("a_table_zeroed")
        q_in = [kit.sem(f"a_q_in{s}") for s in range(SLOTS_Q)]
        k_in = [kit.sem(f"a_k_in{n}") for n in range(NCH)]
        v_in = [kit.sem(f"a_v_in{n}") for n in range(NCH)]
        scores_ready = kit.sem("a_scores_ready")
        probs_ready = kit.sem("a_probs_ready")
        pv_done = kit.sem("a_pv_done")
        o_copied = kit.sem("a_o_copied")
        o_stored = [kit.sem(f"a_o_stored{s}") for s in range(2)]
        max_ready = kit.sem("a_max_ready")
        max_reduced = kit.sem("a_max_reduced")
        max_step = kit.sem("a_max_step")
        cols_ready = kit.sem("a_cols_ready")
        turned = kit.sem("a_turned")
        rows_written = kit.sem("a_rows_written")
        passed = kit.sem("a_passed")
        from_one = (scores_ready, *o_stored, o_copied)
        block = ctx.enter_context(nc.Block())
        Q_LOAD, K_LOAD = 4 * 16, 4 * 16
        MAX_STEPS = 4

        EVENT = {what: n for n, what in enumerate(IN_ORDER)}

        def in_group(what, last_group):
            return what[1] < NCH or not last_group

        def load_q(eng, g, c):
            dst, tok = q_sb[c % SLOTS_Q], slice(c * CH, (c + 1) * CH)
            done = q_in[c % SLOTS_Q]
            for part in range(3):
                first, times = Q_PARTS.index(part), Q_PARTS.count(part)
                src = q_parts[g, part * HD:(part + 1) * HD, :, tok]
                eng.dma_start(dst[first * HD:(first + times) * HD, :, :],
                              src.unsqueeze(0).broadcast_to([times, HD, HPG, CH])).then_inc(done, 16)
            eng.dma_start(dst[PROD:ROWS, :, :], q_rows).then_inc(done, 16)

        def load_k(eng, g, n):
            tok = slice(n * CH, (n + 1) * CH)
            for r0, r1 in ((0, 2 * HD), (2 * HD, PART_ROWS), (PART_ROWS, PROD)):
                eng.dma_start(k_sb[r0:r1, :, tok], k_parts[g, 0:r1 - r0, :, tok]).then_inc(k_in[n], 16)
            eng.dma_start(k_sb[PROD:ROWS, :, tok], k_rows[g, :, :, tok]).then_inc(k_in[n], 16)
            eng.dma_start(v_sb[:, n * TPC:(n + 1) * TPC, :],
                          v_aug[tok, :].rearrange("(b p) (g f) -> g p b f", p=P, g=G)[g]).then_inc(v_in[n], 16)

        @block.gpsimd
        def _(pool):
            start_at_one(pool, from_one)
            pool.dma_start(ident[:], masks[0]).then_inc(consts_in, 16)
            pool.dma_start(mask_q[:], masks[1]).then_inc(consts_in, 16)
            pool.dma_start(mask_k[:], masks[2]).then_inc(consts_in, 16)
            pool.memset(max_cols[:], 0.0).then_inc(cols_zero, 1)
            pool.memset(zeros[:], 0.0).then_inc(zeros_ready, 1)
            pool.wait_ge(zeros_ready, 1)
            flat = table.rearrange("(p r) c -> p (r c)", p=P)
            fills = [(flat[:, f:f + ZEROS], zeros[:], table_zeroed) for f in range(0, flat.shape[1], ZEROS)]
            background = fills + [(dst, src, weights_in) for dst, src in weight_loads]
            for n, (dst, src, done) in enumerate(background):
                pool.wait_ge(scores_ready, (n + 1) * (G - 1) * UNITS // len(background) + ONE)
                pool.dma_start(dst, src).then_inc(done, 16)
            pool.wait_ge(table_zeroed, 16 * len(fills))

        @block.sync
        def _(sp):
            def store_o(g, c):
                sp.wait_ge(o_copied, g * NCH + (c + 1) + ONE)
                pass_wait(sp, passed)
                sp.dma_start(o_dram[g, :, c * CH:(c + 1) * CH], o_sb[c % 2][:]).then_inc(o_stored[c % 2], 16)

            for c in range(LEAD):
                load_q(sp, 0, c)
                load_k(sp, 0, c)
            for n in range(LEAD, NCH):
                load_k(sp, 0, n)
            def group(g, nxt):
                for c in range(NCH):
                    if c + LEAD < NCH or nxt is not None:
                        sp.wait_ge(scores_ready, g * UNITS + STEP0[c] * HPG + ONE)
                        pass_wait(sp, passed)
                        load_q(sp, g if c + LEAD < NCH else nxt, (c + LEAD) % NCH)
                    if c > 0:
                        store_o(g, c - 1)
                for n in range(NCH if nxt is not None else 0):
                    last_step = STEP0[NCH - 1] + TPC * (n + 1)
                    sp.wait_ge(scores_ready, g * UNITS + last_step * HPG + ONE)
                    pass_wait(sp, passed)
                    sp.wait_ge(pv_done, g * STEPS + last_step)
                    pass_wait(sp, passed)
                    load_k(sp, nxt, n)
                store_o(g, NCH - 1)

            with sp.Fori(0, G - 1) as g:
                group(g, g + 1)
            group(G - 1, None)
            for s in range(2):
                sp.wait_ge(o_stored[s], 16 * G * NCH // 2 + ONE)

        @block.tensor
        def _(pe):
            pe.wait_ge(consts_in, 48)

            def wait_slot(g, n):
                if n < 2:
                    return
                what, c, *i = IN_ORDER[n - 2]
                if what == "unit":
                    pe.wait_ge(max_reduced, g * MAX_UNITS + (max_unit0(c) + i[0] + 1))
                else:
                    pe.wait_ge(rows_written, (g * NCH + (c + 1)) * HPG)

            def max_unit(slot, c, kc, j, hp):
                diagonal = kc == c % NCH
                width = (j + 1) * P if diagonal else CH
                for hh in range(2):
                    h = 2 * hp + hh
                    last = nc.tensor.matmul(mx_ps[slot][:, hh, 0:width], q_sb[c % SLOTS_Q][0:ROWS, h, j * P:(j + 1) * P],
                                            k_sb[0:ROWS, h, kc * CH:kc * CH + width], start=True, stop=not diagonal)
                    if diagonal:
                        last = nc.tensor.matmul(mx_ps[slot][:, hh, width - P:width], ident[:], mask_q[:],
                                                start=False, stop=True)
                last.then_inc(max_ready, 1)

            def turn(slot):
                for j in range(TPC):
                    last = nc.tensor.matmul(mx_ps[slot][:, 0, j * P:(j + 1) * P],
                                            max_cols[:, j, :, :].rearrange("p h e -> p (h e)"), ident[:],
                                            start=True, stop=True)
                last.then_inc(turned, 1)

            def max_event(g, what, c, i=None):
                n = EVENT[(what, c) if i is None else (what, c, i)]
                if what == "unit":
                    kc, j, hp = max_units(c % NCH)[i]
                    if i == 0:
                        pe.wait_ge(q_in[c % SLOTS_Q], (g * (NCH // SLOTS_Q) + (c // SLOTS_Q + 1)) * Q_LOAD)
                    if kc == c % NCH and j == 0 and hp == 0:
                        pe.wait_ge(k_in[kc], (g + (c // NCH + 1)) * K_LOAD)
                    wait_slot(g, n)
                    max_unit(n % 2, c, kc, j, hp)
                else:
                    wait_slot(g, n)
                    pe.wait_ge(cols_ready, g * NCH + (c + 1))
                    turn(n % 2)

            for c in range(LEAD):
                for what in max_events(c):
                    max_event(0, *what)

            def group(g, last_group):
                def pv(c, b):
                    n = TPC * c
                    q0 = max(0, b - n) * P
                    s = STEP0[c] + b
                    if b == 0:
                        pe.wait_ge(o_copied, g * NCH + c + ONE)
                    if b >= n and c == b // TPC and b % TPC == 0:
                        pe.wait_ge(v_in[c], (g + 1) * 16)
                    pe.wait_ge(probs_ready, g * UNITS + (s + 1) * HPG)
                    for h in range(HPG):
                        last = nc.tensor.matmul(ot_ps[32 * h:32 * h + 32, q0:CH], v_sb[:, b, 32 * h:32 * h + 32],
                                                probs[s % SLOTS_P][:, h, q0:CH], start=(b == 0),
                                                stop=(b == n + TPC - 1))
                    last.then_inc(pv_done, 1)

                pending = None
                for c in range(NCH):
                    pe.wait_ge(rows_written, (g * NCH + (c + 1)) * HPG)
                    for i in range(HPG * chunk_steps(c)):
                        b, h = divmod(i, HPG)
                        u = STEP0[c] * HPG + i
                        j = b - TPC * c
                        q0 = max(0, j) * P
                        if u >= SLOTS_ST:
                            pe.wait_ge(probs_ready, g * UNITS + (u - SLOTS_ST + 1))
                        last = nc.tensor.matmul(st_ps[:, u % SLOTS_ST, q0:CH], k_sb[0:ROWS, h, b * P:(b + 1) * P],
                                                q_sb[c % SLOTS_Q][0:ROWS, h, q0:CH], start=True, stop=(j < 0))
                        if j >= 0:
                            last = nc.tensor.matmul(st_ps[:, u % SLOTS_ST, q0:q0 + P], ident[:], mask_k[:],
                                                    start=False, stop=True)
                        last.then_inc(scores_ready, 1)
                        if h == 2 and pending is not None:
                            pv(*pending)
                        if h == 3:
                            pending = (c, b)
                        for what in PLAN.get(u, ()):
                            if in_group(what, last_group):
                                max_event(g, *what)
                pv(*pending)

            with pe.Fori(0, G - 1) as g:
                group(g, False)
            group(G - 1, True)

        @block.scalar
        def _(act):
            def write_rows(g, c):
                slot = EVENT["turn", c] % 2
                act.wait_ge(turned, g * NCH + (c + 1))
                for h in range(HPG):
                    nc.scalar.activation(q_sb[c % SLOTS_Q][MAXROW:MAXROW + 3, h, :],
                                         mx_ps[slot][32 * h:32 * h + 3, 0, :], ACT.Copy).then_inc(rows_written, 1)

            for c in range(LEAD - 1):
                write_rows(0, c)

            def group(g, last_group):
                def copy_out(c):
                    act.wait_ge(pv_done, g * STEPS + (STEP0[c] + chunk_steps(c)))
                    act.wait_ge(o_stored[c % 2], (g * (NCH // 2) + c // 2) * 16 + ONE)
                    nc.scalar.activation(o_sb[c % 2][:], ot_ps[:], ACT.Copy).then_inc(o_copied, 1)

                for c in range(NCH):
                    for i in range(HPG * chunk_steps(c)):
                        b, h = divmod(i, HPG)
                        s = STEP0[c] + b
                        q0 = max(0, b - TPC * c) * P
                        act.wait_ge(scores_ready, g * UNITS + (s * HPG + h + 1) + ONE)
                        if h == 0 and s >= SLOTS_P:
                            act.wait_ge(pv_done, g * STEPS + (s - SLOTS_P + 1))
                        nc.scalar.activation(probs[s % SLOTS_P][:, h, q0:CH], st_ps[:, (s * HPG + h) % SLOTS_ST, q0:CH],
                                             ACT.Exp).then_inc(probs_ready, 1)
                        if c > 0 and i == 4:
                            copy_out(c - 1)
                        for what in PLAN.get(s * HPG + h, ()):
                            if what[0] == "turn" and in_group(what, last_group):
                                write_rows(g, what[1])
                copy_out(NCH - 1)

            with act.Fori(0, G - 1) as g:
                group(g, False)
            group(G - 1, True)

        @block.vector
        def _(dve):
            def reduce_units(g, c):
                for i, (kc, j, hp) in enumerate(max_units(c % NCH)):
                    width = (j + 1) * P if kc == c % NCH else CH
                    dve.wait_ge(max_ready, g * MAX_UNITS + (max_unit0(c) + i + 1))
                    nc.vector.tensor_reduce(part_max[:, HPG * j + 2 * hp:HPG * j + 2 * hp + 2, kc],
                                            mx_ps[EVENT["unit", c, i] % 2][:, :, 0:width], AX.X,
                                            ALU.max).then_inc(max_reduced, 1)

            def split_max(g, c):
                turn_no = g * NCH + c
                step = turn_no * MAX_STEPS
                dve.wait_ge(max_reduced, g * MAX_UNITS + max_unit0(c + 1))
                nc.vector.tensor_reduce(neg_max[:].rearrange("p j h -> p (j h)"), part_max[:, :, 0:c % NCH + 1], AX.X,
                                        ALU.max, negate=True).then_inc(max_step, 1)
                dve.wait_ge(turned, turn_no)
                dve.wait_ge(max_step, step + 1)
                nc.vector.tensor_copy(max_cols[:, :, :, 0], neg_max[:]).then_inc(max_step, 1)
                dve.wait_ge(max_step, step + 2)
                nc.vector.tensor_tensor(max_rest[:], neg_max[:], max_cols[:, :, :, 0], ALU.subtract).then_inc(
                    max_step, 1)
                dve.wait_ge(max_step, step + 3)
                nc.vector.tensor_copy(max_cols[:, :, :, 1], max_rest[:]).then_inc(max_step, 1)
                dve.wait_ge(max_step, step + 4)
                nc.vector.tensor_tensor(max_cols[:, :, :, 2], max_rest[:], max_cols[:, :, :, 1],
                                        ALU.subtract).then_inc(cols_ready, 1)

            dve.wait_ge(cols_zero, 1)
            for c in range(LEAD):
                reduce_units(0, c)
                split_max(0, c)
            with dve.Fori(0, G - 1) as g:
                for c in range(LEAD, NCH + LEAD):
                    reduce_units(g, c)
                    split_max(g, c)
            for c in range(LEAD, NCH):
                reduce_units(G - 1, c)
                split_max(G - 1, c)


class Steps:

    def __init__(self, eng, sem, base):
        self.eng, self.sem, self.base, self.count = eng, sem, base, 0

    def link(self, instruction):
        self.count += 1
        instruction.then_inc(self.sem, 1)
        self.eng.wait_ge(self.sem, self.base + self.count)


def combine_phase(nc, x, wo, wr, br, eye, tri, tile_starts, o_dram, x1, xs_dram, place, weight, tile_expert, tile_row):
    with ExitStack() as ctx:
        kit = Kit(nc, ctx)
        ident = kit.sb("c_ident", [P, P])
        wo_sb = kit.sb("c_wo", [P, KC, C])
        wr_sb = kit.sb("c_wr", [P, KC, E])
        br_sb = kit.sb("c_br", [P, E])
        tri_sb = kit.sb("c_tri", [P, P])
        ones = kit.sb("c_ones", [P, P])
        starts_sb = kit.sb("c_tile_starts", [P, TILES])
        experts = kit.sb("c_experts", [P, E])
        regions = kit.sb("c_regions", [P, E])
        o_in_sb = [kit.sb(f"c_o{s}", [P, G, CH]) for s in range(2)]
        xn2 = kit.sb("c_xn2", [P, NT, C])
        recip = kit.sb("c_recip", [P, TPC, NH])
        o_norm = kit.sb("c_o_norm", [P, TPC, C])
        o_nT = kit.sb("c_o_nT", [P, TPC, KC * P])
        y = kit.sb("c_y", [P, TPC, C])
        x2T = kit.sb("c_x2T", [P, TPC, KC * P])
        logits = kit.sb("c_logits", [P, TPC, E])
        top8 = kit.sb("c_top8", [P, NT, E])
        idx8 = kit.sb("c_idx8", [P, TPC, E], U32)
        idx_f = kit.sb("c_idx_f", [P, TPC, TOPK])
        chosen = kit.sb("c_chosen", [P, TOPK, TPC, E])
        both = kit.sb("c_both", [P, TPC + 1, E])
        pos = [kit.sb(f"c_pos{s}", [P, TPC + 1, E]) for s in range(2)]
        picked = kit.sb("c_picked", [P, TOPK, TPC, E])
        x_place_f = kit.sb("c_x_place_f", [P, TOPK, NT])
        x_place = kit.sb("c_x_place", [P, TOPK, NT], U32)
        stats = kit.sb("c_stats", [P, TPC, 6])
        mv = kit.sb("c_mv", [P, TPC, 2])
        rstd = kit.sb("c_rstd", [P, TPC])
        var_eps = [kit.sb(f"c_var_eps{s}", [P, TPC]) for s in range(2)]
        std = [kit.sb(f"c_std{s}", [P, TPC]) for s in range(2)]
        diff = kit.sb("c_diff", [P, NT])
        ex = kit.sb("c_ex", [P, NT])
        denom = kit.sb("c_denom", [P, NT])
        padded = kit.sb("c_padded", [P, E])
        count_i = kit.sb("c_count_i", [P, E], I32)
        ends = kit.sb("c_ends", [P, E])
        skip = kit.sb("c_skip", [P, E])
        below = kit.sb("c_below", [P, TILES, E - 1])
        skipped = kit.sb("c_skipped", [P, TILES, E - 1])
        tile_f = kit.sb("c_tile_f", [P, 2, TILES])
        behind = kit.sb("c_behind", [P, TOPK * NT, E - 1])
        place_f = kit.sb("c_place_f", [P, TOPK * NT])
        o_ps = [kit.ps(f"c_o_ps{s}", [P, NH, 32]) for s in range(2)]
        tr_ps = [kit.ps(f"c_tr_ps{s}", [P, 2, KC * P]) for s in range(2)]
        att_ps = kit.ps("c_att_ps", [P, TPC, C])
        log_ps = kit.ps("c_log_ps", [P, TPC, E])
        pos_ps = kit.ps("c_pos_ps", [P, TPC + 1, E])

        weights_in = kit.sem("c_weights_in")
        o_in = [kit.sem(f"c_o_in{s}") for s in range(2)]
        x_in = [kit.sem(f"c_x_in{n}") for n in range(NCH)]
        ones_ready = kit.sem("c_ones_ready")
        o_turned = kit.sem("c_o_turned")
        o_divided = kit.sem("c_o_divided")
        tr_turned = kit.sem("c_tr_turned")
        tr_copied = kit.sem("c_tr_copied")
        att_done = kit.sem("c_att_done")
        att_read = kit.sem("c_att_read")
        ln_var = kit.sem("c_ln_var")
        ln_std = kit.sem("c_ln_std")
        x2_ready = kit.sem("c_x2_ready")
        logits_done = kit.sem("c_logits_done")
        logits_read = kit.sem("c_logits_read")
        both_ready = kit.sem("c_both_ready")
        counted = kit.sem("c_counted")
        pos_ready = kit.sem("c_pos_ready")
        places_ready = kit.sem("c_places_ready")
        scattered = kit.sem("c_scattered")
        diff_ready = kit.sem("c_diff_ready")
        exp_ready = kit.sem("c_exp_ready")
        step = kit.sem("c_step")
        block = ctx.enter_context(nc.Block())
        LAST = NCH + 2

        TR_USES = [(kind, m, jj) for n in range(LAST) for kind, m in (("x2", n - 2), ("o", n)) if 0 <= m < NCH
                   for jj in range(2)]
        TR_USE = {use: number for number, use in enumerate(TR_USES)}

        @block.sync
        def _(sp):
            def load_o(n):
                sp.dma_start(o_in_sb[n % 2][:], o_dram[:, :, n * CH:(n + 1) * CH].rearrange("g r t -> r g t")
                             ).then_inc(o_in[n % 2], 16)

            def load_x(n):
                sp.dma_start(x1[:, n * TPC:(n + 1) * TPC, :], x[n * CH:(n + 1) * CH, :].rearrange(
                    "(j p) c -> p j c", p=P)).then_inc(x_in[n], 16)

            sp.dma_start(ident[:], eye).then_inc(weights_in, 16)
            load_o(0)
            sp.dma_start(wo_sb[:], wo.rearrange("(k p) n -> p k n", p=P)).then_inc(weights_in, 16)
            sp.dma_start(wr_sb[:], wr.rearrange("(k p) n -> p k n", p=P)).then_inc(weights_in, 16)
            load_o(1)
            sp.dma_start(br_sb[:], br.partition_broadcast(P)).then_inc(weights_in, 16)
            sp.dma_start(tri_sb[:], tri).then_inc(weights_in, 16)
            sp.dma_start(starts_sb[:], tile_starts.partition_broadcast(P)).then_inc(weights_in, 16)
            load_x(0)
            load_x(1)
            for n in range(2, NCH):
                sp.wait_ge(o_turned, (n - 1) * TPC)
                load_o(n)
                load_x(n)

        @block.gpsimd
        def _(pool):
            pool.memset(ones[:], 1.0)
            pool.memset(both[:, TPC, :], 0.0)
            pool.iota(experts[:], [[1, E]], base=0, channel_multiplier=0, allow_small_or_imprecise_dtypes=True)
            pool.iota(regions[:], [[T, E]], base=0, channel_multiplier=0,
                      allow_small_or_imprecise_dtypes=True).then_inc(ones_ready, 1)
            for n in range(NCH):
                pool.wait_ge(places_ready, n + 1)
                for t in range(n * TPC, (n + 1) * TPC):
                    for k in range(TOPK):
                        pool.indirect_dma_start(out=xs_dram, out_offset=bass.IndirectOffsetOnAxis(
                            ap=x_place[:, k, t:t + 1], axis=0), in_=xn2[:, t, :], in_offset=None).then_inc(scattered, 16)
            pool.wait_ge(scattered, TOPK * NT * 16)

        @block.tensor
        def _(pe):
            def turn_o(n, j):
                if j == 0:
                    pe.wait_ge(o_in[n % 2], 16 * (n // 2 + 1))
                if n * TPC + j >= 2:
                    pe.wait_ge(o_divided, n * TPC + j - 1)
                for g in range(G):
                    last = nc.tensor.transpose(o_ps[j % 2][:, 4 * g:4 * g + 4, :].rearrange("p h e -> p (h e)"),
                                               o_in_sb[n % 2][:, g, j * P:(j + 1) * P], ident[:])
                last.then_inc(o_turned, 1)

            def turn_pair(kind, m, jj):
                use = TR_USE[kind, m, jj]
                if use >= 2:
                    pe.wait_ge(tr_copied, use - 1)
                if kind == "x2":
                    pe.wait_ge(x2_ready, m + 1)
                else:
                    pe.wait_ge(o_divided, m * TPC + 2 * jj + 2)
                for j in (2 * jj, 2 * jj + 1):
                    src = xn2[:, m * TPC + j, :] if kind == "x2" else o_norm[:, j, :]
                    for k in range(KC):
                        last = nc.tensor.transpose(tr_ps[jj][:, j % 2, k * P:(k + 1) * P], src[:, k * P:(k + 1) * P],
                                                   ident[:])
                last.then_inc(tr_turned, 1)

            def multiply(kind, m, dst, srcT, w, done):
                for jj in range(2):
                    pe.wait_ge(tr_copied, TR_USE[kind, m, jj] + 1)
                    for j in (2 * jj, 2 * jj + 1):
                        for k in range(KC):
                            last = nc.tensor.matmul(dst[:, j, :], srcT[:, j, k * P:(k + 1) * P], w[:, k, :],
                                                    start=(k == 0), stop=(k == KC - 1))
                last.then_inc(done, 1)

            def count(m):
                pe.wait_ge(both_ready, m + 1)
                if m >= 1:
                    pe.wait_ge(pos_ready, m)
                flat = both[:].rearrange("p j e -> p (j e)")
                out = pos_ps[:].rearrange("p j e -> p (j e)")
                nc.tensor.matmul(out, tri_sb[:], flat, start=True, stop=False)
                for back in range(1, TPC + 1):
                    last = nc.tensor.matmul(out[:, back * E:], ones[:], flat[:, 0:(TPC + 1 - back) * E], start=False,
                                            stop=(back == TPC))
                last.then_inc(counted, 1)

            pe.wait_ge(weights_in, 6 * 16)
            pe.wait_ge(ones_ready, 1)
            turn_o(0, 0)
            turn_o(0, 1)
            for n in range(LAST):
                routed = n - 2 if n >= 2 else None
                if routed is not None:
                    turn_pair("x2", routed, 0)
                    turn_pair("x2", routed, 1)
                if n < NCH:
                    turn_o(n, 2)
                    turn_o(n, 3)
                if routed is not None:
                    if routed >= 1:
                        pe.wait_ge(logits_read, routed)
                    multiply("x2", routed, log_ps, x2T, wr_sb, logits_done)
                if n < NCH:
                    turn_pair("o", n, 0)
                    turn_pair("o", n, 1)
                if routed is not None:
                    count(routed)
                if n + 1 < NCH:
                    turn_o(n + 1, 0)
                    turn_o(n + 1, 1)
                if n < NCH:
                    if n >= 1:
                        pe.wait_ge(att_read, n)
                    multiply("o", n, att_ps, o_nT, wo_sb, att_done)

        @block.scalar
        def _(act):
            def copy_pair(kind, m, jj):
                if m >= 1 and jj == 0:
                    act.wait_ge(logits_done if kind == "x2" else att_done, m)
                act.wait_ge(tr_turned, TR_USE[kind, m, jj] + 1)
                dst = x2T if kind == "x2" else o_nT
                nc.scalar.activation(dst[:, 2 * jj:2 * jj + 2, :], tr_ps[jj][:], ACT.Copy).then_inc(tr_copied, 1)

            for n in range(LAST):
                if n >= 2:
                    copy_pair("x2", n - 2, 0)
                    copy_pair("x2", n - 2, 1)
                if n < NCH:
                    copy_pair("o", n, 0)
                    copy_pair("o", n, 1)
                if 1 <= n <= NCH:
                    for k in range(2):
                        act.wait_ge(ln_var, 2 * (n - 1) + k + 1)
                        nc.scalar.activation(std[k][:], var_eps[k][:], ACT.Sqrt).then_inc(ln_std, 1)
            act.wait_ge(diff_ready, 1)
            nc.scalar.activation(ex[:], diff[:], ACT.Exp).then_inc(exp_ready, 1)

        @block.vector
        def _(dve):
            st = Steps(dve, step, 0)

            def divide(n):
                if n >= 1:
                    dve.wait_ge(tr_turned, TR_USE["o", n - 1, 1] + 1)
                for j in range(TPC):
                    dve.wait_ge(o_turned, n * TPC + (j + 1))
                    st.link(nc.vector.reciprocal(recip[:, j, :], o_ps[j % 2][:, :, HD]))
                    nc.vector.tensor_tensor(o_norm[:, j, :].rearrange("p (h d) -> p h d", h=NH),
                                            o_ps[j % 2][:, :, 0:HD],
                                            recip[:, j, :].unsqueeze(2).broadcast_to([P, NH, HD]),
                                            ALU.mult).then_inc(o_divided, 1)

            def variance(src, k):
                for j in range(TPC):
                    last = nc.vector.bn_stats(stats[:, j, :], src[:, j, :])
                st.link(last)
                for j in range(TPC):
                    last = nc.vector.bn_aggr(mv[:, j, :], stats[:, j, :])
                st.link(last)
                nc.vector.tensor_scalar_add(var_eps[k][:], mv[:, :, 1], EPS).then_inc(ln_var, 1)

            def norm(dst, src, k, n):
                dve.wait_ge(ln_std, 2 * n + k + 1)
                st.link(nc.vector.reciprocal(rstd[:], std[k][:]))
                for j in range(TPC):
                    last = nc.vector.tensor_scalar(dst[:, j, :], src[:, j, :], mv[:, j, 0:1], rstd[:, j:j + 1],
                                                   ALU.subtract, ALU.mult)
                return last

            def choose(m):
                dve.wait_ge(logits_done, m + 1)
                nc.vector.tensor_tensor(logits[:], log_ps[:], br_sb[:].unsqueeze(1).broadcast_to([P, TPC, E]),
                                        ALU.add).then_inc(logits_read, 1)
                dve.wait_ge(logits_read, m + 1)
                for j in range(TPC):
                    last = nc.vector.max(top8[:, m * TPC + j, :], logits[:, j, :])
                st.link(last)
                for j in range(TPC):
                    last = nc.vector.max_index(idx8[:, j, :], top8[:, m * TPC + j, :], logits[:, j, :])
                st.link(last)
                st.link(nc.vector.tensor_copy(idx_f[:], idx8[:, :, 0:TOPK]))
                for k in range(TOPK):
                    last = nc.vector.tensor_tensor(chosen[:, k], idx_f[:, :, k:k + 1].broadcast_to([P, TPC, E]),
                                                   experts[:].unsqueeze(1).broadcast_to([P, TPC, E]), ALU.is_equal)
                st.link(last)
                if m >= 1:
                    dve.wait_ge(counted, m)
                nc.vector.tensor_tensor(both[:, 0:TPC, :], chosen[:, 0], chosen[:, 1], ALU.add).then_inc(both_ready, 1)

            def locate(m):
                dve.wait_ge(counted, m + 1)
                before = pos[(m - 1) % 2][:, TPC, :] if m >= 1 else regions[:]
                nc.vector.tensor_tensor(pos[m % 2][:], pos_ps[:], before.unsqueeze(1).broadcast_to([P, TPC + 1, E]),
                                        ALU.add).then_inc(pos_ready, 1)
                dve.wait_ge(pos_ready, m + 1)
                for k in range(TOPK):
                    last = nc.vector.tensor_tensor(picked[:, k], pos[m % 2][:, 0:TPC, :], chosen[:, k], ALU.mult)
                st.link(last)
                here = slice(m * TPC, (m + 1) * TPC)
                st.link(nc.vector.tensor_reduce(x_place_f[:, :, here], picked[:], AX.X, ALU.add))
                nc.vector.tensor_copy(x_place[:, :, here], x_place_f[:, :, here]).then_inc(places_ready, 1)

            dve.wait_ge(weights_in, 6 * 16)
            dve.wait_ge(ones_ready, 1)
            for n in range(LAST):
                normed = n - 1 if 1 <= n <= NCH else None
                if n < NCH:
                    divide(n)
                if normed is not None:
                    if normed >= 1:
                        dve.wait_ge(x2_ready, normed)
                    dve.wait_ge(att_done, normed + 1)
                    variance(att_ps, 0)
                if n >= 2:
                    choose(n - 2)
                if normed is not None:
                    x1_c = x1[:, normed * TPC:(normed + 1) * TPC, :]
                    norm(y, att_ps, 0, normed).then_inc(att_read, 1)
                    dve.wait_ge(att_read, normed + 1)
                    dve.wait_ge(x_in[normed], 16)
                    st.link(nc.vector.tensor_tensor(x1_c, y[:], x1_c, ALU.add))
                    variance(x1_c, 1)
                if n >= 2:
                    locate(n - 2)
                if normed is not None:
                    norm(xn2[:, normed * TPC:(normed + 1) * TPC, :], x1_c, 1, normed).then_inc(x2_ready, 1)

            st.link(nc.vector.tensor_tensor(padded[:], pos[(NCH - 1) % 2][:, TPC, :], regions[:], ALU.subtract))
            st.link(nc.vector.tensor_scalar_add(padded[:], padded[:], float(P - 1)))
            st.link(nc.vector.tensor_copy(count_i[:], padded[:]))
            shift = P.bit_length() - 1
            st.link(nc.vector.tensor_scalar(count_i[:], count_i[:], shift, shift, ALU.arith_shift_right,
                                            ALU.logical_shift_left))
            st.link(nc.vector.tensor_copy(padded[:], count_i[:]))
            st.link(nc.vector.tensor_tensor_scan(ends[:], ones[:, 0:E], padded[:], 0.0, ALU.mult, ALU.add))
            nc.vector.tensor_scalar(skip[:], padded[:], -1.0, float(T), ALU.mult, ALU.add)
            st.link(nc.vector.tensor_tensor(below[:], ends[:, 0:E - 1].unsqueeze(1).broadcast_to([P, TILES, E - 1]),
                                            starts_sb[:].unsqueeze(2).broadcast_to([P, TILES, E - 1]), ALU.is_le))
            nc.vector.tensor_reduce(tile_f[:, 0, :], below[:], AX.X, ALU.add)
            st.link(nc.vector.tensor_tensor(skipped[:], below[:],
                                            skip[:, 0:E - 1].unsqueeze(1).broadcast_to([P, TILES, E - 1]), ALU.mult))
            st.link(nc.vector.tensor_reduce(tile_f[:, 1, :], skipped[:], AX.X, ALU.add))
            nc.vector.tensor_copy(tile_expert[:], tile_f[:, 0, :])
            st.link(nc.vector.tensor_tensor(tile_f[:, 1, :], tile_f[:, 1, :], starts_sb[:], ALU.add))
            nc.vector.tensor_copy(tile_row[:], tile_f[:, 1, :])
            nc.vector.tensor_tensor(diff[:], top8[:, :, 1], top8[:, :, 0], ALU.subtract).then_inc(diff_ready, 1)
            wide = [P, TOPK * NT, E - 1]
            flat = x_place_f[:].rearrange("p k t -> p (k t)")
            st.link(nc.vector.tensor_tensor(behind[:], regions[:, 1:E].unsqueeze(1).broadcast_to(wide),
                                            flat.unsqueeze(2).broadcast_to(wide), ALU.is_le))
            st.link(nc.vector.tensor_tensor(behind[:], behind[:], skip[:, 0:E - 1].unsqueeze(1).broadcast_to(wide),
                                            ALU.mult))
            st.link(nc.vector.tensor_reduce(place_f[:], behind[:], AX.X, ALU.add))
            nc.vector.tensor_tensor(place[:].rearrange("p k t -> p (k t)"), flat, place_f[:], ALU.subtract)
            dve.wait_ge(exp_ready, 1)
            st.link(nc.vector.tensor_scalar_add(denom[:], ex[:], 1.0))
            st.link(nc.vector.reciprocal(weight[:, 0, :], denom[:]))
            nc.vector.tensor_tensor(weight[:, 1, :], ex[:], weight[:, 0, :], ALU.mult)


def experts_phase(nc, eye, w1_sb, w3_sb, w2_sb, weights_in, weights_count, tile_expert, tile_row, xs_dram, ys_dram):
    with ExitStack() as ctx:
        kit = Kit(nc, ctx)
        FC = FF // P
        ident = kit.sb("e_ident", [P, P])
        xs = [kit.sb(f"e_xs{s}", [P, C]) for s in range(2)]
        xsT = [kit.sb(f"e_xsT{s}", [P, C]) for s in range(2)]
        act_gate = kit.sb("e_act_gate", [P, FF])
        hidden = kit.sb("e_hidden", [P, FF])
        hT = kit.sb("e_hT", [P, FF])
        ys = [kit.sb(f"e_ys{s}", [P, C]) for s in range(2)]
        xT_ps = kit.ps("e_xT_ps", [P, C])
        gate_ps = [kit.ps(f"e_gate_ps{s}", [P, FF]) for s in range(2)]
        up_ps = [kit.ps(f"e_up_ps{s}", [P, FF]) for s in range(2)]
        hT_ps = kit.ps("e_hT_ps", [P, FF])
        y_ps = kit.ps("e_y_ps", [P, C])

        ident_in = kit.sem("e_ident_in")
        x_in = [kit.sem(f"e_x_in{s}") for s in range(2)]
        x_turned = kit.sem("e_x_turned")
        xT_copied = kit.sem("e_xT_copied")
        gate_done = kit.sem("e_gate_done")
        up_done = kit.sem("e_up_done")
        silu_done = kit.sem("e_silu_done")
        hidden_done = kit.sem("e_hidden_done")
        h_turned = kit.sem("e_h_turned")
        hT_copied = kit.sem("e_hT_copied")
        y_done = kit.sem("e_y_done")
        y_copied = kit.sem("e_y_copied")
        y_stored = [kit.sem(f"e_y_stored{s}") for s in range(2)]
        passed = kit.sem("e_passed")
        from_one = (*y_stored,)
        block = ctx.enter_context(nc.Block())

        @block.sync
        def _(sp):
            def rows(n):
                row = sp.value_load(tile_row[0:1, bass.ds(n, 1)], min_val=0, max_val=TABLE_ROWS - P)
                return bass.ds(row, P)

            def load(n, s):
                sp.dma_start(xs[s][:], xs_dram[rows(n), :]).then_inc(x_in[s], 16)

            def next_load(n, s):
                sp.wait_ge(x_turned, n - 1)
                pass_wait(sp, passed)
                load(n, s)

            def store(n, s):
                sp.wait_ge(y_copied, n + 1)
                pass_wait(sp, passed)
                sp.dma_start(ys_dram[bass.ds(n * P, P), :], ys[s][:]).then_inc(y_stored[s], 16)

            load(0, 0)
            load(1, 1)
            sp.dma_start(ident[:], eye).then_inc(ident_in, 16)
            next_load(2, 0)
            next_load(3, 1)
            with sp.Fori(2, TILES // 2) as it:
                for s in range(2):
                    n = it * 2 + s
                    next_load(n, s)
                    store(n - 4, s)
            for n in range(TILES - 4, TILES):
                store(n, n % 2)
            for s in range(2):
                sp.wait_ge(y_stored[s], 16 * TILES // 2 + ONE)

        @block.gpsimd
        def _(pool):
            start_at_one(pool, from_one)

        @block.tensor
        def _(pe):
            pe.wait_ge(ident_in, 16)
            pe.wait_ge(weights_in, weights_count)

            def turn_x(n, s):
                pe.wait_ge(x_in[s], (n + (2 - s)) * 8)
                pe.wait_ge(xT_copied, n)
                for k in range(KC):
                    last = nc.tensor.transpose(xT_ps[:, k * P:(k + 1) * P], xs[s][:, k * P:(k + 1) * P], ident[:])
                last.then_inc(x_turned, 1)

            def product(n, s, dst, w, expert, done):
                for k in range(KC):
                    last = nc.tensor.matmul(dst[s][:], xsT[s][:, k * P:(k + 1) * P], w[:, k, bass.ds(expert * FF, FF)],
                                            start=(k == 0), stop=(k == KC - 1))
                last.then_inc(done, 1)

            def hidden_layer(n, s, after, between=None):
                e = pe.value_load(tile_expert[0:1, bass.ds(n, 1)], min_val=0, max_val=E - 1)
                pe.wait_ge(xT_copied, n + 1)
                if after:
                    pe.wait_ge(silu_done, n - 1)
                product(n, s, gate_ps, w1_sb, e, gate_done)
                if between is not None:
                    turn_hidden(between)
                if after:
                    pe.wait_ge(hidden_done, n - 1)
                product(n, s, up_ps, w3_sb, e, up_done)

            def turn_hidden(n):
                pe.wait_ge(hidden_done, n + 1)
                pe.wait_ge(hT_copied, n)
                for k in range(FC):
                    last = nc.tensor.transpose(hT_ps[:, k * P:(k + 1) * P], hidden[:, k * P:(k + 1) * P], ident[:])
                last.then_inc(h_turned, 1)

            def down(n):
                e = pe.value_load(tile_expert[0:1, bass.ds(n, 1)], min_val=0, max_val=E - 1)
                pe.wait_ge(hT_copied, n + 1)
                pe.wait_ge(y_copied, n)
                for k in range(FC):
                    last = nc.tensor.matmul(y_ps[:], hT[:, k * P:(k + 1) * P], w2_sb[:, k, bass.ds(e * C, C)],
                                            start=(k == 0), stop=(k == FC - 1))
                last.then_inc(y_done, 1)

            turn_x(0, 0)
            hidden_layer(0, 0, False)
            turn_x(1, 1)
            hidden_layer(1, 1, False, 0)
            turn_x(2, 0)
            down(0)
            with pe.Fori(0, TILES // 2 - 2) as it:
                for s in range(2):
                    n = it * 2 + (2 + s)
                    hidden_layer(n, s, True, n - 1)
                    turn_x(n + 1, 1 - s)
                    down(n - 1)
            hidden_layer(TILES - 2, 0, True, TILES - 3)
            turn_x(TILES - 1, 1)
            down(TILES - 3)
            hidden_layer(TILES - 1, 1, True, TILES - 2)
            down(TILES - 2)
            turn_hidden(TILES - 1)
            down(TILES - 1)

        @block.scalar
        def _(act):
            def silu(n, s):
                act.wait_ge(gate_done, n + 1)
                act.wait_ge(hidden_done, n)
                nc.scalar.activation(act_gate[:], gate_ps[s][:], ACT.Silu).then_inc(silu_done, 1)

            def copy_hT(n):
                act.wait_ge(h_turned, n + 1)
                act.wait_ge(y_done, n)
                nc.scalar.activation(hT[:], hT_ps[:], ACT.Copy).then_inc(hT_copied, 1)

            silu(0, 0)
            silu(1, 1)
            copy_hT(0)
            with act.Fori(0, TILES // 2 - 1) as it:
                for s in range(2):
                    n = it * 2 + (2 + s)
                    silu(n, s)
                    copy_hT(n - 1)
            copy_hT(TILES - 1)

        @block.vector
        def _(dve):
            def copy_xT(n, s, after):
                dve.wait_ge(x_turned, n + 1)
                if after:
                    dve.wait_ge(up_done, n - 1)
                nc.vector.tensor_copy(xsT[s][:], xT_ps[:]).then_inc(xT_copied, 1)

            def hide(n, s):
                dve.wait_ge(silu_done, n + 1)
                dve.wait_ge(up_done, n + 1)
                dve.wait_ge(h_turned, n)
                nc.vector.tensor_tensor(hidden[:], up_ps[s][:], act_gate[:], ALU.mult).then_inc(hidden_done, 1)

            def copy_y(n, s):
                dve.wait_ge(y_done, n + 1)
                dve.wait_ge(y_stored[s], (n - s) * 8 + ONE)
                nc.vector.tensor_copy(ys[s][:], y_ps[:]).then_inc(y_copied, 1)

            copy_xT(0, 0, False)
            copy_xT(1, 1, False)
            hide(0, 0)
            hide(1, 1)
            copy_xT(2, 0, True)
            copy_y(0, 0)
            with dve.Fori(0, TILES // 2 - 2) as it:
                for s in range(2):
                    n = it * 2 + (2 + s)
                    hide(n, s)
                    copy_xT(n + 1, 1 - s, True)
                    copy_y(n - 1, 1 - s)
            hide(TILES - 2, 0)
            copy_xT(TILES - 1, 1, True)
            copy_y(TILES - 3, 1)
            hide(TILES - 1, 1)
            copy_y(TILES - 2, 0)
            copy_y(TILES - 1, 1)


def gather_phase(nc, x1, place, weight, ys_dram, out):
    with ExitStack() as ctx:
        kit = Kit(nc, ctx)
        SLOTS = 4
        rows_sb = [[kit.sb(f"g_rows{s}_{k}", [P, TPC, C]) for k in range(TOPK)] for s in range(SLOTS)]
        out_sb = [kit.sb(f"g_out{s}", [P, TPC, C]) for s in range(2)]
        mixed = kit.sb("g_mixed", [P, TPC, C])
        normed = kit.sb("g_normed", [P, TPC, C])
        stats = kit.sb("g_stats", [P, TPC, 6])
        mv = kit.sb("g_mv", [P, TPC, 2])
        var_eps = kit.sb("g_var_eps", [P, TPC])
        std = kit.sb("g_std", [P, TPC])
        rstd = kit.sb("g_rstd", [P, TPC])
        rows_in = [kit.sem(f"g_rows_in{s}") for s in range(SLOTS)]
        mixed_done = kit.sem("g_mixed_done")
        step = kit.sem("g_step")
        var_ready = kit.sem("g_var_ready")
        std_ready = kit.sem("g_std_ready")
        out_ready = kit.sem("g_out_ready")
        stored = [kit.sem(f"g_stored{s}") for s in range(2)]
        block = ctx.enter_context(nc.Block())
        ROWS_IN = TPC * TOPK * 16
        STEPS_HERE = 5

        @block.gpsimd
        def _(pool):
            for n in range(NCH):
                if n >= SLOTS:
                    pool.wait_ge(mixed_done, n - SLOTS + 1)
                for j in range(TPC):
                    for k in range(TOPK):
                        t = n * TPC + j
                        pool.indirect_dma_start(out=rows_sb[n % SLOTS][k][:, j, :], out_offset=None, in_=ys_dram,
                                                in_offset=bass.IndirectOffsetOnAxis(ap=place[:, k, t:t + 1], axis=0)
                                                ).then_inc(rows_in[n % SLOTS], 16)

        @block.vector
        def _(dve):
            for n in range(NCH):
                st = Steps(dve, step, n * STEPS_HERE)
                s = n % SLOTS
                dve.wait_ge(rows_in[s], (n // SLOTS + 1) * ROWS_IN)
                for j in range(TPC):
                    t = n * TPC + j
                    last = nc.vector.tensor_scalar(mixed[:, j, :], rows_sb[s][0][:, j, :], weight[:, 0, t:t + 1], None,
                                                   ALU.mult)
                st.link(last)
                for j in range(TPC):
                    t = n * TPC + j
                    last = nc.vector.scalar_tensor_tensor(out=mixed[:, j, :], in0=rows_sb[s][1][:, j, :],
                                                          scalar=weight[:, 1, t:t + 1], in1=mixed[:, j, :],
                                                          op0=ALU.mult, op1=ALU.add)
                last.then_inc(mixed_done, 1)
                dve.wait_ge(mixed_done, n + 1)
                for j in range(TPC):
                    last = nc.vector.bn_stats(stats[:, j, :], mixed[:, j, :])
                st.link(last)
                for j in range(TPC):
                    last = nc.vector.bn_aggr(mv[:, j, :], stats[:, j, :])
                st.link(last)
                nc.vector.tensor_scalar_add(var_eps[:], mv[:, :, 1], EPS).then_inc(var_ready, 1)
                dve.wait_ge(std_ready, n + 1)
                st.link(nc.vector.reciprocal(rstd[:], std[:]))
                for j in range(TPC):
                    last = nc.vector.tensor_scalar(normed[:, j, :], mixed[:, j, :], mv[:, j, 0:1], rstd[:, j:j + 1],
                                                   ALU.subtract, ALU.mult)
                st.link(last)
                if n >= 2:
                    dve.wait_ge(stored[n % 2], 16 * (n // 2))
                nc.vector.tensor_tensor(out_sb[n % 2][:], normed[:], x1[:, n * TPC:(n + 1) * TPC, :], ALU.add).then_inc(out_ready, 1)

        @block.scalar
        def _(act):
            for n in range(NCH):
                act.wait_ge(var_ready, n + 1)
                nc.scalar.activation(std[:], var_eps[:], ACT.Sqrt).then_inc(std_ready, 1)

        @block.sync
        def _(sp):
            for n in range(NCH):
                sp.wait_ge(out_ready, n + 1)
                sp.dma_start(out[n * CH:(n + 1) * CH, :].rearrange("(j p) c -> p j c", p=P),
                             out_sb[n % 2][:]).then_inc(stored[n % 2], 16)
            for s in range(2):
                sp.wait_ge(stored[s], 16 * NCH // 2)


def block_program(nc, x, wq, wk, wv, wo, wr, br, w1, w3, w2, eye, tri, tile_starts, q_rows, k_rows, masks, out):
    x = x.rearrange("b t c -> (b t) c")
    out = out.rearrange("b t c -> (b t) c")
    q_parts = nc.dram_tensor("q_parts", [G, PART_ROWS, HPG, T], BF16).ap()
    k_parts = nc.dram_tensor("k_parts", [G, PART_ROWS, HPG, T], BF16).ap()
    v_aug = nc.dram_tensor("v_aug", [T, NH * 32], F32).ap()
    o_dram = nc.dram_tensor("o_heads", [G, P, T], F32).ap()
    xs_dram = nc.dram_tensor("table_x", [TABLE_ROWS, C], F32).ap()
    ys_dram = nc.dram_tensor("table_y", [TILES * P, C], F32).ap()

    project_phase(nc, x, wq, wk, wv, eye, q_parts, k_parts, v_aug)
    with ExitStack() as ctx:
        kit = Kit(nc, ctx)
        w1_sb = kit.sb("w1", [P, KC, E * FF])
        w3_sb = kit.sb("w3", [P, KC, E * FF])
        w2_sb = kit.sb("w2", [P, FF // P, E * C])
        weights_in = kit.sem("expert_weights_in")
        loads = [(w1_sb[:, :, e * FF:(e + 1) * FF], w1[e].rearrange("(k p) f -> p k f", p=P)) for e in range(E)]
        loads += [(w3_sb[:, :, e * FF:(e + 1) * FF], w3[e].rearrange("(k p) f -> p k f", p=P)) for e in range(E)]
        loads += [(w2_sb[:, :, e * C:(e + 1) * C], w2[e].rearrange("(k p) c -> p k c", p=P)) for e in range(E)]
        attention_phase(nc, q_parts, k_parts, v_aug, q_rows, k_rows, masks, o_dram, xs_dram, loads, weights_in)
        x1 = kit.sb("x1", [P, NT, C])
        place = kit.sb("place", [P, TOPK, NT], U32)
        weight = kit.sb("weight", [P, TOPK, NT])
        tile_expert = kit.sb("tile_expert", [P, TILES], I32)
        tile_row = kit.sb("tile_row", [P, TILES], I32)
        combine_phase(nc, x, wo, wr, br, eye, tri, tile_starts, o_dram, x1, xs_dram, place, weight, tile_expert, tile_row)
        experts_phase(nc, eye, w1_sb, w3_sb, w2_sb, weights_in, 16 * len(loads), tile_expert, tile_row, xs_dram, ys_dram)
        gather_phase(nc, x1, place, weight, ys_dram, out)


INPUTS = ("L0_attn_x", "L0_attn_Wq", "L0_attn_Wk", "L0_attn_Wv", "L0_attn_Wo", "L0_ffn_Wr", "L0_ffn_br",
          "L0_ffn_W1", "L0_ffn_W3", "L0_ffn_W2")
CONSTANTS = ("eye", "tri", "tile_starts", "q_rows", "k_rows", "masks")


def kernel(**inputs):
    import numpy as np
    import concourse.bacc as bacc
    from concourse.bass_utils import run_bass_kernel_spmd

    nc = bacc.Bacc("TRN2", target_bir_lowering=False, num_devices=1)
    constants = host_constants()
    arrays, args = {}, []
    for name in INPUTS + CONSTANTS:
        a = np.ascontiguousarray(inputs[name] if name in inputs else constants[name])
        arrays[name] = a
        args.append(nc.dram_tensor(name, a.shape, mybir.dt.from_np(a.dtype), kind="ExternalInput").ap())
    out = nc.dram_tensor("out", (1, T, C), F32, kind="ExternalOutput").ap()
    block_program(nc, *args, out)
    result = run_bass_kernel_spmd(nc, [arrays], core_ids=[0])
    return result.results[0]["out"]
```

```python
from contextlib import ExitStack

import concourse.bass as bass
from concourse import mybir

ALU = mybir.AluOpType
ACT = mybir.ActivationFunctionType
AX = mybir.AxisListType
F32 = mybir.dt.float32
BF16 = mybir.dt.bfloat16
I32 = mybir.dt.int32
U32 = mybir.dt.uint32

P = 128
T, C = 4096, 256
NH, HD = 16, 16
E, FF, TOPK = 8, 512, 2
KC = C // P
CH = 512
NCH = T // CH
TPC = CH // P
NT = T // P
G, HPG = 4, 4
EPS = 1e-5
ONE = 1
SCALE = HD ** -0.5

Q_PARTS = (1, 1, 2, 0, 0, 0)
K_PARTS = (0, 1, 0, 0, 1, 2)
PROD = len(Q_PARTS) * HD
MAXROW = PROD
ROWS = PROD + 6
PART_ROWS = 3 * HD

TILES = (TOPK * T + E * (P - 1)) // P
TABLE_ROWS = (E - 1) * T + (TILES + 1) * P
ROW = C + 2
FAR = 2 ** 16


def slopes():
    import numpy as np

    start = 2.0 ** (-(2.0 ** -(NH.bit_length() - 1 - 3)))
    return np.array([start * start ** i for i in range(NH)], np.float32)


def host_constants():
    import numpy as np

    bf16 = np.dtype(mybir.dt.np(BF16))
    f32 = np.float32
    bias = slopes()[:, None] * (np.arange(T, dtype=f32) - f32(511))
    high = bias.astype(bf16)
    mid = (bias - high.astype(f32)).astype(bf16)
    low = (bias - high.astype(f32) - mid.astype(f32)).astype(bf16)
    k_rows = np.ones((G, 6, HPG, T), bf16)
    for n, part in enumerate((high, mid, low)):
        k_rows[:, 3 + n] = part.reshape(G, HPG, T)
    q_rows = np.zeros((6, HPG, CH), bf16)
    q_rows[3:] = 1
    future = np.triu(np.ones((P, P), f32), 1) * f32(-1e30)
    masks = np.stack([np.eye(P, dtype=f32), future, future.T]).astype(bf16)
    tri = np.triu(np.ones((P, P), f32), 1)
    tile_starts = (np.arange(TILES) * P).astype(f32)
    return {"eye": np.eye(P, dtype=f32), "tri": tri, "tile_starts": tile_starts, "q_rows": q_rows, "k_rows": k_rows, "masks": masks}


class Kit:

    def __init__(self, nc, ctx):
        self.nc, self.ctx = nc, ctx

    def sb(self, name, shape, dt=F32):
        return self.ctx.enter_context(self.nc.sbuf_tensor(name, shape, dt))

    def ps(self, name, shape, dt=F32):
        return self.ctx.enter_context(self.nc.psum_tensor(name, shape, dt))

    def sem(self, name):
        return self.ctx.enter_context(self.nc.semaphore(name))


def start_at_one(eng, semaphores):
    for semaphore in semaphores:
        eng.sem_inc(semaphore, ONE)


def pass_wait(eng, passed):
    eng.sem_inc(passed, 1)


def project_phase(nc, x, wq, wk, wv, eye, q_parts, k_parts, v_aug, operands):
    with ExitStack() as ctx:
        kit = Kit(nc, ctx)
        ident = kit.sb("p_ident", [P, P])
        w_sb = [kit.sb(f"p_w{n}", [P, KC, C]) for n in "qkv"]
        x_sb = [kit.sb(f"p_x{s}", [P, TPC, C]) for s in range(2)]
        xn = kit.sb("p_xn", [P, TPC, C])
        stats = kit.sb("p_stats", [P, TPC, 6])
        mv = kit.sb("p_mv", [P, TPC, 2])
        var_eps = kit.sb("p_var_eps", [P, TPC])
        std = kit.sb("p_std", [P, TPC])
        rstd = kit.sb("p_rstd", [P, TPC])
        xnT = [kit.sb(f"p_xnT{s}", [P, KC, CH]) for s in range(2)]
        w_raw = [xnT[1][:, :, n * C:(n + 1) * C] for n in range(2)]
        rest = kit.sb("p_rest", [P, CH])
        parts = [kit.sb(f"p_parts{s}", [P, 4, 3, CH], BF16) for s in range(2)]
        v_st = [kit.sb(f"p_v{s}", [P, TPC, NH, 32]) for s in range(2)]
        xT_ps = kit.ps("p_xT_ps", [P, KC, CH])
        qk_ps = kit.ps("p_qk_ps", [P, 4, CH])
        v_ps = kit.ps("p_v_ps", [P, 2, 2, C])

        ident_in = kit.sem("p_ident_in")
        weights_in = kit.sem("p_weights_in")
        weights_ordered = kit.sem("p_weights_ordered")
        x_in = [kit.sem(f"p_x_in{s}") for s in range(2)]
        v_ones = kit.sem("p_v_ones")
        ln = kit.sem("p_ln")
        split_step = kit.sem("p_split_step")
        var_ready = kit.sem("p_var_ready")
        std_ready = kit.sem("p_std_ready")
        xn_ready = kit.sem("p_xn_ready")
        transposed = kit.sem("p_transposed")
        xT_ready = kit.sem("p_xT_ready")
        qk_done = kit.sem("p_qk_done")
        v_done = kit.sem("p_v_done")
        high_ready = kit.sem("p_high_ready")
        split_done = kit.sem("p_split_done")
        v_ready = kit.sem("p_v_ready")
        qk_stored = [kit.sem(f"p_qk_stored{s}") for s in range(2)]
        v_stored = [kit.sem(f"p_v_stored{s}") for s in range(2)]
        passed = kit.sem("p_passed")
        from_one = (transposed, v_done, *qk_stored, *v_stored, xT_ready, split_done, v_ready)
        block = ctx.enter_context(nc.Block())
        STORES = 4 * 2
        LN_STEPS, SPLIT_STEPS = 3, 2 * 4

        def pipelined(eng, ahead, main):
            ahead(0, 0)
            with eng.Fori(0, NCH // 2 - 1) as it:
                for s in range(2):
                    main(it * 2 + s, s, True)
            main(NCH - 2, 0, True)
            main(NCH - 1, 1, False)

        @block.gpsimd
        def _(pool):
            start_at_one(pool, from_one)
            pool.dma_start(ident[:], eye).then_inc(ident_in, 16)
            for w, src in zip((*w_raw, w_sb[2][:]), (wq, wk, wv)):
                pool.dma_start(w, src.rearrange("(k p) n -> p k n", p=P)).then_inc(weights_in, 16)
            pool.wait_ge(weights_in, 48)
            for w, raw in zip(w_sb, w_raw):
                for k in range(KC):
                    last = pool.tensor_copy(w[:, k, :].rearrange("p (g d h) -> p g h d", g=G, d=HD),
                                            raw[:, k, :].rearrange("p (g h d) -> p g h d", g=G, d=HD))
            last.then_inc(weights_ordered, 1)
            for s in range(2):
                pool.memset(v_st[s][:, :, :, HD:HD + 1], 1.0)
                last = pool.memset(v_st[s][:, :, :, HD + 1:32], 0.0)
            last.then_inc(v_ones, 1)
            operands.load_masks(pool)

        @block.sync
        def _(sp):
            def load_x(n, s):
                sp.dma_start(x_sb[s][:], x[bass.ds(n * CH, CH), :].rearrange("(j p) c -> p j c", p=P)).then_inc(
                    x_in[s], 16)

            def stores(n, s, n_more):
                if n_more:
                    sp.wait_ge(xn_ready, n + 1)
                    pass_wait(sp, passed)
                    load_x(n + 2, s)
                for t in range(4):
                    sp.wait_ge(split_done, n * 4 + (t + 1) + ONE)
                    pass_wait(sp, passed)
                    store = (q_parts, k_parts)[t // 2]
                    for gg in range(2):
                        dst = store[2 * (t % 2) + gg, 0:PART_ROWS, :, bass.ds(n * CH, CH)].rearrange(
                            "(part d) h t -> (d h) part t", d=HD)
                        sp.dma_start(dst, parts[s][64 * gg:64 * gg + 64, t, :, :]).then_inc(qk_stored[s], 16)
                for u in range(2):
                    sp.wait_ge(v_ready, n * 2 + (u + 1) + ONE)
                    pass_wait(sp, passed)
                    sp.dma_start(v_aug[bass.ds(n * CH + u * (CH // 2), CH // 2), :].rearrange("(j p) f -> p j f", p=P),
                                 v_st[s][:, 2 * u:2 * u + 2].rearrange("p j h e -> p j (h e)")).then_inc(
                                     v_stored[s], 16)

            load_x(0, 0)
            load_x(1, 1)
            with sp.Fori(0, NCH // 2 - 1) as it:
                for s in range(2):
                    stores(it * 2 + s, s, True)
            assert EARLY == 2
            for c in range(EARLY):
                sp.wait_ge(qk_stored[c], 16 * STORES + ONE)
                operands.load_q(sp, 0, c)
                operands.load_k(sp, 0, c)
                stores(NCH - 2 + c, c, False)
            for s in range(2):
                sp.wait_ge(qk_stored[s], 16 * STORES * NCH // 2 + ONE)
                sp.wait_ge(v_stored[s], 2 * 16 * NCH // 2 + ONE)

        @block.vector
        def _(dve):
            def norm(n, s):
                base = n * LN_STEPS
                dve.wait_ge(x_in[s], (n + (2 - s)) * 8)
                for j in range(TPC):
                    last = nc.vector.bn_stats(stats[:, j, :], x_sb[s][:, j, :])
                last.then_inc(ln, 1)
                dve.wait_ge(ln, base + 1)
                pass_wait(dve, passed)
                for j in range(TPC):
                    last = nc.vector.bn_aggr(mv[:, j, :], stats[:, j, :])
                last.then_inc(ln, 1)
                dve.wait_ge(ln, base + 2)
                nc.vector.tensor_scalar_add(var_eps[:], mv[:, :, 1], EPS).then_inc(var_ready, 1)
                dve.wait_ge(std_ready, n + 1)
                nc.vector.reciprocal(rstd[:], std[:]).then_inc(ln, 1)
                dve.wait_ge(ln, base + 3)
                dve.wait_ge(transposed, n + ONE)
                for j in range(TPC):
                    last = nc.vector.tensor_scalar(xn[:, j, :], x_sb[s][:, j, :], mv[:, j, 0:1],
                                                   rstd[:, j:j + 1], ALU.subtract, ALU.mult)
                last.then_inc(xn_ready, 1)

            def split(n, s, more):
                if more:
                    norm(n + 1, 1 - s)
                for t in range(4):
                    base = n * SPLIT_STEPS + 2 * t
                    dve.wait_ge(high_ready, n * 4 + (t + 1))
                    nc.vector.scalar_tensor_tensor(
                        out=rest[:], in0=qk_ps[:, t, :], scalar=SCALE if t < 2 else 1.0,
                        in1=parts[s][:, t, 0, :], op0=ALU.mult, op1=ALU.subtract).then_inc(split_step, 1)
                    dve.wait_ge(split_step, base + 1)
                    nc.vector.tensor_copy(parts[s][:, t, 1, :], rest[:]).then_inc(split_step, 1)
                    dve.wait_ge(split_step, base + 2)
                    nc.vector.tensor_tensor(parts[s][:, t, 2, :], rest[:], parts[s][:, t, 1, :],
                                            ALU.subtract).then_inc(split_done, 1)
                    dve.wait_ge(split_done, n * 4 + (t + 1) + ONE)

            pipelined(dve, norm, split)

        @block.scalar
        def _(act):
            def take_std(n):
                act.wait_ge(var_ready, n + 1)
                nc.scalar.activation(std[:], var_eps[:], ACT.Sqrt).then_inc(std_ready, 1)

            def copy_xT(n, s, after):
                act.wait_ge(transposed, n + 1 + ONE)
                if after:
                    act.wait_ge(v_done, (n - 1) * 2 + ONE)
                for k in range(KC):
                    last = nc.scalar.activation(xnT[s][:, k, :], xT_ps[:, k, :], ACT.Copy)
                last.then_inc(xT_ready, 1)

            def begin(n, s):
                take_std(n)
                copy_xT(n, s, False)
                act.wait_ge(v_ones, 1)
                act.wait_ge(weights_ordered, 1)

            def take_out(n, s, more):
                if more:
                    take_std(n + 1)
                act.wait_ge(qk_stored[s], (n - s) * (8 * STORES) + ONE)
                for t in range(4):
                    act.wait_ge(qk_done, n * 4 + (t + 1))
                    nc.scalar.activation(parts[s][:, t, 0, :], qk_ps[:, t, :], ACT.Copy,
                                         scale=SCALE if t < 2 else 1.0).then_inc(high_ready, 1)
                if more:
                    copy_xT(n + 1, 1 - s, True)
                act.wait_ge(v_stored[s], (n - s) * (2 * 8) + ONE)
                for u in range(2):
                    act.wait_ge(v_done, n * 2 + (u + 1) + ONE)
                    nc.scalar.activation(v_st[s][:, 2 * u:2 * u + 2, :, 0:HD],
                                         v_ps[:, u, :, :].rearrange("p j (h d) -> p j h d", h=NH),
                                         ACT.Copy).then_inc(v_ready, 1)

            pipelined(act, begin, take_out)

        @block.tensor
        def _(pe):
            def turn(n, s):
                pe.wait_ge(xn_ready, n + 1)
                pe.wait_ge(xT_ready, n + ONE)
                for k in range(KC):
                    for j in range(TPC):
                        last = nc.tensor.transpose(xT_ps[:, k, j * P:(j + 1) * P],
                                                   xn[:, j, k * P:(k + 1) * P], ident[:])
                last.then_inc(transposed, 1)

            def begin(n, s):
                pe.wait_ge(ident_in, 16)
                turn(n, s)
                pe.wait_ge(weights_in, 48)
                pe.wait_ge(weights_ordered, 1)

            def products(n, s, more):
                pe.wait_ge(xT_ready, n + 1 + ONE)
                pe.wait_ge(split_done, n * 4 + ONE)
                for t in range(4):
                    w, m = w_sb[t // 2], t % 2
                    for k in range(KC):
                        last = nc.tensor.matmul(qk_ps[:, t, :], w[:, k, m * P:(m + 1) * P], xnT[s][:, k, :],
                                                start=(k == 0), stop=(k == KC - 1))
                    last.then_inc(qk_done, 1)
                if more:
                    turn(n + 1, 1 - s)
                pe.wait_ge(v_ready, n * 2 + ONE)
                for j in range(TPC):
                    for k in range(KC):
                        last = nc.tensor.matmul(v_ps[:, j // 2, j % 2, :], xnT[s][:, k, j * P:(j + 1) * P],
                                                w_sb[2][:, k, :], start=(k == 0), stop=(k == KC - 1))
                    if j % 2:
                        last.then_inc(v_done, 1)

            pipelined(pe, begin, products)


def chunk_steps(c):
    return TPC * (c + 1)


STEPS = sum(chunk_steps(c) for c in range(NCH))
UNITS = STEPS * HPG
STEP0 = [sum(chunk_steps(d) for d in range(c)) for c in range(NCH + 1)]
LEAD = 3
FIRST_LEAD = 2
EARLY = 2
TURN_GAP = 7
Q_RELOAD = 16
RELOAD = 10
TAIL = 8


def max_units(c):
    return [(kc, j, hp) for kc in range(c + 1) for j in range(TPC) for hp in range(2)]


def max_unit0(c):
    return c // NCH * MAX_UNITS + sum(len(max_units(d)) for d in range(c % NCH))


MAX_UNITS = sum(len(max_units(c)) for c in range(NCH))


def turn_behind(c):
    return 0 if c % NCH == NCH - 1 else 4


def max_events(c):
    events = [("unit", c, i) for i in range(len(max_units(c % NCH)))]
    if c > 0:
        events.insert(turn_behind(c - 1), ("turn", c - 1))
    return events


def group_plan(first=False, last=False):
    lead = FIRST_LEAD if first else LEAD
    deadlines = [(STEP0[c] * HPG - TAIL, max_unit0(c + 1)) for c in range(lead, NCH)]
    at, done = 0 if first else Q_RELOAD, max_unit0(lead)
    after = {}
    place = {}
    while deadlines:
        knot = max(deadlines, key=lambda d: (d[1] - done) / (d[0] - at))
        for m in range(done, knot[1]):
            place[m] = at + (m - done) * (knot[0] - at) // (knot[1] - done)
        deadlines = [d for d in deadlines if d[0] > knot[0]]
        at, done = knot
    at = (STEP0[NCH - 1] + TPC) * HPG + RELOAD
    for m in range(done, max_unit0(NCH + LEAD)):
        place[m] = at + (m - done) * (UNITS - TAIL - at) // (max_unit0(NCH + LEAD) - done)
    u = 0
    for c in range(lead, NCH + LEAD):
        for what in max_events(c):
            if last and what[1] >= NCH:
                continue
            if what[0] == "unit":
                u = max(u, place[max_unit0(c) + what[2]])
            elif turn_behind(what[1]) == 0:
                u += TURN_GAP
            if c >= NCH and what[0] == "unit":
                u = max(u, (STEP0[NCH - 1] + TPC * (c - NCH + 1)) * HPG + RELOAD)
            u = min(u, UNITS - 1)
            after.setdefault(u, []).append(what)
    return after


class Operands:

    def __init__(self, kit, q_parts, k_parts, q_rows, k_rows, masks):
        self.q_parts, self.k_parts, self.q_rows, self.k_rows = q_parts, k_parts, q_rows, k_rows
        self.k_sb = kit.sb("a_k", [P, HPG, T], BF16)
        self.q_sb = [kit.sb(f"a_q{s}", [P, HPG, CH], BF16) for s in range(EARLY)]
        self.q_in = [kit.sem(f"a_q_in{s}") for s in range(EARLY)]
        self.k_in = [kit.sem(f"a_k_in{n}") for n in range(NCH)]
        self.masks = masks
        self.masks_sb = [kit.sb(f"a_mask{n}", [P, P], BF16) for n in range(3)]
        self.masks_in = kit.sem("a_masks_in")

    def load_masks(self, eng):
        for n, dst in enumerate(self.masks_sb):
            eng.dma_start(dst[:], self.masks[n]).then_inc(self.masks_in, 16)

    def load_q(self, eng, g, c):
        dst, done = self.q_sb[c % len(self.q_sb)], self.q_in[c % len(self.q_sb)]
        tok = slice(c * CH, (c + 1) * CH)
        for part in range(3):
            first, times = Q_PARTS.index(part), Q_PARTS.count(part)
            src = self.q_parts[g, part * HD:(part + 1) * HD, :, tok]
            eng.dma_start(dst[first * HD:(first + times) * HD, :, :],
                          src.unsqueeze(0).broadcast_to([times, HD, HPG, CH])).then_inc(done, 16)
        eng.dma_start(dst[PROD:ROWS, :, :], self.q_rows).then_inc(done, 16)

    def load_k(self, eng, g, n):
        tok = slice(n * CH, (n + 1) * CH)
        for r0, r1 in ((0, 2 * HD), (2 * HD, PART_ROWS), (PART_ROWS, PROD)):
            eng.dma_start(self.k_sb[r0:r1, :, tok], self.k_parts[g, 0:r1 - r0, :, tok]).then_inc(self.k_in[n], 16)
        eng.dma_start(self.k_sb[PROD:ROWS, :, tok], self.k_rows[g, :, :, tok]).then_inc(self.k_in[n], 16)


def attention_phase(nc, operands, v_aug, o_dram, table, weight_loads, weights_in):
    with ExitStack() as ctx:
        kit = Kit(nc, ctx)
        SLOTS_Q, SLOTS_ST, SLOTS_P = LEAD + 1, 3, 3
        assert NCH % SLOTS_Q == 0
        PLAN, FIRST_PLAN, LAST_PLAN = group_plan(), group_plan(first=True), group_plan(last=True)
        IN_ORDER = [w for c in range(NCH + LEAD) for w in max_events(c)]
        EVENTS = MAX_UNITS + NCH
        assert EVENTS % 2 == 0 and STEPS % SLOTS_P == 0 and UNITS % SLOTS_ST == 0
        v_sb = kit.sb("a_v", [P, NT, HPG * 32])
        for s in range(EARLY, SLOTS_Q):
            operands.q_sb.append(kit.sb(f"a_q{s}", [P, HPG, CH], BF16))
            operands.q_in.append(kit.sem(f"a_q_in{s}"))
        q_sb, k_sb, q_in, k_in = operands.q_sb, operands.k_sb, operands.q_in, operands.k_in
        ident, mask_q, mask_k = operands.masks_sb
        probs = [kit.sb(f"a_p{s}", [P, HPG, CH]) for s in range(SLOTS_P)]
        o_sb = [kit.sb(f"a_o{s}", [P, CH]) for s in range(2)]
        ZEROS = 8 * ROW
        zeros = kit.sb("a_zeros", [P, ZEROS])
        part_max = kit.sb("a_part_max", [P, TPC * HPG, NCH])
        neg_max = kit.sb("a_neg_max", [P, TPC, HPG])
        max_rest = kit.sb("a_max_rest", [P, TPC, HPG])
        max_cols = kit.sb("a_max_cols", [P, TPC, HPG, 32], BF16)

        st_ps = kit.ps("a_st_ps", [P, SLOTS_ST, CH])
        mx_ps = [kit.ps(f"a_mx_ps{s}", [P, 2, CH]) for s in range(2)]
        ot_ps = kit.ps("a_ot_ps", [P, CH])

        cols_zero = kit.sem("a_cols_zero")
        zeros_ready = kit.sem("a_zeros_ready")
        table_zeroed = kit.sem("a_table_zeroed")
        v_in = [kit.sem(f"a_v_in{n}") for n in range(NCH)]
        scores_ready = kit.sem("a_scores_ready")
        probs_ready = kit.sem("a_probs_ready")
        pv_done = kit.sem("a_pv_done")
        o_copied = kit.sem("a_o_copied")
        o_stored = [kit.sem(f"a_o_stored{s}") for s in range(2)]
        max_ready = kit.sem("a_max_ready")
        max_reduced = kit.sem("a_max_reduced")
        max_step = kit.sem("a_max_step")
        cols_ready = kit.sem("a_cols_ready")
        turned = kit.sem("a_turned")
        rows_written = kit.sem("a_rows_written")
        passed = kit.sem("a_passed")
        from_one = (scores_ready, *o_stored, o_copied)
        block = ctx.enter_context(nc.Block())
        Q_LOAD, K_LOAD = 4 * 16, 4 * 16
        MAX_STEPS = 4

        EVENT = {what: n for n, what in enumerate(IN_ORDER)}

        def load_v(eng, g, n):
            tok = slice(n * CH, (n + 1) * CH)
            eng.dma_start(v_sb[:, n * TPC:(n + 1) * TPC, :],
                          v_aug[tok, :].rearrange("(b p) (g f) -> g p b f", p=P, g=G)[g]).then_inc(v_in[n], 16)

        @block.gpsimd
        def _(pool):
            start_at_one(pool, from_one)
            pool.memset(max_cols[:], 0.0).then_inc(cols_zero, 1)
            pool.memset(zeros[:], 0.0).then_inc(zeros_ready, 1)
            pool.wait_ge(zeros_ready, 1)
            flat = table.rearrange("(p r) c -> p (r c)", p=P)
            fills = [(flat[:, f:f + ZEROS], zeros[:], table_zeroed) for f in range(0, flat.shape[1], ZEROS)]
            background = fills + [(dst, src, weights_in) for dst, src in weight_loads]
            for n, (dst, src, done) in enumerate(background):
                pool.wait_ge(scores_ready, (n + 1) * (G - 1) * UNITS // len(background) + ONE)
                pool.dma_start(dst, src).then_inc(done, 16)
            pool.wait_ge(table_zeroed, 16 * len(fills))

        @block.sync
        def _(sp):
            def store_o(g, c):
                sp.wait_ge(o_copied, g * NCH + (c + 1) + ONE)
                pass_wait(sp, passed)
                sp.dma_start(o_dram[g, :, c * CH:(c + 1) * CH], o_sb[c % 2][:]).then_inc(o_stored[c % 2], 16)

            for n in range(NCH):
                if n >= EARLY:
                    operands.load_k(sp, 0, n)
                if EARLY <= n < LEAD:
                    operands.load_q(sp, 0, n)
                load_v(sp, 0, n)
            def group(g, nxt):
                for c in range(NCH):
                    if c + LEAD < NCH or nxt is not None:
                        sp.wait_ge(scores_ready, g * UNITS + STEP0[c] * HPG + ONE)
                        pass_wait(sp, passed)
                        operands.load_q(sp, g if c + LEAD < NCH else nxt, (c + LEAD) % NCH)
                    if c > 0:
                        store_o(g, c - 1)
                for n in range(NCH if nxt is not None else 0):
                    last_step = STEP0[NCH - 1] + TPC * (n + 1)
                    sp.wait_ge(scores_ready, g * UNITS + last_step * HPG + ONE)
                    pass_wait(sp, passed)
                    sp.wait_ge(pv_done, g * STEPS + last_step)
                    pass_wait(sp, passed)
                    operands.load_k(sp, nxt, n)
                    load_v(sp, nxt, n)
                store_o(g, NCH - 1)

            with sp.Fori(0, G - 1) as g:
                group(g, g + 1)
            group(G - 1, None)
            for s in range(2):
                sp.wait_ge(o_stored[s], 16 * G * NCH // 2 + ONE)

        @block.tensor
        def _(pe):
            pe.wait_ge(operands.masks_in, 48)

            def wait_slot(g, n):
                if n < 2:
                    return
                what, c, *i = IN_ORDER[n - 2]
                if what == "unit":
                    pe.wait_ge(max_reduced, g * MAX_UNITS + (max_unit0(c) + i[0] + 1))
                else:
                    pe.wait_ge(rows_written, (g * NCH + (c + 1)) * HPG)

            def max_unit(slot, c, kc, j, hp):
                diagonal = kc == c % NCH
                width = (j + 1) * P if diagonal else CH
                for hh in range(2):
                    h = 2 * hp + hh
                    last = nc.tensor.matmul(mx_ps[slot][:, hh, 0:width], q_sb[c % SLOTS_Q][0:ROWS, h, j * P:(j + 1) * P],
                                            k_sb[0:ROWS, h, kc * CH:kc * CH + width], start=True, stop=not diagonal)
                    if diagonal:
                        last = nc.tensor.matmul(mx_ps[slot][:, hh, width - P:width], ident[:], mask_q[:],
                                                start=False, stop=True)
                last.then_inc(max_ready, 1)

            def turn(slot):
                for j in range(TPC):
                    last = nc.tensor.matmul(mx_ps[slot][:, 0, j * P:(j + 1) * P],
                                            max_cols[:, j, :, :].rearrange("p h e -> p (h e)"), ident[:],
                                            start=True, stop=True)
                last.then_inc(turned, 1)

            def max_event(g, what, c, i=None):
                n = EVENT[(what, c) if i is None else (what, c, i)]
                if what == "unit":
                    kc, j, hp = max_units(c % NCH)[i]
                    if i == 0:
                        pe.wait_ge(q_in[c % SLOTS_Q], (g * (NCH // SLOTS_Q) + (c // SLOTS_Q + 1)) * Q_LOAD)
                    if kc == c % NCH and j == 0 and hp == 0:
                        pe.wait_ge(k_in[kc], (g + (c // NCH + 1)) * K_LOAD)
                    wait_slot(g, n)
                    max_unit(n % 2, c, kc, j, hp)
                else:
                    wait_slot(g, n)
                    pe.wait_ge(cols_ready, g * NCH + (c + 1))
                    turn(n % 2)

            for c in range(FIRST_LEAD):
                for what in max_events(c):
                    max_event(0, *what)

            def group(g, plan):
                def pv(c, b):
                    n = TPC * c
                    q0 = max(0, b - n) * P
                    s = STEP0[c] + b
                    if b == 0:
                        pe.wait_ge(o_copied, g * NCH + c + ONE)
                    if b >= n and c == b // TPC and b % TPC == 0:
                        pe.wait_ge(v_in[c], (g + 1) * 16)
                    pe.wait_ge(probs_ready, g * UNITS + (s + 1) * HPG)
                    for h in range(HPG):
                        last = nc.tensor.matmul(ot_ps[32 * h:32 * h + 32, q0:CH], v_sb[:, b, 32 * h:32 * h + 32],
                                                probs[s % SLOTS_P][:, h, q0:CH], start=(b == 0),
                                                stop=(b == n + TPC - 1))
                    last.then_inc(pv_done, 1)

                pending = None
                for c in range(NCH):
                    pe.wait_ge(rows_written, (g * NCH + (c + 1)) * HPG)
                    for i in range(HPG * chunk_steps(c)):
                        b, h = divmod(i, HPG)
                        u = STEP0[c] * HPG + i
                        j = b - TPC * c
                        q0 = max(0, j) * P
                        if u >= SLOTS_ST:
                            pe.wait_ge(probs_ready, g * UNITS + (u - SLOTS_ST + 1))
                        last = nc.tensor.matmul(st_ps[:, u % SLOTS_ST, q0:CH], k_sb[0:ROWS, h, b * P:(b + 1) * P],
                                                q_sb[c % SLOTS_Q][0:ROWS, h, q0:CH], start=True, stop=(j < 0))
                        if j >= 0:
                            last = nc.tensor.matmul(st_ps[:, u % SLOTS_ST, q0:q0 + P], ident[:], mask_k[:],
                                                    start=False, stop=True)
                        last.then_inc(scores_ready, 1)
                        if h == 3:
                            pending = (c, b)
                        for what in plan.get(u, ()):
                            max_event(g, *what)
                        if h == 2 and pending is not None:
                            pv(*pending)
                pv(*pending)

            group(0, FIRST_PLAN)
            with pe.Fori(1, G - 1) as g:
                group(g, PLAN)
            group(G - 1, LAST_PLAN)

        @block.scalar
        def _(act):
            def write_rows(g, c):
                slot = EVENT["turn", c] % 2
                act.wait_ge(turned, g * NCH + (c + 1))
                for h in range(HPG):
                    nc.scalar.activation(q_sb[c % SLOTS_Q][MAXROW:MAXROW + 3, h, :],
                                         mx_ps[slot][32 * h:32 * h + 3, 0, :], ACT.Copy).then_inc(rows_written, 1)

            for c in range(FIRST_LEAD - 1):
                write_rows(0, c)

            def group(g, plan):
                def copy_out(c):
                    act.wait_ge(pv_done, g * STEPS + (STEP0[c] + chunk_steps(c)))
                    act.wait_ge(o_stored[c % 2], (g * (NCH // 2) + c // 2) * 16 + ONE)
                    nc.scalar.activation(o_sb[c % 2][:], ot_ps[:], ACT.Copy).then_inc(o_copied, 1)

                for c in range(NCH):
                    for i in range(HPG * chunk_steps(c)):
                        b, h = divmod(i, HPG)
                        s = STEP0[c] + b
                        q0 = max(0, b - TPC * c) * P
                        act.wait_ge(scores_ready, g * UNITS + (s * HPG + h + 1) + ONE)
                        if h == 0 and s >= SLOTS_P:
                            act.wait_ge(pv_done, g * STEPS + (s - SLOTS_P + 1))
                        nc.scalar.activation(probs[s % SLOTS_P][:, h, q0:CH], st_ps[:, (s * HPG + h) % SLOTS_ST, q0:CH],
                                             ACT.Exp).then_inc(probs_ready, 1)
                        if c > 0 and i == 4:
                            copy_out(c - 1)
                        for what in plan.get(s * HPG + h, ()):
                            if what[0] == "turn":
                                write_rows(g, what[1])
                copy_out(NCH - 1)

            group(0, FIRST_PLAN)
            with act.Fori(1, G - 1) as g:
                group(g, PLAN)
            group(G - 1, LAST_PLAN)

        @block.vector
        def _(dve):
            def reduce_units(g, c):
                for i, (kc, j, hp) in enumerate(max_units(c % NCH)):
                    width = (j + 1) * P if kc == c % NCH else CH
                    dve.wait_ge(max_ready, g * MAX_UNITS + (max_unit0(c) + i + 1))
                    nc.vector.tensor_reduce(part_max[:, HPG * j + 2 * hp:HPG * j + 2 * hp + 2, kc],
                                            mx_ps[EVENT["unit", c, i] % 2][:, :, 0:width], AX.X,
                                            ALU.max).then_inc(max_reduced, 1)

            def split_max(g, c):
                turn_no = g * NCH + c
                step = turn_no * MAX_STEPS
                dve.wait_ge(max_reduced, g * MAX_UNITS + max_unit0(c + 1))
                nc.vector.tensor_reduce(neg_max[:].rearrange("p j h -> p (j h)"), part_max[:, :, 0:c % NCH + 1], AX.X,
                                        ALU.max, negate=True).then_inc(max_step, 1)
                dve.wait_ge(turned, turn_no)
                dve.wait_ge(max_step, step + 1)
                nc.vector.tensor_copy(max_cols[:, :, :, 0], neg_max[:]).then_inc(max_step, 1)
                dve.wait_ge(max_step, step + 2)
                nc.vector.tensor_tensor(max_rest[:], neg_max[:], max_cols[:, :, :, 0], ALU.subtract).then_inc(
                    max_step, 1)
                dve.wait_ge(max_step, step + 3)
                nc.vector.tensor_copy(max_cols[:, :, :, 1], max_rest[:]).then_inc(max_step, 1)
                dve.wait_ge(max_step, step + 4)
                nc.vector.tensor_tensor(max_cols[:, :, :, 2], max_rest[:], max_cols[:, :, :, 1],
                                        ALU.subtract).then_inc(cols_ready, 1)

            dve.wait_ge(cols_zero, 1)
            for c in range(NCH + LEAD):
                reduce_units(0, c)
                split_max(0, c)
            with dve.Fori(1, G - 1) as g:
                for c in range(LEAD, NCH + LEAD):
                    reduce_units(g, c)
                    split_max(g, c)
            for c in range(LEAD, NCH):
                reduce_units(G - 1, c)
                split_max(G - 1, c)


class Steps:

    def __init__(self, eng, sem, base):
        self.eng, self.sem, self.base, self.count = eng, sem, base, 0

    def link(self, instruction):
        self.count += 1
        instruction.then_inc(self.sem, 1)
        self.eng.wait_ge(self.sem, self.base + self.count)


def combine_phase(nc, x, wo, wr, br, eye, tri, tile_starts, o_dram, x1, xs_dram, weight, tile_expert, tile_expert_f,
                  tile_row):
    with ExitStack() as ctx:
        kit = Kit(nc, ctx)
        ident = kit.sb("c_ident", [P, P])
        wo_sb = kit.sb("c_wo", [P, KC, C])
        wr_sb = kit.sb("c_wr", [P, KC, E])
        br_sb = kit.sb("c_br", [P, E])
        tri_sb = kit.sb("c_tri", [P, P])
        ones = kit.sb("c_ones", [P, P])
        starts_sb = kit.sb("c_tile_starts", [P, TILES])
        experts = kit.sb("c_experts", [P, E])
        regions = kit.sb("c_regions", [P, E])
        o_in_sb = [kit.sb(f"c_o{s}", [P, G, CH]) for s in range(2)]
        xn2 = kit.sb("c_xn2", [P, NT, ROW])
        recip = kit.sb("c_recip", [P, TPC, NH])
        o_norm = kit.sb("c_o_norm", [P, TPC, C])
        o_nT = kit.sb("c_o_nT", [P, TPC, KC * P])
        y = [kit.sb(f"c_y{s}", [P, TPC, C]) for s in range(2)]
        x2T = kit.sb("c_x2T", [P, TPC, KC * P])
        logits = kit.sb("c_logits", [P, TPC, E])
        top8 = kit.sb("c_top8", [P, NT, E])
        idx8 = kit.sb("c_idx8", [P, TPC, E], U32)
        idx_f = kit.sb("c_idx_f", [P, TPC, TOPK])
        chosen = kit.sb("c_chosen", [P, TOPK, TPC, E])
        both = kit.sb("c_both", [P, TPC + 1, E])
        pos = [kit.sb(f"c_pos{s}", [P, TPC + 1, E]) for s in range(2)]
        picked = kit.sb("c_picked", [P, TOPK, TPC, E])
        x_place_f = kit.sb("c_x_place_f", [P, TOPK, TPC])
        x_place = kit.sb("c_x_place", [P, TOPK, NT], U32)
        stats = kit.sb("c_stats", [P, TPC, 6])
        mv = kit.sb("c_mv", [P, TPC, 2])
        rstd = kit.sb("c_rstd", [P, TPC])
        shift = kit.sb("c_shift", [P, TPC])
        var_eps = [kit.sb(f"c_var_eps{s}", [P, TPC]) for s in range(2)]
        std = [kit.sb(f"c_std{s}", [P, TPC]) for s in range(2)]
        diff = kit.sb("c_diff", [P, NT])
        ex = kit.sb("c_ex", [P, NT])
        denom = kit.sb("c_denom", [P, NT])
        padded = kit.sb("c_padded", [P, E])
        count_i = kit.sb("c_count_i", [P, E], I32)
        ends = kit.sb("c_ends", [P, E])
        skip = kit.sb("c_skip", [P, E])
        below = kit.sb("c_below", [P, TILES, E - 1])
        tile_row_f = kit.sb("c_tile_row_f", [P, TILES])
        o_ps = [kit.ps(f"c_o_ps{s}", [P, NH, 32]) for s in range(2)]
        tr_ps = [kit.ps(f"c_tr_ps{s}", [P, 2, KC * P]) for s in range(2)]
        att_ps = kit.ps("c_att_ps", [P, TPC, C])
        log_ps = kit.ps("c_log_ps", [P, TPC, E])
        pos_ps = kit.ps("c_pos_ps", [P, TPC + 1, E])

        ident_in = kit.sem("c_ident_in")
        weights_in = kit.sem("c_weights_in")
        o_first = [kit.sem(f"c_o_first{half}") for half in range(2)]
        o_in = [kit.sem(f"c_o_in{s}") for s in range(2)]
        x_in = [kit.sem(f"c_x_in{n}") for n in range(NCH)]
        ones_ready = kit.sem("c_ones_ready")
        o_turned = kit.sem("c_o_turned")
        o_divided = kit.sem("c_o_divided")
        tr_turned = kit.sem("c_tr_turned")
        tr_copied = kit.sem("c_tr_copied")
        att_done = kit.sem("c_att_done")
        ln_var = kit.sem("c_ln_var")
        ln_std = kit.sem("c_ln_std")
        ln_shift = kit.sem("c_ln_shift")
        att_copied = kit.sem("c_att_copied")
        y_ready = kit.sem("c_y_ready")
        x2_ready = kit.sem("c_x2_ready")
        logits_done = kit.sem("c_logits_done")
        logits_read = kit.sem("c_logits_read")
        both_ready = kit.sem("c_both_ready")
        counted = kit.sem("c_counted")
        pos_ready = kit.sem("c_pos_ready")
        places_ready = kit.sem("c_places_ready")
        scattered = kit.sem("c_scattered")
        diff_ready = kit.sem("c_diff_ready")
        exp_ready = kit.sem("c_exp_ready")
        step = kit.sem("c_step")
        block = ctx.enter_context(nc.Block())
        STEPS_HERE = NCH + 3

        TR_USES = [(kind, m, jj) for n in range(STEPS_HERE) for kind, m in (("x2", n - 2), ("o", n)) if 0 <= m < NCH
                   for jj in range(2)]
        TR_USE = {use: number for number, use in enumerate(TR_USES)}

        @block.sync
        def _(sp):
            def load_o(n):
                sp.dma_start(o_in_sb[n % 2][:], o_dram[:, :, n * CH:(n + 1) * CH].rearrange("g r t -> r g t")
                             ).then_inc(o_in[n % 2], 16)

            def load_x(n):
                sp.dma_start(x1[:, n * TPC:(n + 1) * TPC, :], x[n * CH:(n + 1) * CH, :].rearrange(
                    "(j p) c -> p j c", p=P)).then_inc(x_in[n], 16)

            sp.dma_start(ident[:], eye).then_inc(ident_in, 16)
            for half in range(2):
                tok = slice(half * CH // 2, (half + 1) * CH // 2)
                sp.dma_start(o_in_sb[0][:, :, tok], o_dram[:, :, tok].rearrange("g r t -> r g t")).then_inc(
                    o_first[half], 16)
            sp.dma_start(wo_sb[:], wo.rearrange("(k p) n -> p k n", p=P)).then_inc(weights_in, 16)
            sp.dma_start(wr_sb[:], wr.rearrange("(k p) n -> p k n", p=P)).then_inc(weights_in, 16)
            load_o(1)
            sp.dma_start(br_sb[:], br.partition_broadcast(P)).then_inc(weights_in, 16)
            sp.dma_start(tri_sb[:], tri).then_inc(weights_in, 16)
            sp.dma_start(starts_sb[:], tile_starts.partition_broadcast(P)).then_inc(weights_in, 16)
            load_x(0)
            load_x(1)
            for n in range(2, NCH):
                sp.wait_ge(o_turned, (n - 1) * TPC)
                load_o(n)
                load_x(n)

        @block.gpsimd
        def _(pool):
            pool.memset(ones[:], 1.0)
            pool.memset(both[:, TPC, :], 0.0)
            pool.iota(xn2[:, :, C], [[P, NT]], base=-FAR, channel_multiplier=1, allow_small_or_imprecise_dtypes=True)
            pool.iota(experts[:], [[1, E]], base=0, channel_multiplier=0, allow_small_or_imprecise_dtypes=True)
            pool.iota(regions[:], [[T, E]], base=0, channel_multiplier=0,
                      allow_small_or_imprecise_dtypes=True).then_inc(ones_ready, 1)
            for n in range(NCH):
                pool.wait_ge(places_ready, n + 1)
                for t in range(n * TPC, (n + 1) * TPC):
                    for k in range(TOPK):
                        pool.indirect_dma_start(out=xs_dram, out_offset=bass.IndirectOffsetOnAxis(
                            ap=x_place[:, k, t:t + 1], axis=0), in_=xn2[:, t, :], in_offset=None).then_inc(scattered, 16)
            pool.wait_ge(scattered, TOPK * NT * 16)

        @block.tensor
        def _(pe):
            def turn_o(n, j):
                if n == 0 and j % 2 == 0:
                    pe.wait_ge(o_first[j // 2], 16)
                if n > 0 and j == 0:
                    pe.wait_ge(o_in[n % 2], 16 * ((n + 1) // 2))
                if n * TPC + j >= 2:
                    pe.wait_ge(o_divided, n * TPC + j - 1)
                for g in range(G):
                    last = nc.tensor.transpose(o_ps[j % 2][:, 4 * g:4 * g + 4, :].rearrange("p h e -> p (h e)"),
                                               o_in_sb[n % 2][:, g, j * P:(j + 1) * P], ident[:])
                last.then_inc(o_turned, 1)

            def turn_pair(kind, m, jj):
                use = TR_USE[kind, m, jj]
                if use >= 2:
                    pe.wait_ge(tr_copied, use - 1)
                if kind == "x2":
                    pe.wait_ge(x2_ready, m + 1)
                else:
                    pe.wait_ge(o_divided, m * TPC + 2 * jj + 2)
                for j in (2 * jj, 2 * jj + 1):
                    src = xn2[:, m * TPC + j, :] if kind == "x2" else o_norm[:, j, :]
                    for k in range(KC):
                        last = nc.tensor.transpose(tr_ps[jj][:, j % 2, k * P:(k + 1) * P], src[:, k * P:(k + 1) * P],
                                                   ident[:])
                last.then_inc(tr_turned, 1)

            def multiply(kind, m, dst, srcT, w, done):
                for jj in range(2):
                    pe.wait_ge(tr_copied, TR_USE[kind, m, jj] + 1)
                    for j in (2 * jj, 2 * jj + 1):
                        for k in range(KC):
                            last = nc.tensor.matmul(dst[:, j, :], srcT[:, j, k * P:(k + 1) * P], w[:, k, :],
                                                    start=(k == 0), stop=(k == KC - 1))
                last.then_inc(done, 1)

            def count(m):
                pe.wait_ge(both_ready, m + 1)
                if m >= 1:
                    pe.wait_ge(pos_ready, m)
                flat = both[:].rearrange("p j e -> p (j e)")
                out = pos_ps[:].rearrange("p j e -> p (j e)")
                nc.tensor.matmul(out, tri_sb[:], flat, start=True, stop=False)
                for back in range(1, TPC + 1):
                    last = nc.tensor.matmul(out[:, back * E:], ones[:], flat[:, 0:(TPC + 1 - back) * E], start=False,
                                            stop=(back == TPC))
                last.then_inc(counted, 1)

            pe.wait_ge(ident_in, 16)
            turn_o(0, 0)
            turn_o(0, 1)
            pe.wait_ge(ones_ready, 1)
            for n in range(STEPS_HERE):
                judged = n - 2 if 0 <= n - 2 < NCH else None
                routed = n - 3 if n >= 3 else None
                if n < NCH:
                    turn_o(n, 2)
                    turn_o(n, 3)
                if n >= NCH:
                    count(routed)
                if judged is not None:
                    turn_pair("x2", judged, 0)
                    turn_pair("x2", judged, 1)
                if n < NCH:
                    turn_pair("o", n, 0)
                if judged is not None:
                    if judged >= 1:
                        pe.wait_ge(logits_read, judged)
                    multiply("x2", judged, log_ps, x2T, wr_sb, logits_done)
                if routed is not None and n < NCH:
                    count(routed)
                if n < NCH:
                    turn_pair("o", n, 1)
                if n == 0:
                    pe.wait_ge(weights_in, 5 * 16)
                if n + 1 < NCH:
                    turn_o(n + 1, 0)
                    turn_o(n + 1, 1)
                if n < NCH:
                    if n >= 1:
                        pe.wait_ge(att_copied, n)
                    multiply("o", n, att_ps, o_nT, wo_sb, att_done)

        @block.scalar
        def _(act):
            def copy_pair(kind, m, jj):
                if m >= 1 and jj == 0:
                    act.wait_ge(logits_done if kind == "x2" else att_done, m)
                act.wait_ge(tr_turned, TR_USE[kind, m, jj] + 1)
                dst = x2T if kind == "x2" else o_nT
                nc.scalar.activation(dst[:, 2 * jj:2 * jj + 2, :], tr_ps[jj][:], ACT.Copy).then_inc(tr_copied, 1)

            def norm(k, m, dst, src, done):
                act.wait_ge(ln_var, 2 * m + k + 1)
                nc.scalar.activation(std[k][:], var_eps[k][:], ACT.Sqrt).then_inc(ln_std, 1)
                act.wait_ge(ln_shift, 2 * m + k + 1)
                for j in range(TPC):
                    last = nc.scalar.activation(dst[:, j, :], src[:, j, :], ACT.Identity, bias=shift[:, j:j + 1],
                                                scale=rstd[:, j:j + 1])
                last.then_inc(done, 1)

            for n in range(STEPS_HERE):
                if 0 <= n - 2 < NCH:
                    copy_pair("x2", n - 2, 0)
                    copy_pair("x2", n - 2, 1)
                if n < NCH:
                    copy_pair("o", n, 0)
                if 1 <= n <= NCH:
                    norm(0, n - 1, y[(n - 1) % 2], y[(n - 1) % 2], y_ready)
                if n < NCH:
                    copy_pair("o", n, 1)
                if 1 <= n <= NCH:
                    here = slice((n - 1) * TPC, n * TPC)
                    norm(1, n - 1, xn2[:, here, 0:C], x1[:, here, :], x2_ready)
                if n < NCH:
                    act.wait_ge(att_done, n + 1)
                    for jj in range(2):
                        last = nc.scalar.activation(y[n % 2][:, 2 * jj:2 * jj + 2, :], att_ps[:, 2 * jj:2 * jj + 2, :],
                                                    ACT.Copy)
                    last.then_inc(att_copied, 1)
            act.wait_ge(diff_ready, 1)
            nc.scalar.activation(ex[:], diff[:], ACT.Exp).then_inc(exp_ready, 1)

        @block.vector
        def _(dve):
            st = Steps(dve, step, 0)

            def divide(n, tiles):
                if n >= 1:
                    dve.wait_ge(tr_turned, TR_USE["o", n - 1, 1] + 1)
                for j in tiles:
                    dve.wait_ge(o_turned, n * TPC + (j + 1))
                    st.link(nc.vector.reciprocal(recip[:, j, :], o_ps[j % 2][:, :, HD]))
                    nc.vector.tensor_tensor(o_norm[:, j, :].rearrange("p (h d) -> p h d", h=NH),
                                            o_ps[j % 2][:, :, 0:HD],
                                            recip[:, j, :].unsqueeze(2).broadcast_to([P, NH, HD]),
                                            ALU.mult).then_inc(o_divided, 1)

            def variance(src, k):
                for j in range(TPC):
                    last = nc.vector.bn_stats(stats[:, j, :], src[:, j, :])
                st.link(last)
                for j in range(TPC):
                    last = nc.vector.bn_aggr(mv[:, j, :], stats[:, j, :])
                st.link(last)
                nc.vector.tensor_scalar_add(var_eps[k][:], mv[:, :, 1], EPS).then_inc(ln_var, 1)

            def scale_and_shift(k, n):
                dve.wait_ge(ln_std, 2 * n + k + 1)
                st.link(nc.vector.reciprocal(rstd[:], std[k][:]))
                nc.vector.scalar_tensor_tensor(out=shift[:], in0=mv[:, :, 0], scalar=-1.0, in1=rstd[:], op0=ALU.mult,
                                               op1=ALU.mult).then_inc(ln_shift, 1)

            def choose(m):
                dve.wait_ge(logits_done, m + 1)
                nc.vector.tensor_tensor(logits[:], log_ps[:], br_sb[:].unsqueeze(1).broadcast_to([P, TPC, E]),
                                        ALU.add).then_inc(logits_read, 1)
                dve.wait_ge(logits_read, m + 1)
                for j in range(TPC):
                    last = nc.vector.max(top8[:, m * TPC + j, :], logits[:, j, :])
                st.link(last)
                for j in range(TPC):
                    last = nc.vector.max_index(idx8[:, j, :], top8[:, m * TPC + j, :], logits[:, j, :])
                st.link(last)
                st.link(nc.vector.tensor_copy(idx_f[:], idx8[:, :, 0:TOPK]))
                nc.vector.tensor_copy(xn2[:, m * TPC:(m + 1) * TPC, C + 1], idx_f[:, :, 0])
                for k in range(TOPK):
                    last = nc.vector.tensor_tensor(chosen[:, k], idx_f[:, :, k:k + 1].broadcast_to([P, TPC, E]),
                                                   experts[:].unsqueeze(1).broadcast_to([P, TPC, E]), ALU.is_equal)
                st.link(last)
                if m >= 1:
                    dve.wait_ge(counted, m)
                nc.vector.tensor_tensor(both[:, 0:TPC, :], chosen[:, 0], chosen[:, 1], ALU.add).then_inc(both_ready, 1)

            def locate(m):
                dve.wait_ge(counted, m + 1)
                before = pos[(m - 1) % 2][:, TPC, :] if m >= 1 else regions[:]
                nc.vector.tensor_tensor(pos[m % 2][:], pos_ps[:], before.unsqueeze(1).broadcast_to([P, TPC + 1, E]),
                                        ALU.add).then_inc(pos_ready, 1)
                dve.wait_ge(pos_ready, m + 1)
                for k in range(TOPK):
                    last = nc.vector.tensor_tensor(picked[:, k], pos[m % 2][:, 0:TPC, :], chosen[:, k], ALU.mult)
                st.link(last)

            def hand_out(m):
                st.link(nc.vector.tensor_reduce(x_place_f[:], picked[:], AX.X, ALU.add))
                nc.vector.tensor_copy(x_place[:, :, m * TPC:(m + 1) * TPC], x_place_f[:]).then_inc(places_ready, 1)
                dve.wait_ge(places_ready, m + 1)

            for n in range(STEPS_HERE):
                if n == 1:
                    dve.wait_ge(weights_in, 5 * 16)
                    dve.wait_ge(ones_ready, 1)
                normed = n - 1 if 1 <= n <= NCH else None
                if n < NCH:
                    divide(n, (0, 1))
                if n >= 3:
                    choose(n - 3)
                if normed is not None:
                    if normed >= 1:
                        dve.wait_ge(x2_ready, normed)
                    dve.wait_ge(att_copied, normed + 1)
                    variance(y[normed % 2], 0)
                if normed is not None:
                    scale_and_shift(0, normed)
                if n < NCH:
                    divide(n, (2, 3))
                if n >= 3:
                    locate(n - 3)
                    hand_out(n - 3)
                if normed is not None:
                    x1_c = x1[:, normed * TPC:(normed + 1) * TPC, :]
                    dve.wait_ge(y_ready, normed + 1)
                    dve.wait_ge(x_in[normed], 16)
                    st.link(nc.vector.tensor_tensor(x1_c, y[normed % 2][:], x1_c, ALU.add))
                    variance(x1_c, 1)
                    scale_and_shift(1, normed)

            st.link(nc.vector.tensor_tensor(padded[:], pos[(NCH - 1) % 2][:, TPC, :], regions[:], ALU.subtract))
            st.link(nc.vector.tensor_scalar_add(padded[:], padded[:], float(P - 1)))
            st.link(nc.vector.tensor_copy(count_i[:], padded[:]))
            log_p = P.bit_length() - 1
            st.link(nc.vector.tensor_scalar(count_i[:], count_i[:], log_p, log_p, ALU.arith_shift_right,
                                            ALU.logical_shift_left))
            st.link(nc.vector.tensor_copy(padded[:], count_i[:]))
            st.link(nc.vector.tensor_tensor_scan(ends[:], ones[:, 0:E], padded[:], 0.0, ALU.mult, ALU.add))
            nc.vector.tensor_scalar(skip[:], padded[:], -1.0, float(T), ALU.mult, ALU.add)
            st.link(nc.vector.tensor_tensor(below[:], ends[:, 0:E - 1].unsqueeze(1).broadcast_to([P, TILES, E - 1]),
                                            starts_sb[:].unsqueeze(2).broadcast_to([P, TILES, E - 1]), ALU.is_le))
            st.link(nc.vector.tensor_reduce(tile_expert_f[:], below[:], AX.X, ALU.add))
            st.link(nc.vector.tensor_tensor(below[:], below[:],
                                            skip[:, 0:E - 1].unsqueeze(1).broadcast_to([P, TILES, E - 1]), ALU.mult))
            st.link(nc.vector.tensor_reduce(tile_row_f[:], below[:], AX.X, ALU.add))
            nc.vector.tensor_copy(tile_expert[:], tile_expert_f[:])
            st.link(nc.vector.tensor_tensor(tile_row_f[:], tile_row_f[:], starts_sb[:], ALU.add))
            nc.vector.tensor_copy(tile_row[:], tile_row_f[:])
            nc.vector.tensor_tensor(diff[:], top8[:, :, 1], top8[:, :, 0], ALU.subtract).then_inc(diff_ready, 1)
            dve.wait_ge(exp_ready, 1)
            st.link(nc.vector.tensor_scalar_add(denom[:], ex[:], 1.0))
            st.link(nc.vector.reciprocal(weight[:, 0, :], denom[:]))
            nc.vector.tensor_tensor(weight[:, 1, :], ex[:], weight[:, 0, :], ALU.mult)


def experts_phase(nc, eye, w1_sb, w3_sb, w2_sb, weights_in, weights_count, tile_expert, tile_expert_f, tile_row, xs_dram,
                  y_dram):
    with ExitStack() as ctx:
        kit = Kit(nc, ctx)
        FC = FF // P
        ident = kit.sb("e_ident", [P, P])
        xs = [kit.sb(f"e_xs{s}", [P, ROW]) for s in range(2)]
        xsT = [kit.sb(f"e_xsT{s}", [P, C]) for s in range(2)]
        act_gate = kit.sb("e_act_gate", [P, FF])
        hidden = kit.sb("e_hidden", [P, FF])
        hT = kit.sb("e_hT", [P, FF])
        ys = [kit.sb(f"e_ys{s}", [P, C]) for s in range(2)]
        dump = kit.sb("e_dump", [P, TILES])
        second = kit.sb("e_second", [P, 1])
        far_place = kit.sb("e_far_place", [P, 1])
        place_f = [kit.sb(f"e_place_f{s}", [P, 1]) for s in range(2)]
        place = [kit.sb(f"e_place{s}", [P, 1], U32) for s in range(2)]
        xT_ps = kit.ps("e_xT_ps", [P, C])
        gate_ps = [kit.ps(f"e_gate_ps{s}", [P, FF]) for s in range(2)]
        up_ps = [kit.ps(f"e_up_ps{s}", [P, FF]) for s in range(2)]
        hT_ps = kit.ps("e_hT_ps", [P, FF])
        y_ps = kit.ps("e_y_ps", [P, C])

        ident_in = kit.sem("e_ident_in")
        x_in = [kit.sem(f"e_x_in{s}") for s in range(2)]
        x_turned = kit.sem("e_x_turned")
        xT_copied = kit.sem("e_xT_copied")
        gate_done = kit.sem("e_gate_done")
        up_done = kit.sem("e_up_done")
        silu_done = kit.sem("e_silu_done")
        hidden_done = kit.sem("e_hidden_done")
        h_turned = kit.sem("e_h_turned")
        hT_copied = kit.sem("e_hT_copied")
        y_done = kit.sem("e_y_done")
        y_copied = kit.sem("e_y_copied")
        place_step = kit.sem("e_place_step")
        place_known = kit.sem("e_place_known")
        place_ready = kit.sem("e_place_ready")
        dump_ready = kit.sem("e_dump_ready")
        y_stored = [kit.sem(f"e_y_stored{s}") for s in range(2)]
        passed = kit.sem("e_passed")
        passed_pool = kit.sem("e_passed_pool")
        assert TILES % 2 == 1
        LAST = TILES - 1
        block = ctx.enter_context(nc.Block())

        @block.sync
        def _(sp):
            def rows(n):
                row = sp.value_load(tile_row[0:1, bass.ds(n, 1)], min_val=0, max_val=TABLE_ROWS - P)
                return bass.ds(row, P)

            def load(n, s):
                sp.dma_start(xs[s][:], xs_dram[rows(n), :]).then_inc(x_in[s], 16)

            def next_load(n, s):
                sp.wait_ge(place_known, n - 1)
                pass_wait(sp, passed)
                load(n, s)

            load(0, 0)
            load(1, 1)
            sp.dma_start(ident[:], eye).then_inc(ident_in, 16)
            with sp.Fori(1, TILES // 2) as it:
                for s in range(2):
                    next_load(it * 2 + s, s)
            next_load(LAST, 0)

        @block.gpsimd
        def _(pool):
            pool.iota(dump[:], [[P, TILES]], base=TOPK * T, channel_multiplier=1,
                      allow_small_or_imprecise_dtypes=True).then_inc(dump_ready, 1)

            def scatter(n, s):
                pool.wait_ge(y_copied, n + 1)
                pass_wait(pool, passed_pool)
                pool.indirect_dma_start(out=y_dram, out_offset=bass.IndirectOffsetOnAxis(ap=place[s][:], axis=0),
                                        in_=ys[s][:], in_offset=None).then_inc(y_stored[s], 16)

            with pool.Fori(0, TILES // 2) as it:
                for s in range(2):
                    scatter(it * 2 + s, s)
            scatter(LAST, 0)
            for s in range(2):
                pool.wait_ge(y_stored[s], 16 * (TILES // 2 + (1 - s)))

        @block.tensor
        def _(pe):
            pe.wait_ge(ident_in, 16)
            pe.wait_ge(weights_in, weights_count)

            def turn_x(n, s):
                pe.wait_ge(x_in[s], (n + (2 - s)) * 8)
                pe.wait_ge(xT_copied, n)
                for k in range(KC):
                    last = nc.tensor.transpose(xT_ps[:, k * P:(k + 1) * P], xs[s][:, k * P:(k + 1) * P], ident[:])
                last.then_inc(x_turned, 1)

            def product(n, s, dst, w, expert, done):
                for k in range(KC):
                    last = nc.tensor.matmul(dst[s][:], xsT[s][:, k * P:(k + 1) * P], w[:, k, bass.ds(expert * FF, FF)],
                                            start=(k == 0), stop=(k == KC - 1))
                last.then_inc(done, 1)

            def hidden_layer(n, s, after, between=None):
                e = pe.value_load(tile_expert[0:1, bass.ds(n, 1)], min_val=0, max_val=E - 1)
                pe.wait_ge(xT_copied, n + 1)
                if after:
                    pe.wait_ge(silu_done, n - 1)
                product(n, s, gate_ps, w1_sb, e, gate_done)
                if between is not None:
                    turn_hidden(between)
                if after:
                    pe.wait_ge(hidden_done, n - 1)
                product(n, s, up_ps, w3_sb, e, up_done)

            def turn_hidden(n):
                pe.wait_ge(hidden_done, n + 1)
                pe.wait_ge(hT_copied, n)
                for k in range(FC):
                    last = nc.tensor.transpose(hT_ps[:, k * P:(k + 1) * P], hidden[:, k * P:(k + 1) * P], ident[:])
                last.then_inc(h_turned, 1)

            def down(n):
                e = pe.value_load(tile_expert[0:1, bass.ds(n, 1)], min_val=0, max_val=E - 1)
                pe.wait_ge(hT_copied, n + 1)
                pe.wait_ge(y_copied, n)
                for k in range(FC):
                    last = nc.tensor.matmul(y_ps[:], hT[:, k * P:(k + 1) * P], w2_sb[:, k, bass.ds(e * C, C)],
                                            start=(k == 0), stop=(k == FC - 1))
                last.then_inc(y_done, 1)

            turn_x(0, 0)
            hidden_layer(0, 0, False)
            turn_x(1, 1)
            hidden_layer(1, 1, False, 0)
            turn_x(2, 0)
            down(0)
            with pe.Fori(0, TILES // 2 - 1) as it:
                for s in range(2):
                    n = it * 2 + (2 + s)
                    hidden_layer(n, s, True, n - 1)
                    turn_x(n + 1, 1 - s)
                    down(n - 1)
            hidden_layer(LAST, 0, True, LAST - 1)
            down(LAST - 1)
            turn_hidden(LAST)
            down(LAST)

        @block.scalar
        def _(act):
            def silu(n, s):
                act.wait_ge(gate_done, n + 1)
                act.wait_ge(hidden_done, n)
                nc.scalar.activation(act_gate[:], gate_ps[s][:], ACT.Silu).then_inc(silu_done, 1)

            def copy_hT(n):
                act.wait_ge(h_turned, n + 1)
                act.wait_ge(y_done, n)
                nc.scalar.activation(hT[:], hT_ps[:], ACT.Copy).then_inc(hT_copied, 1)

            silu(0, 0)
            silu(1, 1)
            copy_hT(0)
            with act.Fori(0, TILES // 2 - 1) as it:
                for s in range(2):
                    n = it * 2 + (2 + s)
                    silu(n, s)
                    copy_hT(n - 1)
            silu(LAST, 0)
            copy_hT(LAST - 1)
            copy_hT(LAST)

        @block.vector
        def _(dve):
            def copy_xT(n, s, after):
                dve.wait_ge(x_turned, n + 1)
                if after:
                    dve.wait_ge(up_done, n - 1)
                nc.vector.tensor_copy(xsT[s][:], xT_ps[:]).then_inc(xT_copied, 1)

            def hide(n, s):
                dve.wait_ge(silu_done, n + 1)
                dve.wait_ge(up_done, n + 1)
                dve.wait_ge(h_turned, n)
                nc.vector.tensor_tensor(hidden[:], up_ps[s][:], act_gate[:], ALU.mult).then_inc(hidden_done, 1)

            def find_places(n, s):
                base = n * 2
                nc.vector.tensor_scalar(second[:], xs[s][:, C + 1:ROW], tile_expert_f[:, bass.ds(n, 1)], float(T),
                                        ALU.not_equal, ALU.mult).then_inc(place_step, 1)
                dve.wait_ge(place_step, base + 1)
                nc.vector.scalar_tensor_tensor(out=far_place[:], in0=second[:], scalar=float(FAR),
                                               in1=xs[s][:, C:C + 1], op0=ALU.add, op1=ALU.add).then_inc(place_step, 1)
                dve.wait_ge(place_step, base + 2)
                nc.vector.tensor_tensor(place_f[s][:], far_place[:], dump[:, bass.ds(n, 1)], ALU.min).then_inc(
                    place_known, 1)

            def copy_y(n, s, after):
                dve.wait_ge(y_done, n + 1)
                dve.wait_ge(place_known, n + 1)
                if after:
                    dve.wait_ge(y_stored[s], (n - s) * 8)
                nc.vector.tensor_copy(place[s][:], place_f[s][:]).then_inc(place_ready, 1)
                dve.wait_ge(place_ready, n + 1)
                nc.vector.tensor_copy(ys[s][:], y_ps[:]).then_inc(y_copied, 1)

            def step(n, s, after):
                hide(n, s)
                copy_xT(n + 1, 1 - s, True)
                copy_y(n - 1, 1 - s, after)
                find_places(n + 1, 1 - s)

            dve.wait_ge(dump_ready, 1)
            copy_xT(0, 0, False)
            find_places(0, 0)
            copy_xT(1, 1, False)
            find_places(1, 1)
            hide(0, 0)
            step(1, 1, False)
            step(2, 0, False)
            step(3, 1, True)
            with dve.Fori(2, TILES // 2) as it:
                step(it * 2, 0, True)
                step(it * 2 + 1, 1, True)
            hide(LAST, 0)
            copy_y(LAST - 1, 1, True)
            copy_y(LAST, 0, True)


def mix_phase(nc, x1, weight, y_dram, out):
    with ExitStack() as ctx:
        kit = Kit(nc, ctx)
        SLOTS = 3
        y_sb = [kit.sb(f"m_y{s}", [P, TOPK, TPC, C]) for s in range(SLOTS)]
        out_sb = [kit.sb(f"m_out{s}", [P, TPC, C]) for s in range(2)]
        first = [kit.sb(f"m_first{s}", [P, TPC, C]) for s in range(2)]
        mixed = [kit.sb(f"m_mixed{s}", [P, TPC, C]) for s in range(2)]
        normed = [kit.sb(f"m_normed{s}", [P, TPC, C]) for s in range(2)]
        stats = kit.sb("m_stats", [P, TPC, 6])
        mv = kit.sb("m_mv", [P, TPC, 2])
        var_eps = kit.sb("m_var_eps", [P, TPC])
        std = kit.sb("m_std", [P, TPC])
        rstd = kit.sb("m_rstd", [P, TPC])
        shift = kit.sb("m_shift", [P, TPC])
        y_in = [[kit.sem(f"m_y{k}_in{s}") for s in range(SLOTS)] for k in range(TOPK)]
        first_ready = kit.sem("m_first_ready")
        mixed_ready = kit.sem("m_mixed_ready")
        step = kit.sem("m_step")
        var_ready = kit.sem("m_var_ready")
        std_ready = kit.sem("m_std_ready")
        shift_ready = kit.sem("m_shift_ready")
        normed_ready = kit.sem("m_normed_ready")
        out_ready = kit.sem("m_out_ready")
        stored = [kit.sem(f"m_stored{s}") for s in range(2)]
        block = ctx.enter_context(nc.Block())

        @block.sync
        def _(sp):
            def load(n):
                for k in range(TOPK):
                    sp.dma_start(y_sb[n % SLOTS][:, k], y_dram[k * T + n * CH:k * T + (n + 1) * CH, :].rearrange(
                        "(j p) c -> p j c", p=P)).then_inc(y_in[k][n % SLOTS], 16)

            for n in range(SLOTS):
                load(n)
            for n in range(NCH):
                if n + SLOTS < NCH:
                    sp.wait_ge(mixed_ready, n + 1)
                    load(n + SLOTS)
                sp.wait_ge(out_ready, n + 1)
                sp.dma_start(out[n * CH:(n + 1) * CH, :].rearrange("(j p) c -> p j c", p=P),
                             out_sb[n % 2][:]).then_inc(stored[n % 2], 16)
            for s in range(2):
                sp.wait_ge(stored[s], 16 * NCH // 2)

        @block.scalar
        def _(act):
            def weigh(n):
                act.wait_ge(y_in[0][n % SLOTS], 16 * (n // SLOTS + 1))
                if n >= 2:
                    act.wait_ge(mixed_ready, n - 1)
                for j in range(TPC):
                    t = n * TPC + j
                    last = nc.scalar.activation(first[n % 2][:, j, :], y_sb[n % SLOTS][:, 0, j, :], ACT.Copy,
                                                scale=weight[:, 0, t:t + 1])
                last.then_inc(first_ready, 1)

            weigh(0)
            for n in range(NCH):
                if n + 1 < NCH:
                    weigh(n + 1)
                act.wait_ge(var_ready, n + 1)
                nc.scalar.activation(std[:], var_eps[:], ACT.Sqrt).then_inc(std_ready, 1)
                act.wait_ge(shift_ready, n + 1)
                if n >= 2:
                    act.wait_ge(out_ready, n - 1)
                for j in range(TPC):
                    last = nc.scalar.activation(normed[n % 2][:, j, :], mixed[n % 2][:, j, :], ACT.Identity,
                                                bias=shift[:, j:j + 1], scale=rstd[:, j:j + 1])
                last.then_inc(normed_ready, 1)

        @block.vector
        def _(dve):
            st = Steps(dve, step, 0)

            def finish(n):
                dve.wait_ge(normed_ready, n + 1)
                if n >= 2:
                    dve.wait_ge(stored[n % 2], 16 * (n // 2))
                nc.vector.tensor_tensor(out_sb[n % 2][:], normed[n % 2][:], x1[:, n * TPC:(n + 1) * TPC, :],
                                        ALU.add).then_inc(out_ready, 1)

            for n in range(NCH):
                s = n % SLOTS
                dve.wait_ge(y_in[1][s], 16 * (n // SLOTS + 1))
                dve.wait_ge(first_ready, n + 1)
                if n >= 2:
                    dve.wait_ge(normed_ready, n - 1)
                for j in range(TPC):
                    t = n * TPC + j
                    last = nc.vector.scalar_tensor_tensor(out=mixed[n % 2][:, j, :], in0=y_sb[s][:, 1, j, :],
                                                          scalar=weight[:, 1, t:t + 1], in1=first[n % 2][:, j, :],
                                                          op0=ALU.mult, op1=ALU.add)
                last.then_inc(mixed_ready, 1)
                dve.wait_ge(mixed_ready, n + 1)
                for j in range(TPC):
                    last = nc.vector.bn_stats(stats[:, j, :], mixed[n % 2][:, j, :])
                st.link(last)
                for j in range(TPC):
                    last = nc.vector.bn_aggr(mv[:, j, :], stats[:, j, :])
                st.link(last)
                nc.vector.tensor_scalar_add(var_eps[:], mv[:, :, 1], EPS).then_inc(var_ready, 1)
                if n >= 1:
                    finish(n - 1)
                dve.wait_ge(std_ready, n + 1)
                st.link(nc.vector.reciprocal(rstd[:], std[:]))
                nc.vector.scalar_tensor_tensor(out=shift[:], in0=mv[:, :, 0], scalar=-1.0, in1=rstd[:], op0=ALU.mult,
                                               op1=ALU.mult).then_inc(shift_ready, 1)
                dve.wait_ge(shift_ready, n + 1)
            finish(NCH - 1)


def block_program(nc, x, wq, wk, wv, wo, wr, br, w1, w3, w2, eye, tri, tile_starts, q_rows, k_rows, masks, out):
    x = x.rearrange("b t c -> (b t) c")
    out = out.rearrange("b t c -> (b t) c")
    q_parts = nc.dram_tensor("q_parts", [G, PART_ROWS, HPG, T], BF16).ap()
    k_parts = nc.dram_tensor("k_parts", [G, PART_ROWS, HPG, T], BF16).ap()
    v_aug = nc.dram_tensor("v_aug", [T, NH * 32], F32).ap()
    o_dram = nc.dram_tensor("o_heads", [G, P, T], F32).ap()
    xs_dram = nc.dram_tensor("table_x", [TABLE_ROWS, ROW], F32).ap()
    y_dram = nc.dram_tensor("chosen_y", [TOPK * T + TILES * P, C], F32).ap()

    with ExitStack() as ctx:
        kit = Kit(nc, ctx)
        w1_sb = kit.sb("w1", [P, KC, E * FF])
        w3_sb = kit.sb("w3", [P, KC, E * FF])
        w2_sb = kit.sb("w2", [P, FF // P, E * C])
        weights_in = kit.sem("expert_weights_in")
        loads = [(w1_sb[:, :, e * FF:(e + 1) * FF], w1[e].rearrange("(k p) f -> p k f", p=P)) for e in range(E)]
        loads += [(w3_sb[:, :, e * FF:(e + 1) * FF], w3[e].rearrange("(k p) f -> p k f", p=P)) for e in range(E)]
        loads += [(w2_sb[:, :, e * C:(e + 1) * C], w2[e].rearrange("(k p) c -> p k c", p=P)) for e in range(E)]
        with ExitStack() as scores:
            operands = Operands(Kit(nc, scores), q_parts, k_parts, q_rows, k_rows, masks)
            project_phase(nc, x, wq, wk, wv, eye, q_parts, k_parts, v_aug, operands)
            attention_phase(nc, operands, v_aug, o_dram, xs_dram, loads, weights_in)
        x1 = kit.sb("x1", [P, NT, C])
        weight = kit.sb("weight", [P, TOPK, NT])
        tile_expert = kit.sb("tile_expert", [P, TILES], I32)
        tile_expert_f = kit.sb("tile_expert_f", [P, TILES])
        tile_row = kit.sb("tile_row", [P, TILES], I32)
        combine_phase(nc, x, wo, wr, br, eye, tri, tile_starts, o_dram, x1, xs_dram, weight, tile_expert,
                      tile_expert_f, tile_row)
        experts_phase(nc, eye, w1_sb, w3_sb, w2_sb, weights_in, 16 * len(loads), tile_expert,
                      tile_expert_f, tile_row, xs_dram, y_dram)
        mix_phase(nc, x1, weight, y_dram, out)


INPUTS = ("L0_attn_x", "L0_attn_Wq", "L0_attn_Wk", "L0_attn_Wv", "L0_attn_Wo", "L0_ffn_Wr", "L0_ffn_br",
          "L0_ffn_W1", "L0_ffn_W3", "L0_ffn_W2")
CONSTANTS = ("eye", "tri", "tile_starts", "q_rows", "k_rows", "masks")


def kernel(**inputs):
    import numpy as np
    import concourse.bacc as bacc
    from concourse.bass_utils import run_bass_kernel_spmd

    nc = bacc.Bacc("TRN2", target_bir_lowering=False, num_devices=1)
    constants = host_constants()
    arrays, args = {}, []
    for name in INPUTS + CONSTANTS:
        a = np.ascontiguousarray(inputs[name] if name in inputs else constants[name])
        arrays[name] = a
        args.append(nc.dram_tensor(name, a.shape, mybir.dt.from_np(a.dtype), kind="ExternalInput").ap())
    out = nc.dram_tensor("out", (1, T, C), F32, kind="ExternalOutput").ap()
    block_program(nc, *args, out)
    result = run_bass_kernel_spmd(nc, [arrays], core_ids=[0])
    return result.results[0]["out"]
```
